# Optimizing a Trainium2 kernel written in Bass

```python
import numpy as np
import jax
import jax.numpy as jnp

def _softmax(x, axis=-1):
    return jax.nn.softmax(x, axis=axis)

def _gelu(x):
    return jax.nn.gelu(x, approximate=True)

def _silu(x):
    return jax.nn.silu(x)

def _sigmoid(x):
    return jax.nn.sigmoid(x)

def _layernorm(x, axis=-1, eps=1e-05):
    m = jnp.mean(x, axis=axis, keepdims=True)
    v = jnp.var(x, axis=axis, keepdims=True)
    return (x - m) / jnp.sqrt(v + eps)

def _scatter_add(tgt, idx, src, axis=0):
    return tgt.at[idx].add(src)

def _segment_sum(src, seg, n):
    return jax.ops.segment_sum(src, seg, n)
kernel_name = 'mk_xattn_ffn_d2_seqx_r8_9170d0'

def setup_inputs(seed: int=0):
    np.random.seed(seed)
    _w = jnp.asarray

    def _rec_inputs():
        import jax
        import jax.numpy as jnp
        _rk = jax.random.key(seed)
        x = -0.0003929 + 0.9999 * jax.random.normal(jax.random.fold_in(_rk, 1), (32, 128, 128), jnp.float32)
        _lenS = 128 - jax.random.randint(jax.random.fold_in(_rk, 7), (32,), 0, max(1, 128 // 4) + 1, jnp.int32)
        _lenS2 = 128 - jax.random.randint(jax.random.fold_in(_rk, 8), (32,), 0, max(1, 128 // 4) + 1, jnp.int32)
        _ctx_768P = jax.random.normal(jax.random.fold_in(_rk, 11), (32, 16, 96), jnp.float32)
        _ctx_768c = jax.random.dirichlet(jax.random.fold_in(_rk, 511), 0.3 * jnp.ones((16,), jnp.float32), (32, 128))
        _ctx_768t = jnp.einsum('bsk,bkd->bsd', _ctx_768c, _ctx_768P)
        _ctx_768t = _ctx_768t * jax.lax.rsqrt(jnp.mean(jnp.square(_ctx_768t)) + 1e-12) * 0.953939
        ctx_768 = -7.36909e-05 + 0.999899 * (_ctx_768t + 0.3 * jax.random.normal(jax.random.fold_in(_rk, 611), (32, 128, 96), jnp.float32))
        return (x, ctx_768)
    x, ctx_768 = _rec_inputs()

    def _L0_xattn_setup():
        import jax, jax.numpy as jnp
        import numpy as np
        EPS = 1e-08
        key = jax.random.key(seed)
        kv, kt, k1, k2, k3, k4 = jax.random.split(key, 6)
        B, S = (16, 128)
        VD, TD, H = (128, 96, 64)
        visual_features = jax.random.normal(kv, (B, S, VD), dtype=jnp.float32)
        text_features = jax.random.normal(kt, (B, S, TD), dtype=jnp.float32)
        Wv = jax.random.normal(k1, (H, VD), dtype=jnp.float32) * (1.0 / np.sqrt(VD))
        bv = jax.random.normal(k2, (H,), dtype=jnp.float32) * 0.01
        Wt = jax.random.normal(k3, (H, TD), dtype=jnp.float32) * (1.0 / np.sqrt(TD))
        bt = jax.random.normal(k4, (H,), dtype=jnp.float32) * 0.01
        return {'visual_features': visual_features, 'text_features': text_features, 'Wv': Wv, 'bv': bv, 'Wt': Wt, 'bt': bt}
    _L0_xattn_all = _L0_xattn_setup()
    _L0_xattn_in = {k: v for k, v in _L0_xattn_all.items() if k in ('Wv', 'bv', 'Wt', 'bt')}
    del _L0_xattn_all

    def _L0_ffn_setup():
        import jax, jax.numpy as jnp
        import numpy as np
        TOP_K = 2
        N_GROUP = 4
        TOPK_GROUP = 2
        ROUTED_SCALE = 2.5

        def _gate(xf, gate_w, gate_bias):
            logits = xf.astype(jnp.float32) @ gate_w.astype(jnp.float32)
            scores = jax.nn.sigmoid(logits)
            sfc = scores + gate_bias.astype(jnp.float32)[None]
            T, E = sfc.shape
            e_g = E // N_GROUP
            group_feat = sfc.reshape(T, N_GROUP, e_g)
            group_scores = jax.lax.top_k(group_feat, 2)[0].sum(axis=-1)
            _, group_idx = jax.lax.top_k(group_scores, TOPK_GROUP)
            group_mask = jax.nn.one_hot(group_idx, N_GROUP, dtype=sfc.dtype).sum(axis=1)
            score_mask = jnp.broadcast_to(group_mask[..., None], (T, N_GROUP, e_g)).reshape(T, E)
            tmp_scores = jnp.where(score_mask > 0, sfc, 0.0)
            _, topk_idx = jax.lax.top_k(tmp_scores, TOP_K)
            topk_w = jnp.take_along_axis(sfc, topk_idx, axis=-1)
            topk_w = topk_w / (topk_w.sum(axis=-1, keepdims=True) + 1e-20)
            return (topk_idx, topk_w * ROUTED_SCALE)
        key = jax.random.key(seed)
        ks = jax.random.split(key, 9)
        B, N, H, I, E, SH_I = (2, 128, 128, 64, 8, 128)
        s = lambda k, shape, scale: jax.random.normal(k, shape, jnp.float32) * scale
        return {'x': s(ks[0], (B, N, H), 1.0), 'gate_w': s(ks[1], (H, E), 0.02), 'gate_bias': s(ks[2], (E,), 0.02), 'w_gate': s(ks[3], (E, H, I), 0.02), 'w_up': s(ks[4], (E, H, I), 0.02), 'w_down': s(ks[5], (E, I, H), 0.02), 'sw_gate': s(ks[6], (H, SH_I), 0.02), 'sw_up': s(ks[7], (H, SH_I), 0.02), 'sw_down': s(ks[8], (SH_I, H), 0.02)}
    _L0_ffn_all = _L0_ffn_setup()
    _L0_ffn_in = {k: v for k, v in _L0_ffn_all.items() if k in ('gate_w', 'gate_bias', 'w_gate', 'w_up', 'w_down', 'sw_gate', 'sw_up', 'sw_down')}
    del _L0_ffn_all

    def _L1_xattn_setup():
        import jax, jax.numpy as jnp
        import numpy as np
        NUM_HEADS = 16
        CLAMP = 10000.0
        key = jax.random.key(seed)
        ks = jax.random.split(key, 8)
        B, Nq, Nkv, Cq, Ckv = (4, 256, 256, 128, 96)
        s_q = 1.0 / np.sqrt(Cq)
        s_kv = 1.0 / np.sqrt(Ckv)
        return {'query': jax.random.normal(ks[0], (B, Nq, Cq), jnp.float32), 'key_value': jax.random.normal(ks[1], (B, Nkv, Ckv), jnp.float32), 'Wq': jax.random.normal(ks[2], (Cq, Cq), jnp.float32) * s_q, 'bq': jnp.zeros((Cq,), jnp.float32), 'Wk': jax.random.normal(ks[3], (Ckv, Cq), jnp.float32) * s_kv, 'bk': jnp.zeros((Cq,), jnp.float32), 'Wv': jax.random.normal(ks[4], (Ckv, Cq), jnp.float32) * s_kv, 'bv': jnp.zeros((Cq,), jnp.float32), 'Wo': jax.random.normal(ks[5], (Cq, Cq), jnp.float32) * s_q, 'bo': jnp.zeros((Cq,), jnp.float32)}
    _L1_xattn_all = _L1_xattn_setup()
    _L1_xattn_in = {k: v for k, v in _L1_xattn_all.items() if k in ('Wq', 'bq', 'Wk', 'bk', 'Wv', 'bv', 'Wo', 'bo')}
    del _L1_xattn_all

    def _L1_ffn_setup():
        import jax, jax.numpy as jnp
        import numpy as np
        EPS = 1e-05
        NUM_HEADS = 16
        NUM_KV_HEADS = 4
        NUM_EXPERTS = 8
        TOP_K = 2

        def _layernorm(x, w, b):
            mu = jnp.mean(x, axis=-1, keepdims=True)
            var = jnp.mean((x - mu) ** 2, axis=-1, keepdims=True)
            return (x - mu) * jax.lax.rsqrt(var + EPS) * w + b
        key = jax.random.key(seed)
        ks = jax.random.split(key, 8)
        S, B, H = (128, 4, 128)
        F = 256
        hd = H // NUM_HEADS
        qkv_out = (NUM_HEADS + 2 * NUM_KV_HEADS) * hd
        w_scale = 0.02
        return {'hidden_states': jax.random.normal(ks[0], (S, B, H), jnp.float32), 'ln1_weight': jnp.ones((H,), jnp.float32), 'ln1_bias': jnp.zeros((H,), jnp.float32), 'ln2_weight': jnp.ones((H,), jnp.float32), 'ln2_bias': jnp.zeros((H,), jnp.float32), 'qkv_weight': jax.random.normal(ks[1], (qkv_out, H), jnp.float32) * w_scale, 'proj_weight': jax.random.normal(ks[2], (H, H), jnp.float32) * w_scale, 'router_weight': jax.random.normal(ks[3], (NUM_EXPERTS, H), jnp.float32) * w_scale, 'moe_w1': jax.random.normal(ks[4], (NUM_EXPERTS, H, F), jnp.float32) * w_scale, 'moe_w2': jax.random.normal(ks[5], (NUM_EXPERTS, F, H), jnp.float32) * w_scale}
    _L1_ffn_all = _L1_ffn_setup()
    _L1_ffn_in = {k: v for k, v in _L1_ffn_all.items() if k in ('ln1_weight', 'ln1_bias', 'ln2_weight', 'ln2_bias', 'qkv_weight', 'proj_weight', 'router_weight', 'moe_w1', 'moe_w2')}
    del _L1_ffn_all
    return {'x': x, 'ctx_768': ctx_768, 'L0_xattn_Wv': _L0_xattn_in['Wv'], 'L0_xattn_bv': _L0_xattn_in['bv'], 'L0_xattn_Wt': _L0_xattn_in['Wt'], 'L0_xattn_bt': _L0_xattn_in['bt'], 'L0_ffn_gate_w': _L0_ffn_in['gate_w'], 'L0_ffn_gate_bias': _L0_ffn_in['gate_bias'], 'L0_ffn_w_gate': _L0_ffn_in['w_gate'], 'L0_ffn_w_up': _L0_ffn_in['w_up'], 'L0_ffn_w_down': _L0_ffn_in['w_down'], 'L0_ffn_sw_gate': _L0_ffn_in['sw_gate'], 'L0_ffn_sw_up': _L0_ffn_in['sw_up'], 'L0_ffn_sw_down': _L0_ffn_in['sw_down'], 'L1_xattn_Wq': _L1_xattn_in['Wq'], 'L1_xattn_bq': _L1_xattn_in['bq'], 'L1_xattn_Wk': _L1_xattn_in['Wk'], 'L1_xattn_bk': _L1_xattn_in['bk'], 'L1_xattn_Wv': _L1_xattn_in['Wv'], 'L1_xattn_bv': _L1_xattn_in['bv'], 'L1_xattn_Wo': _L1_xattn_in['Wo'], 'L1_xattn_bo': _L1_xattn_in['bo'], 'L1_ffn_ln1_weight': _L1_ffn_in['ln1_weight'], 'L1_ffn_ln1_bias': _L1_ffn_in['ln1_bias'], 'L1_ffn_ln2_weight': _L1_ffn_in['ln2_weight'], 'L1_ffn_ln2_bias': _L1_ffn_in['ln2_bias'], 'L1_ffn_qkv_weight': _L1_ffn_in['qkv_weight'], 'L1_ffn_proj_weight': _L1_ffn_in['proj_weight'], 'L1_ffn_router_weight': _L1_ffn_in['router_weight'], 'L1_ffn_moe_w1': _L1_ffn_in['moe_w1'], 'L1_ffn_moe_w2': _L1_ffn_in['moe_w2']}

def reference(x, ctx_768, L0_xattn_Wv, L0_xattn_bv, L0_xattn_Wt, L0_xattn_bt, L0_ffn_gate_w, L0_ffn_gate_bias, L0_ffn_w_gate, L0_ffn_w_up, L0_ffn_w_down, L0_ffn_sw_gate, L0_ffn_sw_up, L0_ffn_sw_down, L1_xattn_Wq, L1_xattn_bq, L1_xattn_Wk, L1_xattn_bk, L1_xattn_Wv, L1_xattn_bv, L1_xattn_Wo, L1_xattn_bo, L1_ffn_ln1_weight, L1_ffn_ln1_bias, L1_ffn_ln2_weight, L1_ffn_ln2_bias, L1_ffn_qkv_weight, L1_ffn_proj_weight, L1_ffn_router_weight, L1_ffn_moe_w1, L1_ffn_moe_w2):
    import jax
    import jax.numpy as jnp

    def _L0_xattn_ref(visual_features, text_features, Wv, bv, Wt, bt):
        import jax, jax.numpy as jnp
        import numpy as np
        EPS = 1e-08
        v = jnp.einsum('bsd,hd->bsh', visual_features, Wv) + bv
        t = jnp.einsum('bsd,hd->bsh', text_features, Wt) + bt
        dots = jnp.einsum('bih,bjh->bij', v, t)
        vn = jnp.linalg.norm(v, axis=-1)
        tn = jnp.linalg.norm(t, axis=-1)
        denom = jnp.maximum(vn[:, :, None] * tn[:, None, :], EPS)
        return dots / denom

    def _L0_ffn_ref(x, gate_w, gate_bias, w_gate, w_up, w_down, sw_gate, sw_up, sw_down):
        import jax, jax.numpy as jnp
        import numpy as np
        TOP_K = 2
        N_GROUP = 4
        TOPK_GROUP = 2
        ROUTED_SCALE = 2.5

        def _gate(xf, gate_w, gate_bias):
            logits = xf.astype(jnp.float32) @ gate_w.astype(jnp.float32)
            scores = jax.nn.sigmoid(logits)
            sfc = scores + gate_bias.astype(jnp.float32)[None]
            T, E = sfc.shape
            e_g = E // N_GROUP
            group_feat = sfc.reshape(T, N_GROUP, e_g)
            group_scores = jax.lax.top_k(group_feat, 2)[0].sum(axis=-1)
            _, group_idx = jax.lax.top_k(group_scores, TOPK_GROUP)
            group_mask = jax.nn.one_hot(group_idx, N_GROUP, dtype=sfc.dtype).sum(axis=1)
            score_mask = jnp.broadcast_to(group_mask[..., None], (T, N_GROUP, e_g)).reshape(T, E)
            tmp_scores = jnp.where(score_mask > 0, sfc, 0.0)
            _, topk_idx = jax.lax.top_k(tmp_scores, TOP_K)
            topk_w = jnp.take_along_axis(sfc, topk_idx, axis=-1)
            topk_w = topk_w / (topk_w.sum(axis=-1, keepdims=True) + 1e-20)
            return (topk_idx, topk_w * ROUTED_SCALE)
        B, N, H = x.shape
        xf = x.reshape(-1, H)
        topk_idx, topk_w = _gate(xf, gate_w, gate_bias)
        g = jax.nn.silu(jnp.einsum('th,ehi->tei', xf, w_gate))
        u = jnp.einsum('th,ehi->tei', xf, w_up)
        experts_y = jnp.einsum('tei,eih->teh', g * u, w_down)
        masked_y = jnp.take_along_axis(experts_y, topk_idx[:, :, None], axis=1)
        y = jnp.einsum('tkh,tk->th', masked_y, topk_w.astype(x.dtype)).reshape(B, N, H)
        shared = jax.nn.silu(x @ sw_gate) * (x @ sw_up) @ sw_down
        return y + shared

    def _L1_xattn_ref(query, key_value, Wq, bq, Wk, bk, Wv, bv, Wo, bo):
        import jax, jax.numpy as jnp
        import numpy as np
        NUM_HEADS = 16
        CLAMP = 10000.0
        B, Nq, Cq = query.shape
        Nkv = key_value.shape[1]
        H = NUM_HEADS
        D = Cq // H
        scale = D ** (-0.5)
        q = (query @ Wq + bq).reshape(B, Nq, H, D).transpose(0, 2, 1, 3)
        k = (key_value @ Wk + bk).reshape(B, Nkv, H, D).transpose(0, 2, 1, 3)
        v = (key_value @ Wv + bv).reshape(B, Nkv, H, D).transpose(0, 2, 1, 3)
        attn = jnp.einsum('bhqd,bhkd->bhqk', q, k) * scale
        attn = jnp.clip(attn, -CLAMP, CLAMP)
        attn = jax.nn.softmax(attn, axis=-1)
        attn = jnp.where(jnp.any(jnp.isnan(attn)), jnp.asarray(1.0 / Nkv, attn.dtype), attn)
        x = jnp.einsum('bhqk,bhkd->bqhd', attn, v).reshape(B, Nq, Cq)
        return x @ Wo + bo

    def _L1_ffn_ref(hidden_states, ln1_weight, ln1_bias, ln2_weight, ln2_bias, qkv_weight, proj_weight, router_weight, moe_w1, moe_w2):
        import jax, jax.numpy as jnp
        import numpy as np
        EPS = 1e-05
        NUM_HEADS = 16
        NUM_KV_HEADS = 4
        NUM_EXPERTS = 8
        TOP_K = 2

        def _layernorm(x, w, b):
            mu = jnp.mean(x, axis=-1, keepdims=True)
            var = jnp.mean((x - mu) ** 2, axis=-1, keepdims=True)
            return (x - mu) * jax.lax.rsqrt(var + EPS) * w + b
        S, B, H = hidden_states.shape
        hd = H // NUM_HEADS
        rep = NUM_HEADS // NUM_KV_HEADS
        scale = 1.0 / hd ** 0.5
        ln1_out = _layernorm(hidden_states, ln1_weight, ln1_bias)
        qkv = jnp.einsum('sbh,oh->sbo', ln1_out, qkv_weight)
        q = qkv[..., :NUM_HEADS * hd].reshape(S, B, NUM_HEADS, hd)
        k = qkv[..., NUM_HEADS * hd:(NUM_HEADS + NUM_KV_HEADS) * hd].reshape(S, B, NUM_KV_HEADS, hd)
        v = qkv[..., (NUM_HEADS + NUM_KV_HEADS) * hd:].reshape(S, B, NUM_KV_HEADS, hd)
        k = jnp.repeat(k, rep, axis=2)
        v = jnp.repeat(v, rep, axis=2)
        scores = jnp.einsum('sbhd,tbhd->bhst', q, k) * scale
        causal = jnp.tril(jnp.ones((S, S), bool))
        scores = jnp.where(causal, scores, jnp.finfo(scores.dtype).min)
        probs = jax.nn.softmax(scores, axis=-1)
        attn = jnp.einsum('bhst,tbhd->sbhd', probs, v).reshape(S, B, H)
        proj_out = jnp.einsum('sbh,oh->sbo', attn, proj_weight)
        hidden_after_attn = hidden_states + proj_out
        ln2_out = _layernorm(hidden_after_attn, ln2_weight, ln2_bias)
        x = ln2_out.reshape(-1, H)
        logits = jnp.einsum('th,eh->te', x, router_weight)
        gate = jax.nn.softmax(logits, axis=-1)
        top_probs, top_idx = jax.lax.top_k(gate, TOP_K)
        h_mid = jax.nn.gelu(jnp.einsum('th,ehf->etf', x, moe_w1))
        expert_out = jnp.einsum('etf,efh->eth', h_mid, moe_w2)
        e_ids = jnp.arange(NUM_EXPERTS)[:, None, None]
        weights = jnp.sum(jnp.where(top_idx[None] == e_ids, top_probs[None], 0.0), axis=-1)
        moe_out = jnp.einsum('eth,et->th', expert_out, weights).reshape(S, B, H)
        return hidden_after_attn + moe_out
    x = x + _L0_xattn_ref(_layernorm(x, axis=-1), ctx_768, L0_xattn_Wv, L0_xattn_bv, L0_xattn_Wt, L0_xattn_bt)
    x = x + _L0_ffn_ref(_layernorm(x, axis=-1), L0_ffn_gate_w, L0_ffn_gate_bias, L0_ffn_w_gate, L0_ffn_w_up, L0_ffn_w_down, L0_ffn_sw_gate, L0_ffn_sw_up, L0_ffn_sw_down)
    x = x + _L1_xattn_ref(_layernorm(x, axis=-1), ctx_768, L1_xattn_Wq, L1_xattn_bq, L1_xattn_Wk, L1_xattn_bk, L1_xattn_Wv, L1_xattn_bv, L1_xattn_Wo, L1_xattn_bo)
    x = x + _L1_ffn_ref(_layernorm(x, axis=-1), L1_ffn_ln1_weight, L1_ffn_ln1_bias, L1_ffn_ln2_weight, L1_ffn_ln2_bias, L1_ffn_qkv_weight, L1_ffn_proj_weight, L1_ffn_router_weight, L1_ffn_moe_w1, L1_ffn_moe_w2)
    return x

_drawn_inputs = setup_inputs


def setup_inputs(seed=0):
    import zlib

    import numpy as np

    out = dict(_drawn_inputs(seed))
    spreads = {'L1_xattn_bq': (0.0, 0.402),
     'L1_xattn_bk': (0.0, 0.8),
     'L1_xattn_bv': (0.0, 0.1),
     'L1_xattn_bo': (0.0, 0.1),
     'L1_ffn_ln1_weight': (1.0, 0.6),
     'L1_ffn_ln1_bias': (0.0, 0.8),
     'L1_ffn_ln2_weight': (1.0, 0.6),
     'L1_ffn_ln2_bias': (0.0, 0.8)}
    factors = {'L0_xattn_bv': 8.0,
     'L0_xattn_bt': 8.0,
     'L0_ffn_gate_w': 8.0,
     'L0_ffn_gate_bias': 8.0,
     'L0_ffn_w_gate': 8.0,
     'L0_ffn_w_up': 8.0,
     'L0_ffn_w_down': 8.0,
     'L0_ffn_sw_gate': 8.0,
     'L0_ffn_sw_up': 8.0,
     'L0_ffn_sw_down': 8.0,
     'L1_ffn_qkv_weight': 6.208,
     'L1_ffn_proj_weight': 5.961,
     'L1_ffn_router_weight': 8.0,
     'L1_ffn_moe_w1': 8.0,
     'L1_ffn_moe_w2': 8.0}
    for name, (base, spread) in spreads.items():
        noise = np.random.default_rng([zlib.crc32(name.encode()), seed]).standard_normal(out[name].shape)
        drawn = base * np.exp(spread * noise) if base else spread * noise
        out[name] = jnp.asarray(drawn.astype(out[name].dtype))
    for name, factor in factors.items():
        out[name] = (out[name] * factor).astype(out[name].dtype)
    return out
```

```python
from contextlib import ExitStack

import concourse.bass as bass
from concourse import mybir

F32 = mybir.dt.float32
F16 = mybir.dt.float16
BF16 = mybir.dt.bfloat16
ALU = mybir.AluOpType
ACT = mybir.ActivationFunctionType
AX = mybir.AxisListType

B, S, C, CT = 32, 128, 128, 96
GB = 4
G = B // GB
N = GB * S
NE = 8
DV = 64
NH, HD = 16, 8
LN_EPS = 1e-5
COS_EPS = 1e-8
ROUTED_SCALE = 2.5
GATE_STEPS = 20
NBLK = NE * 64 // C + 1


def after(eng, sem, value):
    if not isinstance(value, int) or value > 0:
        eng.wait_ge(sem, value)


def wait_alone(eng, sem, value, carrier):
    eng.wait_ge(sem, value)
    if not isinstance(value, int):
        eng.sem_inc(carrier, 1)


def after_alone(eng, sem, value, carrier):
    if not isinstance(value, int) or value > 0:
        wait_alone(eng, sem, value, carrier)


def before(k, p):
    return k - 1 if p == 0 else k - 3 if p == 1 else k - 2


def over_groups(eng, step, first, last):
    step(first)
    step(first + 1)
    with eng.Fori(first + 2, last) as g:
        step(g)
    step(last)


class Room:

    def __init__(self, nc, ctx, part):
        self.nc, self.ctx, self.part, self.held = nc, ctx, part, []

    def sb(self, name, shape, dt=F32):
        return self.ctx.enter_context(self.nc.sbuf_tensor(name, shape, dt))

    def sems(self, names):
        got = {n: self.nc.alloc_semaphore(f"{self.part}_{n}") for n in names.split()}
        self.held += got.values()
        return got

    def end(self):
        self.nc.clear_and_free_semaphores(self.held)
        self.nc.all_engine_barrier()


def tok(t, g, lo=0, n=N, rows=None):
    at = g * N + lo
    cols = slice(at, at + n) if isinstance(g, int) else bass.ds(at, n)
    return t[:, cols] if rows is None else t[0:rows, cols]


def split_product(pe, ps, lhs, rhs, start=True, stop=True, **kw):
    pe.matmul(ps, lhs[0], rhs[0], start=start, stop=False, **kw)
    pe.matmul(ps, lhs[0], rhs[1], start=False, stop=False, **kw)
    return pe.matmul(ps, lhs[1], rhs[0], start=False, stop=stop, **kw)


def layer0(nc, d, bank, keep):
    X, ident, ident16, ones, cT = keep["X"], keep["ident"], keep["ident16"], keep["ones"], keep["cT"]
    with ExitStack() as ctx:
        room = Room(nc, ctx, "layer0")
        sb = room.sb
        xT = [sb(f"xT{i}", [C, B * S], F16) for i in range(2)]
        wvh_raw = sb("wvh_raw", [DV, C])
        wth_raw = sb("wth_raw", [DV, CT])
        bv0 = sb("bv0", [DV, 1])
        bt0 = sb("bt0", [DV, 1])
        wv0 = [sb(f"wv0_{i}", [C, DV], F16) for i in range(2)]
        wt0 = [sb(f"wt0_{i}", [CT, DV], F16) for i in range(2)]
        gw_raw = sb("gw_raw", [C, NE])
        gw = [sb(f"gw{i}", [C, NE], F16) for i in range(2)]
        gbias = sb("gbias", [128, NE])
        w_raw = sb("w_raw", [128, 3, NBLK, 128])
        w0 = [sb(f"w0_{i}", [128, 3, NBLK, 128], F16) for i in range(2)]
        before4 = sb("before4", [128, 4, 4])
        before8 = sb("before8", [128, NE, NE])
        pick = sb("pick", [2 * NE, NBLK - 1, 128], F16)
        cload = sb("cload", [S, GB, CT])
        st = sb("st", [128, GB, 6])
        mv = sb("mv", [128, GB, 2])
        rs = sb("rs", [128, 4, GB])
        half = sb("half", [128, 8])
        xn = sb("xn", [S, GB, C])
        vt = [sb(f"vt{i}", [DV, N]) for i in range(2)]
        sq = sb("sq", [DV, 2, N])
        n2 = sb("n2", [128, 2 * GB])
        rn = sb("rn", [128, 2 * GB])
        dg = sb("dg", [128, GB, 128])
        wm = sb("wm", [128, GB, 128])
        th = sb("th", [128, GB, NE])
        sfc = sb("sfc", [128, GB, NE])
        gs = sb("gs", [128, GB, 4])
        c4 = sb("c4", [128, 3, GB, 4, 4])
        cnt4 = sb("cnt4", [128, 2, GB, 4])
        tmp8 = sb("tmp8", [128, GB, NE])
        c8 = sb("c8", [128, 3, GB, NE, NE])
        cnt8 = sb("cnt8", [128, GB, NE])
        sel = sb("sel", [128, GB, NE])
        den0 = sb("den0", [128, 2, GB])
        wgt = sb("wgt", [128, GB, NE])
        wst = sb("wst", [128, GB, 2 * NE], F16)
        eT = sb("eT", [2 * NE, B * S], F16)
        sg = sb("sg", [128, 2, N])
        su = sb("su", [128, 2, N])
        hm = sb("hm", [128, 2, N])
        hp = [sb(f"hp{i}", [128, NBLK, N], F16) for i in range(2)]
        xa = [sb(f"xa{i}", [C, N], F16) for i in range(2)]

        names = """consts bf_ready w_raw_loaded small_loaded gate_loaded wTr_ready w0_split w0t_split pow_const
            x_loaded c_loaded stA mvA epsA rsA xnA cT_psum xnT_psum cT_hi cT_lo xA_hi xA_lo vt_psum vt_sb
            sq_ready dots_psum n2_ready rn_ready dg_ready rb_psum wm_min wm_ready x1_ready
            stB mvB epsB rsB xnB xBT_psum xB_hi xB_lo logit_psum th_ready gate_step carrier wst_ready eT_psum eT_ready
            gu_psum sg_ready su_ready hm_ready hi_ready lo_ready down_psum x2_ready"""
        s = room.sems(names)
        block = ctx.enter_context(nc.Block())

        def xg(g):
            return X[:, bass.ds(GB * g, GB), :] if not isinstance(g, int) else X[:, GB * g:GB * g + GB, :]

        P0, P1, G0, G1, U0, U1, WB, DN = bank
        GP, UP = [G0, G1], [U0, U1]

        @block.sync
        def _(sp):
            sp.dma_start(wvh_raw[:], d["L0_xattn_Wv"]).then_inc(s["small_loaded"], 16)
            sp.dma_start(wth_raw[:], d["L0_xattn_Wt"]).then_inc(s["small_loaded"], 16)
            sp.dma_start(bv0[:], d["L0_xattn_bv"].rearrange("(h a) -> h a", a=1)).then_inc(s["small_loaded"], 16)
            sp.dma_start(bt0[:], d["L0_xattn_bt"].rearrange("(h a) -> h a", a=1)).then_inc(s["small_loaded"], 16)
            sp.dma_start(gw_raw[:], d["L0_ffn_gate_w"]).then_inc(s["gate_loaded"], 16)
            sp.dma_start(gbias[:], d["L0_ffn_gate_bias"].partition_broadcast(128)).then_inc(s["gate_loaded"], 16)
            for k, (routed, shared) in enumerate((("w_gate", "sw_gate"), ("w_up", "sw_up"))):
                sp.dma_start(w_raw[:, k, 0:NBLK - 1, :].rearrange("p b (e i) -> p (b e) i", e=2),
                             d["L0_ffn_" + routed].rearrange("e h i -> h e i")).then_inc(s["w_raw_loaded"], 16)
                sp.dma_start(w_raw[:, k, NBLK - 1, :], d["L0_ffn_" + shared]).then_inc(s["w_raw_loaded"], 16)
            sp.dma_start(w_raw[:, 2, 0:NBLK - 1, :],
                         d["L0_ffn_w_down"].rearrange("(b e) i h -> (e i) b h", e=2)).then_inc(s["w_raw_loaded"], 16)
            sp.dma_start(w_raw[:, 2, NBLK - 1, :], d["L0_ffn_sw_down"]).then_inc(s["w_raw_loaded"], 16)

            def load(g):
                src_x = d["x"][GB * g:GB * g + GB] if isinstance(g, int) else d["x"][bass.ds(GB * g, GB)]
                src_c = d["ctx_768"][GB * g:GB * g + GB] if isinstance(g, int) else d["ctx_768"][bass.ds(GB * g, GB)]
                sp.dma_start(xg(g), src_x.rearrange("b s c -> s b c")).then_inc(s["x_loaded"], 16)
                if not isinstance(g, int) or g > 0:
                    wait_alone(sp, s["cT_psum"], g, s["carrier"])
                sp.dma_start(cload[:], src_c.rearrange("b s c -> s b c")).then_inc(s["c_loaded"], 16)
                sp.wait_ge(s["x_loaded"], 16 * (g + 1))
                wait_alone(sp, s["c_loaded"], 16 * (g + 1), s["carrier"])
            over_groups(sp, load, 0, G - 1)

        @block.gpsimd
        def _(pool):
            pool.memset(ident[:], 0.0)
            pool.memset(ones[:], 1.0)
            pool.memset(half[:], -0.5)
            pool.memset(before4[:], 1.0)
            pool.memset(before8[:], 1.0).then_inc(s["consts"], 1)
            pool.wait_ge(s["consts"], 1)
            pool.affine_select(out=ident[:], in_=ident[:], compare_op=ALU.not_equal, fill=1.0, base=0,
                               pattern=[[-1, 128]], channel_multiplier=1).then_inc(s["consts"], 1)
            pool.affine_select(out=before4[:], in_=before4[:], compare_op=ALU.is_gt, fill=0.0, base=0,
                               pattern=[[1, 4], [-1, 4]], channel_multiplier=0)
            pool.affine_select(out=before8[:], in_=before8[:], compare_op=ALU.is_gt, fill=0.0, base=0,
                               pattern=[[1, NE], [-1, NE]], channel_multiplier=0)
            pv = pick[:].rearrange("r b (e i) -> r b e i", e=2)
            pool.wait_ge(s["consts"], 2)
            pool.tensor_copy(ident16[:], ident[:]).then_inc(s["consts"], 1)
            pool.memset(pick[:], 0.0).then_inc(s["consts"], 1)
            for k in range(2):
                pool.wait_ge(s["consts"], 4 + k)
                pool.affine_select(out=pv, in_=pv, compare_op=ALU.not_equal, fill=1.0, base=-NE * k,
                                   pattern=[[-2, NBLK - 1], [-1, 2], [0, 64]],
                                   channel_multiplier=1).then_inc(s["consts"], 1)

            def prep(g, part):
                if part in (0, 3):
                    k = "AB"[part // 3]
                    if part == 3:
                        wait_alone(pool, s["wm_ready"], g + 1, s["carrier"])
                        pool.tensor_tensor(xg(g), xg(g), wm[:], ALU.add).then_inc(s["x1_ready"], 1)
                    wait_alone(pool, s["mv" + k], g + 1, s["carrier"])
                    pool.tensor_scalar(rs[:, 0, :], mv[:, :, 1], 1.0, LN_EPS, ALU.mult, ALU.add
                                       ).then_inc(s["eps" + k], 1)
                    pool.wait_ge(s["eps" + k], g + 1)
                    pool.tensor_tensor(rs[:, 1, :], rs[:, 0, :], half[:, 0:GB], ALU.pow).then_inc(s["rs" + k], 1)
                elif part == 1:
                    pool.wait_ge(s["vt_sb"], 2 * (g + 1))
                    for i in range(2):
                        last = pool.tensor_tensor(sq[:, i, :], vt[i][:], vt[i][:], ALU.mult)
                    last.then_inc(s["sq_ready"], 1)
                elif part == 2:
                    pool.wait_ge(s["n2_ready"], g + 1)
                    pool.tensor_tensor(rn[:], n2[:], half[:], ALU.pow).then_inc(s["rn_ready"], 1)
                    wait_alone(pool, s["rn_ready"], g + 1, s["carrier"])
                    for i in range(GB):
                        last = pool.tensor_scalar(dg[:, i, :], ident[:], rn[:, GB + i:GB + i + 1], 0.0,
                                                  ALU.mult, ALU.add)
                    last.then_inc(s["dg_ready"], 1)

            def lo(g, p):
                pool.wait_ge(s["hi_ready"], NBLK * g + p + 1)
                pool.tensor_tensor(hp[1][:, p, :], hm[:, p % 2, :], hp[0][:, p, :], ALU.subtract
                                   ).then_inc(s["lo_ready"], 1)

            def step(g):
                for p in range(NBLK):
                    if not isinstance(g, int) or g + 1 < G:
                        prep(g + 1, p)
                    if not isinstance(g, int) or g >= 0:
                        lo(g, p)
            over_groups(pool, step, -1, G - 1)

        @block.scalar
        def _(act):
            act.wait_ge(s["w_raw_loaded"], 16 * 6)
            for k in range(3):
                last = act.activation(w0[0][:, k], w_raw[:, k], ACT.Copy)
            act.wait_ge(s["gate_loaded"], 32)
            act.activation(gw[0][:], gw_raw[:], ACT.Copy).then_inc(s["w0_split"], 1)
            act.wait_ge(s["wTr_ready"], 1)
            act.activation(wv0[0][:], P0[:, 0:DV], ACT.Copy)
            act.activation(wt0[0][:], P0[0:CT, DV:2 * DV], ACT.Copy).then_inc(s["w0t_split"], 1)
            act.wait_ge(s["small_loaded"], 64)

            def prep(g, part):
                if part == 0:
                    act.wait_ge(s["xnT_psum"], g + 1)
                    after(act, s["vt_psum"], g)
                    act.activation(xa[0][:], P0[:], ACT.Copy).then_inc(s["xA_hi"], 1)
                    act.wait_ge(s["cT_psum"], g + 1)
                    act.activation(tok(cT[0], g, rows=CT), P1[0:CT, :], ACT.Copy).then_inc(s["cT_hi"], 1)
                elif part == 1:
                    act.wait_ge(s["vt_psum"], g + 1)
                    after(act, s["dots_psum"], g)
                    act.activation(vt[0][:], P0[0:DV, :], ACT.Identity, bias=bv0[:]).then_inc(s["vt_sb"], 1)
                    act.activation(vt[1][:], P1[0:DV, :], ACT.Identity, bias=bt0[:]).then_inc(s["vt_sb"], 1)
                elif part == 3:
                    act.wait_ge(s["xBT_psum"], g + 1)
                    act.activation(tok(xT[0], g), P0[:], ACT.Copy).then_inc(s["xB_hi"], 1)
                elif part == 4:
                    act.wait_ge(s["logit_psum"], g + 1)
                    act.activation(th[:].rearrange("p b e -> p (b e)"), P1[:, 0:GB * NE], ACT.Tanh,
                                   scale=0.5).then_inc(s["th_ready"], 1)
                    act.wait_ge(s["eT_psum"], g + 1)
                    act.activation(tok(eT, g), P1[0:2 * NE, 0:N // 2].bitcast(F16), ACT.Copy).then_inc(s["eT_ready"], 1)

            def step(g):
                cur = not isinstance(g, int) or g >= 0
                for p in range(NBLK):
                    k = NBLK * g + p
                    if cur:
                        act.wait_ge(s["gu_psum"], k + 1)
                        after(act, s["hm_ready"], before(k, p) + 1)
                        act.activation(sg[:, p % 2, :], GP[p % 2][:], ACT.Silu).then_inc(s["sg_ready"], 1)
                    if not isinstance(g, int) or g + 1 < G:
                        prep(g + 1, p)
                    if cur:
                        act.wait_ge(s["hm_ready"], k + 1)
                        after(act, s["down_psum"], k - NBLK + 1)
                        act.activation(hp[0][:, p, :], hm[:, p % 2, :], ACT.Copy).then_inc(s["hi_ready"], 1)
            over_groups(act, step, -1, G - 1)

        @block.vector
        def _(dve):
            dve.memset(cT[0][CT:CT + 1, :], 1.0)
            dve.memset(cT[1][CT:CT + 1, :], 0.0)
            dve.wait_ge(s["w0_split"], 1)
            dve.tensor_tensor(w0[1][:], w_raw[:], w0[0][:], ALU.subtract)
            dve.tensor_tensor(gw[1][:], gw_raw[:], gw[0][:], ALU.subtract).then_inc(s["w0_split"], 1)
            dve.wait_ge(s["w0t_split"], 1)
            dve.tensor_tensor(wv0[1][:], P0[:, 0:DV], wv0[0][:], ALU.subtract)
            dve.tensor_tensor(wt0[1][:], P0[0:CT, DV:2 * DV], wt0[0][:], ALU.subtract).then_inc(s["w0t_split"], 1)

            dve.wait_ge(s["consts"], 6)

            def stats(k, g):
                for i in range(GB):
                    last = dve.bn_stats(st[:, i, :], xg(g)[:, i, :])
                last.then_inc(s["st" + k], 1)
                wait_alone(dve, s["st" + k], g + 1, s["carrier"])
                for i in range(GB):
                    last = dve.bn_aggr(mv[:, i, :], st[:, i, :])
                last.then_inc(s["mv" + k], 1)
                wait_alone(dve, s["rs" + k], g + 1, s["carrier"])
                for i in range(GB):
                    last = dve.tensor_scalar(xn[:, i, :], xg(g)[:, i, :], mv[:, i, 0:1], rs[:, 1, i:i + 1],
                                             ALU.subtract, ALU.mult)
                last.then_inc(s["xn" + k], 1)

            def gate(g):
                steps = 0

                def link(ins):
                    nonlocal steps
                    steps += 1
                    ins.then_inc(s["gate_step"], 1)
                    dve.wait_ge(s["gate_step"], GATE_STEPS * g + steps)

                def rank(values, n, room, mask):
                    shape = [128, GB, n, n]
                    other = values.unsqueeze(2).broadcast_to(shape)
                    own = values.unsqueeze(3).broadcast_to(shape)
                    tie = mask.unsqueeze(1).broadcast_to(shape)
                    dve.tensor_tensor(room[:, 0], other, own, ALU.is_gt)
                    link(dve.tensor_tensor(room[:, 1], other, own, ALU.is_equal))
                    link(dve.tensor_tensor(room[:, 2], room[:, 1], tie, ALU.mult))
                    link(dve.tensor_tensor(room[:, 1], room[:, 0], room[:, 2], ALU.add))

                dve.wait_ge(s["th_ready"], g + 1)
                link(dve.tensor_scalar(th[:], th[:], 0.5, 0.5, ALU.mult, ALU.add))
                link(dve.tensor_tensor(sfc[:], th[:], gbias[:].unsqueeze(1).broadcast_to([128, GB, NE]), ALU.add))
                pairs = sfc[:].rearrange("p b (q e) -> p b q e", e=2)
                link(dve.tensor_tensor(gs[:], pairs[:, :, :, 0], pairs[:, :, :, 1], ALU.add))
                rank(gs[:], 4, c4, before4[:])
                link(dve.tensor_reduce(cnt4[:, 0], c4[:, 1], AX.X, ALU.add))
                link(dve.tensor_scalar(cnt4[:, 1], cnt4[:, 0], 2.0, None, ALU.is_lt))
                link(dve.tensor_tensor(tmp8[:].rearrange("p b (q e) -> p b q e", e=2), pairs,
                                       cnt4[:, 1].unsqueeze(3).broadcast_to([128, GB, 4, 2]), ALU.mult))
                rank(tmp8[:], NE, c8, before8[:])
                link(dve.tensor_reduce(cnt8[:], c8[:, 1], AX.X, ALU.add))
                link(dve.tensor_scalar(sel[:], cnt8[:], 2.0, None, ALU.is_lt))
                link(dve.tensor_tensor(sel[:], sel[:], sfc[:], ALU.mult))
                link(dve.tensor_reduce(den0[:, 0], sel[:], AX.X, ALU.add))
                link(dve.tensor_scalar(den0[:, 0], den0[:, 0], 1e-20, None, ALU.add))
                link(dve.reciprocal(den0[:, 1], den0[:, 0]))
                link(dve.scalar_tensor_tensor(wgt[:], sel[:], ROUTED_SCALE,
                                              den0[:, 1].unsqueeze(2).broadcast_to([128, GB, NE]),
                                              ALU.mult, ALU.mult))
                link(dve.tensor_copy(wst[:, :, 0:NE], wgt[:]))
                dve.tensor_tensor(wst[:, :, NE:], wgt[:], wst[:, :, 0:NE], ALU.subtract).then_inc(s["wst_ready"], 1)
                assert steps == GATE_STEPS

            def prep(g, part):
                if part == 0:
                    wait_alone(dve, s["x_loaded"], 16 * (g + 1), s["carrier"])
                    after(dve, s["xBT_psum"], g)
                    stats("A", g)
                    dve.wait_ge(s["xA_hi"], g + 1)
                    dve.tensor_tensor(xa[1][:], P0[:], xa[0][:], ALU.subtract).then_inc(s["xA_lo"], 1)
                    dve.wait_ge(s["cT_hi"], g + 1)
                    dve.tensor_tensor(tok(cT[1], g, rows=CT), P1[0:CT, :], tok(cT[0], g, rows=CT),
                                      ALU.subtract).then_inc(s["cT_lo"], 1)
                elif part == 2:
                    dve.wait_ge(s["dots_psum"], g + 1)
                    dve.tensor_scalar(n2[:], P1[:, 0:2 * GB], 1e-37, None, ALU.max).then_inc(s["n2_ready"], 1)
                    dve.wait_ge(s["rb_psum"], g + 1)
                    after(dve, s["x1_ready"], g)
                    for i in range(GB):
                        last = dve.tensor_scalar(wm[:, i, :], P1[:, 128 * i:128 * i + 128], rn[:, i:i + 1],
                                                 1.0 / COS_EPS, ALU.mult, ALU.min)
                    last.then_inc(s["wm_min"], 1)
                    dve.wait_ge(s["wm_min"], g + 1)
                    wf = wm[:].rearrange("p b c -> p (b c)")
                    dve.tensor_tensor(wf, P0[:], wf, ALU.mult).then_inc(s["wm_ready"], 1)
                elif part == 3:
                    wait_alone(dve, s["x1_ready"], g + 1, s["carrier"])
                    stats("B", g)
                    dve.wait_ge(s["xB_hi"], g + 1)
                    dve.tensor_tensor(tok(xT[1], g), P0[:], tok(xT[0], g), ALU.subtract).then_inc(s["xB_lo"], 1)
                elif part == 4:
                    gate(g)

            def step(g):
                cur = not isinstance(g, int) or g >= 0
                for p in range(NBLK):
                    k = NBLK * g + p
                    if cur and p == 2:
                        add(g - 1)
                    if cur:
                        i = p % 2
                        dve.wait_ge(s["sg_ready"], k + 1)
                        after(dve, s["lo_ready"], before(k, p) + 1)
                        if p < NBLK - 1:
                            dve.tensor_tensor(su[:, i, :], sg[:, i, :], UP[i][:], ALU.mult).then_inc(s["su_ready"], 1)
                            dve.wait_ge(s["su_ready"], (NBLK - 1) * g + p + 1)
                            dve.tensor_tensor(hm[:, i, :], su[:, i, :], WB[:], ALU.mult).then_inc(s["hm_ready"], 1)
                        else:
                            dve.tensor_tensor(hm[:, i, :], sg[:, i, :], UP[i][:], ALU.mult).then_inc(s["hm_ready"], 1)
                    if not isinstance(g, int) or g + 1 < G:
                        prep(g + 1, p)

            def add(g):
                if isinstance(g, int) and g < 0:
                    return
                dve.wait_ge(s["down_psum"], NBLK * (g + 1))
                xf = xg(g).rearrange("p b c -> p (b c)")
                dve.tensor_tensor(xf, DN[:], xf, ALU.add).then_inc(s["x2_ready"], 1)
            over_groups(dve, step, -1, G - 1)
            add(G - 1)

        @block.tensor
        def _(pe):
            pe.wait_ge(s["consts"], 3)
            pe.wait_ge(s["small_loaded"], 64)
            pe.transpose(P0[:, 0:DV], wvh_raw[:], ident[0:DV, 0:DV])
            pe.transpose(P0[0:CT, DV:2 * DV], wth_raw[:], ident[0:DV, 0:DV]).then_inc(s["wTr_ready"], 1)
            pe.wait_ge(s["w0t_split"], 2)

            def prep(g, part):
                if part == 0:
                    pe.wait_ge(s["xnA"], g + 1)
                    after(pe, s["xB_lo"], g)
                    for i in range(GB):
                        last = pe.transpose(P0[:, 128 * i:128 * i + 128], xn[:, i, :], ident[:])
                    last.then_inc(s["xnT_psum"], 1)
                    pe.wait_ge(s["c_loaded"], 16 * (g + 1))
                    after(pe, s["eT_ready"], g)
                    for i in range(GB):
                        last = pe.transpose(P1[0:CT, 128 * i:128 * i + 128], cload[:, i, :], ident[:])
                    last.then_inc(s["cT_psum"], 1)
                elif part == 1:
                    pe.wait_ge(s["xA_lo"], g + 1)
                    split_product(pe, P0[0:DV, :], [w[:] for w in wv0], [x[:] for x in xa])
                    pe.wait_ge(s["cT_lo"], g + 1)
                    split_product(pe, P1[0:DV, :], [w[:] for w in wt0],
                                  [tok(x, g, rows=CT) for x in cT]).then_inc(s["vt_psum"], 1)
                elif part == 2:
                    pe.wait_ge(s["vt_sb"], 2 * (g + 1))
                    for i in range(GB):
                        pe.matmul(P0[:, 128 * i:128 * i + 128], vt[0][:, 128 * i:128 * i + 128],
                                  vt[1][:, 128 * i:128 * i + 128], start=True, stop=True)
                    pe.wait_ge(s["sq_ready"], g + 1)
                    for j in range(2):
                        for i in range(GB):
                            last = pe.matmul(P1[:, GB * j + i:GB * j + i + 1], sq[:, j, 128 * i:128 * i + 128],
                                             ones[0:DV, 0:1], start=True, stop=True)
                    last.then_inc(s["dots_psum"], 1)
                    pe.wait_ge(s["dg_ready"], g + 1)
                    pe.matmul(P1[:], ones[:], dg[:].rearrange("p b c -> p (b c)"), start=True, stop=True
                              ).then_inc(s["rb_psum"], 1)
                elif part == 3:
                    pe.wait_ge(s["xnB"], g + 1)
                    for i in range(GB):
                        last = pe.transpose(P0[:, 128 * i:128 * i + 128], xn[:, i, :], ident[:])
                    last.then_inc(s["xBT_psum"], 1)
                elif part == 4:
                    pe.wait_ge(s["xB_lo"], g + 1)
                    for i in range(GB):
                        last = split_product(pe, P1[:, NE * i:NE * i + NE], [tok(x, g, 128 * i, 128) for x in xT],
                                             [w[:] for w in gw])
                    last.then_inc(s["logit_psum"], 1)
                    pe.wait_ge(s["wst_ready"], g + 1)
                    for i in range(GB):
                        last = pe.transpose(P1[0:2 * NE, 64 * i:64 * i + 64].bitcast(F16), wst[:, i, :], ident16[:])
                    last.then_inc(s["eT_psum"], 1)

            def up(g, p):
                k = NBLK * g + p
                i = p % 2
                if p == 0:
                    pe.wait_ge(s["eT_ready"], g + 1)
                x = [tok(t, g) for t in xT]
                after(pe, s["sg_ready"], before(k, p) + 1)
                after(pe, s["hm_ready"], before(k, p) + 1)
                split_product(pe, GP[i][:], [w[:, 0, p, :] for w in w0], x)
                last = split_product(pe, UP[i][:], [w[:, 1, p, :] for w in w0], x)
                if p < NBLK - 1:
                    after_alone(pe, s["hm_ready"], k, s["carrier"])
                    last = pe.matmul(WB[:], pick[:, p, :], tok(eT, g), start=True, stop=True)
                last.then_inc(s["gu_psum"], 1)

            def down(g, p):
                if isinstance(g, int) and g < 0:
                    return
                pe.wait_ge(s["lo_ready"], NBLK * g + p + 1)
                if p == 0:
                    after(pe, s["x2_ready"], g)
                for i in range(GB):
                    cols = slice(128 * i, 128 * i + 128)
                    last = split_product(pe, DN[:, cols], [h[:, p, cols] for h in hp], [w[:, 2, p, :] for w in w0],
                                         start=(p == 0 and i == 0), stop=(p == NBLK - 1), skip_group_check=True)
                last.then_inc(s["down_psum"], 1)

            pe.wait_ge(s["w0_split"], 2)
            pe.wait_ge(s["consts"], 6)

            def step(g):
                for p in range(NBLK):
                    if not isinstance(g, int) or g >= 0:
                        up(g, p)
                    if not isinstance(g, int) or g + 1 < G:
                        prep(g + 1, p)
                    if not isinstance(g, int) or g >= 0:
                        down(g if p >= 2 else g - 1, (p - 2) % NBLK)
            over_groups(pe, step, -1, G - 1)
            down(G - 1, NBLK - 2)
            down(G - 1, NBLK - 1)
    return room


def attention1(nc, d, bank, keep, X3):
    X, ident, ident16, ones, cT = keep["X"], keep["ident"], keep["ident16"], keep["ones"], keep["cT"]
    SCALE = HD ** -0.5
    CLIP = 10000.0 / SCALE
    RING = 4
    U = NH // 4
    with ExitStack() as ctx:
        room = Room(nc, ctx, "cross")
        sb = room.sb
        wq_raw = sb("wq_raw", [C, C])
        wk_raw = sb("wk_raw", [CT + 1, C])
        wv_raw = sb("wv_raw", [CT + 1, C])
        wo = sb("wo", [C, C])
        bo = sb("bo", [1, C])
        bq_raw = sb("bq_raw", [2, C])
        wq_c = [sb(f"wq_c{i}", [C, C], F16) for i in range(2)]
        wk_c = [sb(f"wk_c{i}", [CT + 1, C], F16) for i in range(2)]
        wv_c = [sb(f"wv_c{i}", [CT + 1, C], F16) for i in range(2)]
        bq_c = [sb(f"bq_c{i}", [2, C], F16) for i in range(3)]
        wq = [sb(f"wq{i}", [C, NH, 4, HD], F16) for i in range(2)]
        wk = [sb(f"wk{i}", [CT + 1, NH, 4, HD], F16) for i in range(2)]
        bq = sb("bq", [2, NH, 4, HD], F16)
        ones16 = sb("ones16", [2, 128], F16)
        low_rows = sb("low_rows", [128, 2])
        negsel = sb("negsel", [NH, NH, 128], F16)
        st = sb("st1", [128, B, 6])
        mv = sb("mv1", [128, B, 2])
        rs = sb("rs1", [128, 2, B])
        half = sb("half1", [128, B])
        xn = sb("xn1", [S, C])
        xh = [sb(f"xh{i}", [C, S], F16) for i in range(2)]
        qhi = sb("qhi", [128, U * S], F16)
        khi = sb("khi", [128, U * S], F16)
        Q = [sb(f"Q{i}", [128, U * S], F16) for i in range(RING)]
        K = [sb(f"K{i}", [128, U * S], F16) for i in range(RING)]
        V = [sb(f"V{i}", [S, NH, 32]) for i in range(RING)]
        mx = sb("mx", [S, NH])
        m16 = sb("m16", [S, NH], F16)
        mT = sb("mT", [NH, S], F16)
        P = [sb(f"P{i}", [S, 4 * S]) for i in range(RING)]
        OE = sb("OE", [128, U * S])
        dn = sb("dn", [S, NH])
        On = sb("On", [S, C])
        OT = sb("OT", [C, S])
        s = room.sems("""w_loaded small_const w_hi w_lo w_rep stats_a stats_b stats_c stats_d carrier1 xn_ready xT_psum
            xT_hi xT_lo k_psum k_hi k_ready q_psum q_hi q_ready v_psum v_ready s_psum s_max m_ready mT_psum mT_ready
            t_psum t_clip t_neg p_ready o_psum oT_sb f_psum dn_ready o_norm a_psum a_sb y_psum x3_ready""")
        block = ctx.enter_context(nc.Block())
        S0, S1, T0, T1, QK, M, O, F = bank
        SB, TB = [S0, S1], [T0, T1]

        def has(b):
            return not isinstance(b, int) or 0 <= b < B

        def sweep(eng, step):
            for b in range(-3, RING):
                step(b, b % RING)
            with eng.Fori(1, B // RING - 1) as q:
                for i in range(RING):
                    step(q * RING + i, i)
            for b in range(B - RING, B + 2):
                step(b, b % RING)

        def batch(t, b):
            return t[:, b, :] if isinstance(b, int) else t[:, bass.ds(b, 1), :].rearrange("p a c -> p (a c)")

        def btok(t, b):
            return t[:, b * S:b * S + S] if isinstance(b, int) else t[:, bass.ds(b * S, S)]

        def head(t, j, u=None):
            return t[32 * j:32 * j + 32, 128 * u:128 * u + 128]

        @block.sync
        def _(sp):
            for t, n in ((wq_raw, "Wq"), (wo, "Wo")):
                sp.dma_start(t[:], d["L1_xattn_" + n]).then_inc(s["w_loaded"], 16)
            for t, n in ((wk_raw, "k"), (wv_raw, "v")):
                sp.dma_start(t[0:CT, :], d["L1_xattn_W" + n]).then_inc(s["w_loaded"], 16)
                sp.dma_start(t[CT:CT + 1, :], d["L1_xattn_b" + n].rearrange("(a c) -> a c", a=1)
                             ).then_inc(s["w_loaded"], 16)
            sp.dma_start(bq_raw[:], d["L1_xattn_bq"].partition_broadcast(2)).then_inc(s["w_loaded"], 16)
            sp.dma_start(bo[:], d["L1_xattn_bo"].rearrange("(a c) -> a c", a=1)).then_inc(s["w_loaded"], 16)

        @block.gpsimd
        def _(pool):
            pool.memset(half[:], -0.5)
            pool.memset(ones16[:], 1.0)
            for t in (wq[0], wq[1], wk[0], wk[1], bq):
                pool.memset(t[:], 0.0)
            for t in V:
                pool.memset(t[:, :, 0:HD], 0.0)
                pool.memset(t[:, :, HD:HD + 1], 1.0)
                last = pool.memset(t[:, :, HD + 1:], 0.0)
            last.then_inc(s["small_const"], 1)
            pool.wait_ge(s["stats_b"], 1)
            pool.tensor_scalar(rs[:, 0, :], mv[:, :, 1], 1.0, LN_EPS, ALU.mult, ALU.add).then_inc(s["stats_c"], 1)
            pool.wait_ge(s["stats_c"], 1)
            pool.tensor_tensor(rs[:, 1, :], rs[:, 0, :], half[:], ALU.pow).then_inc(s["stats_d"], 1)

        @block.scalar
        def _(act):
            act.wait_ge(s["w_loaded"], 16 * 8)
            for raw, c in ((wq_raw, wq_c), (wk_raw, wk_c), (wv_raw, wv_c), (bq_raw, bq_c)):
                last = act.activation(c[0][:], raw[:], ACT.Copy)
            last.then_inc(s["w_hi"], 1)
            act.wait_ge(s["w_lo"], 2)
            act.wait_ge(s["small_const"], 1)
            for w, c in ((wq, wq_c), (wk, wk_c)):
                rows = c[0].shape[0]
                for i in range(2):
                    last = act.activation(w[i][:, :, 0:3, :], c[i][:].rearrange("p (h d) -> p h d", d=HD).unsqueeze(2)
                                          .broadcast_to([rows, NH, 3, HD]), ACT.Copy)
            last = act.activation(bq[:, :, 0:3, :], bq_c[2][:].rearrange("p (h d) -> p h d", d=HD).unsqueeze(2)
                                  .broadcast_to([2, NH, 3, HD]), ACT.Copy)
            last.then_inc(s["w_rep"], 1)

            def exp(b, j, i):
                u = U * b + j
                act.wait_ge(s["t_neg"], u + 1)
                after(act, s["o_psum"], u - 3)
                act.activation(P[j][:], TB[j % 2][:], ACT.Exp, scale=SCALE).then_inc(s["p_ready"], 1)

            def step(b, i):
                i2 = (i + 2) % RING
                if has(b):
                    act.wait_ge(s["mT_psum"], b + 1)
                    after(act, s["t_neg"], U * b)
                    act.activation(mT[:], M[0:NH, 256:256 + S // 2].bitcast(F16), ACT.Copy).then_inc(s["mT_ready"], 1)
                if has(b + 2):
                    act.wait_ge(s["xT_psum"], b + 3)
                    after(act, s["q_psum"], b + 2)
                    act.activation(xh[0][:], M[:, 0:S], ACT.Copy).then_inc(s["xT_hi"], 1)
                if has(b - 1):
                    exp(b - 1, U - 1, (i - 1) % RING)
                if has(b + 2):
                    act.wait_ge(s["k_psum"], b + 3)
                    after(act, s["k_ready"], b + 2)
                    act.activation(khi[:], QK[:], ACT.Copy, scale=low_rows[:, 1:2]).then_inc(s["k_hi"], 1)
                if has(b - 2):
                    act.wait_ge(s["a_psum"], b - 1)
                    after(act, s["y_psum"], b - 2)
                    act.activation(OT[:], F[:, 0:S], ACT.Copy).then_inc(s["a_sb"], 1)
                if has(b):
                    exp(b, 0, i)
                if has(b + 2):
                    act.wait_ge(s["v_psum"], b + 3)
                    after(act, s["o_psum"], U * (b - 1))
                    act.activation(V[i2][:, :, 0:HD], M[:, S:2 * S].rearrange("p (h d) -> p h d", d=HD), ACT.Copy
                                   ).then_inc(s["v_ready"], 1)
                if has(b - 1):
                    act.wait_ge(s["o_psum"], U * b)
                    after(act, s["f_psum"], b - 1)
                    act.activation(OE[:], O[:], ACT.Copy).then_inc(s["oT_sb"], 1)
                if has(b):
                    exp(b, 1, i)
                if has(b + 2):
                    act.wait_ge(s["q_psum"], b + 3)
                    after(act, s["q_ready"], b + 2)
                    act.activation(qhi[:], QK[:], ACT.Copy, scale=low_rows[:, 0:1]).then_inc(s["q_hi"], 1)
                if has(b):
                    exp(b, 2, i)
            sweep(act, step)

        @block.vector
        def _(dve):
            for b in range(B):
                last = dve.bn_stats(st[:, b, :], X[:, b, :])
            last.then_inc(s["stats_a"], 1)
            idv = ident[:].rearrange("p (j r d) -> p j r d", r=4, d=HD)
            dve.tensor_reduce(low_rows[:, 0:1], idv[:, :, 2, :], AX.XY, ALU.add)
            dve.tensor_reduce(low_rows[:, 1:2], idv[:, :, 1, :], AX.XY, ALU.add)
            dve.tensor_scalar(negsel[:], ident[0:NH, 0:NH].unsqueeze(2).broadcast_to([NH, NH, 128]), -1.0, None, ALU.mult)
            dve.wait_ge(s["stats_a"], 1)
            for b in range(B):
                last = dve.bn_aggr(mv[:, b, :], st[:, b, :])
            last.then_inc(s["stats_b"], 1)
            dve.wait_ge(s["w_hi"], 1)
            for raw, c in ((wq_raw, wq_c), (wk_raw, wk_c), (wv_raw, wv_c), (bq_raw, bq_c)):
                last = dve.tensor_tensor(c[1][:], raw[:], c[0][:], ALU.subtract)
            last.then_inc(s["w_lo"], 1)
            dve.wait_ge(s["w_lo"], 1)
            dve.tensor_scalar(bq_c[2][:], bq_c[1][:], ident[0:2, 1:2], None, ALU.mult).then_inc(s["stats_a"], 1)
            dve.wait_ge(s["stats_a"], 2)
            dve.scalar_tensor_tensor(bq_c[2][:], bq_c[0][:], ident[0:2, 0:1], bq_c[2][:], ALU.mult, ALU.add
                                     ).then_inc(s["w_lo"], 1)
            dve.wait_ge(s["stats_d"], 1)

            def normalise(b):
                if has(b):
                    after_alone(dve, s["xT_psum"], b, s["carrier1"])
                    m, r = ((mv[:, b, 0:1], rs[:, 1, b:b + 1]) if isinstance(b, int) else
                            (mv[:, bass.ds(b, 1), 0:1].rearrange("p a c -> p (a c)"), rs[:, 1, bass.ds(b, 1)]))
                    dve.tensor_scalar(xn[:], batch(X, b), m, r, ALU.subtract, ALU.mult).then_inc(s["xn_ready"], 1)

            def clip(b, j):
                if has(b):
                    dve.wait_ge(s["t_psum"], U * b + j + 1)
                    dve.tensor_scalar(TB[j % 2][:], TB[j % 2][:], -CLIP, CLIP, ALU.max, ALU.min
                                      ).then_inc(s["t_clip"], 1)

            def maxima(b, j):
                if has(b):
                    dve.wait_ge(s["s_psum"], U * b + j + 1)
                    if j == 0:
                        after(dve, s["m_ready"], b)
                    dve.tensor_reduce(mx[:, 4 * j:4 * j + 4], SB[j % 2][:].rearrange("p (h k) -> p h k", h=4), AX.X,
                                      ALU.max).then_inc(s["s_max"], 1)

            def step(b, i):
                i2 = (i + 2) % RING
                if has(b + 2):
                    dve.wait_ge(s["xT_hi"], b + 3)
                    dve.tensor_tensor(xh[1][:], M[:, 0:S], xh[0][:], ALU.subtract).then_inc(s["xT_lo"], 1)
                clip(b, 0)
                maxima(b + 1, 0)
                if has(b + 2):
                    dve.wait_ge(s["k_hi"], b + 3)
                    dve.tensor_tensor(K[i2][:], QK[:], khi[:], ALU.subtract).then_inc(s["k_ready"], 1)
                clip(b, 1)
                maxima(b + 1, 1)
                if has(b - 2):
                    wait_alone(dve, s["y_psum"], b - 1, s["carrier1"])
                    dve.tensor_tensor(batch(X3, b - 2), F[:, S:2 * S], batch(X, b - 2), ALU.add
                                      ).then_inc(s["x3_ready"], 1)
                clip(b, 2)
                maxima(b + 1, 2)
                if has(b + 2):
                    dve.wait_ge(s["q_hi"], b + 3)
                    dve.tensor_tensor(Q[i2][:], QK[:], qhi[:], ALU.subtract).then_inc(s["q_ready"], 1)
                clip(b, 3)
                maxima(b + 1, 3)
                if has(b + 1):
                    dve.wait_ge(s["s_max"], U * (b + 2))
                    after(dve, s["mT_psum"], b + 1)
                    dve.tensor_scalar(m16[:], mx[:], -CLIP, CLIP, ALU.max, ALU.min).then_inc(s["m_ready"], 1)
                if has(b - 1):
                    fv = F[:].rearrange("p (j h w) -> p j h w", h=4, w=32)
                    dve.wait_ge(s["f_psum"], b)
                    dve.reciprocal(dn[:].rearrange("p (j h) -> p j h", h=4), fv[:, :, :, HD]).then_inc(s["dn_ready"], 1)
                    dve.wait_ge(s["dn_ready"], b)
                    after(dve, s["a_psum"], b - 1)
                    dve.tensor_tensor(On[:].rearrange("p (h j d) -> p j h d", h=4, d=HD), fv[:, :, :, 0:HD],
                                      dn[:].rearrange("p (j h) -> p j h", h=4).unsqueeze(3)
                                      .broadcast_to([S, U, 4, HD]), ALU.mult).then_inc(s["o_norm"], 1)
                normalise(b + 3)
            sweep(dve, step)

        @block.tensor
        def _(pe):
            pe.wait_ge(s["w_rep"], 1)

            def score(b, j, i):
                after(pe, s["s_max"], U * b + j - 1)
                for h in range(4):
                    last = pe.matmul(SB[j % 2][:, 128 * h:128 * h + 128], head(Q[i], j, h), head(K[i], j, h),
                                     start=True, stop=True, tile_position=(32 * j, 0))
                last.then_inc(s["s_psum"], 1)

            def score_t(b, j, i):
                after(pe, s["p_ready"], U * b + j - 1)
                for h in range(4):
                    last = pe.matmul(TB[j % 2][:, 128 * h:128 * h + 128], head(K[i], j, h), head(Q[i], j, h),
                                     start=(h == 0), stop=False, tile_position=(32 * j, 0), skip_group_check=True)
                last.then_inc(s["t_psum"], 1)

            def less_max(b, j):
                pe.wait_ge(s["mT_ready"], b + 1)
                pe.wait_ge(s["t_clip"], U * b + j + 1)
                for h in range(4):
                    last = pe.matmul(TB[j % 2][:, 128 * h:128 * h + 128], negsel[:, 4 * j + h, :], mT[:],
                                     start=False, stop=True, skip_group_check=True)
                last.then_inc(s["t_neg"], 1)

            def values(b, j, i):
                pe.wait_ge(s["p_ready"], U * b + j + 1)
                if j == 0:
                    pe.wait_ge(s["v_ready"], b + 1)
                    after(pe, s["oT_sb"], b)
                for h in range(4):
                    last = pe.matmul(O[32 * h:32 * h + 32, 128 * j:128 * j + 128], V[i][:, 4 * h + j, :],
                                     P[j][:, 128 * h:128 * h + 128], start=True, stop=True, tile_position=(0, 32 * h))
                last.then_inc(s["o_psum"], 1)

            def project(b, i, w, x, done, bias=False):
                for j in range(U):
                    cols = QK[:, 128 * j:128 * j + 128]
                    if bias:
                        pe.matmul(cols, bq[:, 4 * j:4 * j + 4].rearrange("p h r d -> p (h r d)"), ones16[:],
                                  start=True, stop=False)
                    last = split_product(pe, cols, [a[:, 4 * j:4 * j + 4].rearrange("p h r d -> p (h r d)") for a in w],
                                         x, start=not bias)
                last.then_inc(done, 1)

            def step(b, i):
                i1, b1 = (i + 1) % RING, b + 1
                ip = (i - 1) % RING
                if has(b + 2):
                    pe.wait_ge(s["xn_ready"], b + 3)
                    after(pe, s["v_ready"], b + 2)
                    pe.transpose(M[:, 0:S], xn[:], ident[:]).then_inc(s["xT_psum"], 1)
                if has(b):
                    pe.wait_ge(s["m_ready"], b + 1)
                    pe.transpose(M[0:NH, 256:256 + S // 2].bitcast(F16), m16[:], ident16[:]).then_inc(s["mT_psum"], 1)
                if has(b1):
                    pe.wait_ge(s["k_ready"], b + 2)
                    pe.wait_ge(s["q_ready"], b + 2)
                    score(b1, 0, i1)
                if has(b - 1):
                    less_max(b - 1, 3)
                if has(b):
                    score_t(b, 0, i)
                if has(b + 2):
                    after(pe, s["q_ready"], b + 2)
                    project(b + 2, i, wk, [btok(c, b + 2) for c in cT], s["k_psum"])
                if has(b - 1):
                    values(b - 1, 2, ip)
                if has(b1):
                    score(b1, 1, i1)
                if has(b):
                    less_max(b, 0)
                    score_t(b, 1, i)
                if has(b - 1):
                    values(b - 1, 3, ip)
                if has(b + 2):
                    pe.wait_ge(s["xT_lo"], b + 3)
                    split_product(pe, M[:, S:2 * S], [btok(c, b + 2) for c in cT], [w[:] for w in wv_c]
                                  ).then_inc(s["v_psum"], 1)
                if has(b - 2):
                    pe.wait_ge(s["a_sb"], b - 1)
                    pe.matmul(F[:, S:2 * S], OT[:], wo[:], start=True, stop=False)
                    pe.matmul(F[:, S:2 * S], ones[0:1, :], bo[:], start=False, stop=True).then_inc(s["y_psum"], 1)
                if has(b1):
                    score(b1, 2, i1)
                if has(b):
                    less_max(b, 1)
                    score_t(b, 2, i)
                    values(b, 0, i)
                if has(b + 2):
                    pe.wait_ge(s["xT_lo"], b + 3)
                    pe.wait_ge(s["k_ready"], b + 3)
                    project(b + 2, i, wq, [x[:] for x in xh], s["q_psum"], bias=True)
                if has(b1):
                    score(b1, 3, i1)
                if has(b):
                    less_max(b, 2)
                    score_t(b, 3, i)
                if has(b - 1):
                    pe.wait_ge(s["oT_sb"], b)
                    after(pe, s["x3_ready"], b - 1)
                    for j in range(U):
                        last = pe.transpose(F[:, 128 * j:128 * j + 128], OE[:, 128 * j:128 * j + 128], ident[:])
                    last.then_inc(s["f_psum"], 1)
                if has(b):
                    values(b, 1, i)
                if has(b - 1):
                    pe.wait_ge(s["o_norm"], b)
                    pe.transpose(F[:, 0:S], On[:], ident[:]).then_inc(s["a_psum"], 1)
            sweep(pe, step)
    return room


def attention2(nc, d, bank, keep, X3, H, AT, wp):
    ident, ident16, ones = keep["ident"], keep["ident16"], keep["ones"]
    NG, T = 4, B
    R = 3 * NG * HD
    SCALE = HD ** -0.5
    QUADS = S // 4
    LOWEST = -3.0e38
    with ExitStack() as ctx:
        room = Room(nc, ctx, "causal")
        sb = room.sb
        qw = sb("qw", [128, C])
        kvw = sb("kvw", [64, C])
        pw = sb("pw", [C, 128])
        pwp = sb("pwp", [C, 128])
        lnw = sb("lnw", [C, 1])
        lnb = sb("lnb", [C, 1])
        wT = sb("wT", [C, 192])
        w8f = sb("w8f", [C, 8, R])
        w8 = [sb(f"w8_{i}", [C, 8, R], F16) for i in range(2)]
        wvr = sb("wvr", [C, 4, NG * HD])
        wv = [sb(f"wvd{i}", [C, NG * HD], F16) for i in range(2)]
        low = sb("low", [R, 2])
        b8 = sb("b8", [R, 8])
        b8m = sb("b8m", [R, 8])
        bv = sb("bvd", [128, 1])
        st = sb("st2", [128, B, 6])
        mv = sb("mv2", [128, B, 2])
        rs = sb("rs2", [128, 6, B])
        half = sb("half2", [128, B])
        xn = sb("xn2", [S, GB, C])
        xT = [sb(f"xTd{i}", [C, B * S], F16) for i in range(2)]
        hm = sb("hmd", [R, 4, N], F16)
        QK = sb("QKd", [R, 8, B * S], F16)
        s = room.sems("""d_loaded d_consts d_raw d_wT d_pwp d_pT d_stack d_hi d_lo d_bias d_b8 d_stats d_mv
            d_rs h_ready dxn dT_psum dT_hi dT_lo e_psum e_hi e_ready carrier2""")
        PT, PB = bank[0], bank[2:6]

        with nc.Block() as block:
            @block.sync
            def _(sp):
                sp.dma_start(qw[:], d["L1_ffn_qkv_weight"][0:128]).then_inc(s["d_loaded"], 16)
                sp.dma_start(kvw[:], d["L1_ffn_qkv_weight"][128:192]).then_inc(s["d_loaded"], 16)
                sp.dma_start(pw[:], d["L1_ffn_proj_weight"]).then_inc(s["d_loaded"], 16)
                sp.dma_start(lnw[:], d["L1_ffn_ln1_weight"].rearrange("(h a) -> h a", a=1)).then_inc(s["d_loaded"], 16)
                sp.dma_start(lnb[:], d["L1_ffn_ln1_bias"].rearrange("(h a) -> h a", a=1)).then_inc(s["d_loaded"], 16)

            @block.gpsimd
            def _(pool):
                pool.memset(w8f[:], 0.0)
                pool.memset(half[:], -0.5).then_inc(s["d_consts"], 1)
                pool.wait_ge(s["d_mv"], 1)

                def link(ins, n):
                    ins.then_inc(s["d_rs"], 1)
                    pool.wait_ge(s["d_rs"], n)
                link(pool.tensor_scalar(rs[:, 0, :], mv[:, :, 1], 1.0, LN_EPS, ALU.mult, ALU.add), 1)
                link(pool.tensor_tensor(rs[:, 1, :], rs[:, 0, :], half[:], ALU.pow), 2)
                link(pool.tensor_tensor(rs[:, 2, :], rs[:, 1, :], rs[:, 1, :], ALU.mult), 3)
                link(pool.tensor_tensor(rs[:, 2, :], rs[:, 2, :], mv[:, :, 1], ALU.mult), 4)
                link(pool.tensor_scalar(rs[:, 3, :], rs[:, 2, :], 1.0, LN_EPS, ALU.mult, ALU.add), 5)
                link(pool.tensor_tensor(rs[:, 4, :], rs[:, 3, :], half[:], ALU.pow), 6)
                link(pool.tensor_tensor(rs[:, 5, :], rs[:, 4, :], rs[:, 1, :], ALU.mult), 7)
                for b in range(B):
                    last = pool.tensor_scalar(H[:, b, :], X3[:, b, :], mv[:, b, 0:1], rs[:, 1, b:b + 1],
                                              ALU.subtract, ALU.mult)
                last.then_inc(s["h_ready"], 1)

            @block.scalar
            def _(act):
                act.wait_ge(s["d_loaded"], 16 * 5)
                act.activation(pwp[:].rearrange("p (l g d) -> p l g d", l=4, d=HD),
                               pw[:].rearrange("p (g l d) -> p l g d", l=4, d=HD), ACT.Copy).then_inc(s["d_pwp"], 1)
                act.wait_ge(s["d_raw"], 1)
                act.activation(wT[:], bank[0][:, 0:192], ACT.Copy).then_inc(s["d_wT"], 1)
                act.wait_ge(s["d_wT"], 1)
                act.wait_ge(s["d_consts"], 1)
                wq = wT[:, 0:128].rearrange("p (g l d) -> p l g d", l=4, d=HD)
                w8v = w8f[:].rearrange("p k (r g d) -> p k r g d", g=NG, d=HD)
                for l in range(4):
                    for r in range(3):
                        act.activation(w8v[:, l, r], wq[:, l], ACT.Copy)
                for g in range(NG):
                    act.activation(w8v[:, 4 + g, :, g, :], wT[:, 128 + HD * g:136 + HD * g].unsqueeze(1)
                                   .broadcast_to([C, 3, HD]), ACT.Copy)
                act.activation(wvr[:], wT[:, 160:192].unsqueeze(1).broadcast_to([C, 4, NG * HD]), ACT.Copy
                               ).then_inc(s["d_stack"], 1)
                act.wait_ge(s["d_stack"], 1)
                act.activation(w8[0][:], w8f[:], ACT.Copy, scale=lnw[:])
                act.activation(wv[0][:], wvr[:, 0, :], ACT.Copy, scale=lnw[:])
                act.wait_ge(s["d_pT"], 1)
                act.activation(wp[0][:], bank[1][:, 0:128], ACT.Copy).then_inc(s["d_hi"], 1)
                act.wait_ge(s["d_bias"], 1)
                act.activation(b8[:], bank[2][0:R, 0:8], ACT.Copy)
                act.activation(bv[:], bank[3][:, 0:1], ACT.Copy).then_inc(s["d_b8"], 1)
                act.wait_ge(s["d_b8"], 3)

                def hi(g):
                    act.wait_ge(s["dT_psum"], g + 1)
                    act.activation(tok(xT[0], g), PT[:], ACT.Copy).then_inc(s["dT_hi"], 1)

                def step(g):
                    for k in range(8):
                        if not isinstance(g, int) or g >= 0:
                            act.wait_ge(s["e_psum"], 8 * g + k + 1)
                            after(act, s["e_ready"], 8 * g + k - 3)
                            act.activation(hm[:, k % 4], PB[k % 4][0:R, :], ACT.Identity, bias=b8m[:, k:k + 1],
                                           scale=low[:, k // 4:k // 4 + 1]).then_inc(s["e_hi"], 1)
                        if k == 5 and (not isinstance(g, int) or g + 1 < G):
                            hi(g + 1)
                over_groups(act, step, -1, G - 1)

            @block.vector
            def _(dve):
                for b in range(B):
                    last = dve.bn_stats(st[:, b, :], X3[:, b, :])
                last.then_inc(s["d_stats"], 1)
                dve.wait_ge(s["d_stats"], 1)
                for b in range(B):
                    last = dve.bn_aggr(mv[:, b, :], st[:, b, :])
                last.then_inc(s["d_mv"], 1)
                idv = ident[0:R, 0:R].rearrange("p (r x) -> p r x", r=3)
                dve.tensor_reduce(low[:, 0:1], idv[:, 2, :], AX.X, ALU.add)
                dve.tensor_reduce(low[:, 1:2], idv[:, 1, :], AX.X, ALU.add)
                dve.wait_ge(s["d_hi"], 1)
                dve.tensor_tensor(wp[1][:], bank[1][:, 0:128], wp[0][:], ALU.subtract)
                dve.scalar_tensor_tensor(w8[1][:], w8f[:], lnw[:], w8[0][:], ALU.mult, ALU.subtract)
                dve.scalar_tensor_tensor(wv[1][:], wvr[:, 0, :], lnw[:], wv[0][:], ALU.mult, ALU.subtract
                                         ).then_inc(s["d_lo"], 1)
                dve.wait_ge(s["d_b8"], 1)
                dve.wait_ge(s["d_lo"], 1)
                for k in range(2):
                    dve.tensor_scalar(b8m[:, 4 * k:4 * k + 4], b8[:, 4 * k:4 * k + 4], low[:, k:k + 1], None, ALU.mult
                                      ).then_inc(s["d_b8"], 1)
                dve.wait_ge(s["d_rs"], 7)

                def normalise(g):
                    after_alone(dve, s["dT_psum"], g, s["carrier2"])
                    for i in range(GB):
                        if isinstance(g, int):
                            b = GB * g + i
                            m, r, x = mv[:, b, 0:1], rs[:, 5, b:b + 1], X3[:, b, :]
                        else:
                            at = bass.ds(GB * g + i, 1)
                            m, r = mv[:, at, 0:1].rearrange("p a c -> p (a c)"), rs[:, 5, at]
                            x = X3[:, at, :].rearrange("p a c -> p (a c)")
                        last = dve.tensor_scalar(xn[:, i, :], x, m, r, ALU.subtract, ALU.mult)
                    last.then_inc(s["dxn"], 1)

                def step(g):
                    for k in range(8):
                        if k == 0 and (not isinstance(g, int) or g + 1 < G):
                            normalise(g + 1)
                        if not isinstance(g, int) or g >= 0:
                            dve.wait_ge(s["e_hi"], 8 * g + k + 1)
                            dst = QK[:, k, g * N:g * N + N] if isinstance(g, int) else QK[:, k, bass.ds(g * N, N)]
                            dve.scalar_tensor_tensor(dst, PB[k % 4][0:R, :], b8[:, k:k + 1], hm[:, k % 4],
                                                     ALU.add, ALU.subtract).then_inc(s["e_ready"], 1)
                        if k == 5 and (not isinstance(g, int) or g + 1 < G):
                            dve.wait_ge(s["dT_hi"], g + 2)
                            dve.tensor_tensor(tok(xT[1], g + 1), PT[:], tok(xT[0], g + 1), ALU.subtract
                                              ).then_inc(s["dT_lo"], 1)
                over_groups(dve, step, -1, G - 1)

            @block.tensor
            def _(pe):
                pe.wait_ge(s["d_loaded"], 16 * 5)
                pe.transpose(bank[0][:, 0:128], qw[:], ident[:])
                pe.transpose(bank[0][:, 128:192], kvw[:], ident[0:64, 0:64]).then_inc(s["d_raw"], 1)
                pe.wait_ge(s["d_pwp"], 1)
                pe.transpose(bank[1][:, 0:128], pwp[:], ident[:]).then_inc(s["d_pT"], 1)
                pe.wait_ge(s["d_stack"], 1)
                for k in range(8):
                    pe.matmul(bank[2][0:R, k:k + 1], w8f[:, k], lnb[:], start=True, stop=True)
                pe.matmul(bank[3][:, 0:1], wvr[:].rearrange("p l x -> p (l x)"), lnb[:], start=True, stop=True
                          ).then_inc(s["d_bias"], 1)
                pe.wait_ge(s["d_b8"], 3)
                pe.wait_ge(s["d_lo"], 1)

                def step(g):
                    for k in range(8):
                        if not isinstance(g, int) or g >= 0:
                            if k == 0:
                                pe.wait_ge(s["dT_lo"], g + 1)
                            after(pe, s["e_ready"], 8 * g + k - 3)
                            split_product(pe, PB[k % 4][0:R, :], [w[:, k] for w in w8], [tok(x, g) for x in xT]
                                          ).then_inc(s["e_psum"], 1)
                        if k == 3 and (not isinstance(g, int) or g + 1 < G):
                            pe.wait_ge(s["dxn"], g + 2)
                            after(pe, s["dT_lo"], g + 1)
                            for i in range(GB):
                                last = pe.transpose(PT[:, 128 * i:128 * i + 128], xn[:, i, :], ident[:])
                            last.then_inc(s["dT_psum"], 1)
                over_groups(pe, step, -1, G - 1)

        identb = sb("identb", [128, 128], BF16)
        cm = sb("cm", [128, 128], BF16)
        cmT = sb("cmT", [128, 128], BF16)
        gm = sb("gm", [128, NG * HD])
        nsel = sb("nsel", [32, 4, 128], BF16)
        mx = sb("mxd", [128, 16])
        m2 = sb("m2", [128, 32], BF16)
        mT = sb("mTd", [32, 128], BF16)
        Vq = [sb(f"Vq{i}", [128, 4, NG * HD]) for i in range(2)]
        xq = [[sb(f"xq{k}_{i}", [C, 4, NG, T], F16) for i in range(2)] for k in range(2)]
        P = [sb(f"Pd{i}", [128, 4, 128]) for i in range(2)]
        Dn = sb("Dn", [128, 512])
        Dr = sb("Dr", [128, 512])
        Af = sb("Af", [128, 512])
        u = room.sems("""f_consts f_ident ds_psum ds_max dm_hi dm_ready dmT_psum dmT_ready dt_psum dp_ready dv_psum
            dv_ready pv_done dd_sb dd_inv at_f at_hi at_lo xq_hi xq_lo carrier3""")
        SB, T0, T1, VM, MT, O, D = bank[:7]
        TB = [T0, T1]

        def has(q):
            return not isinstance(q, int) or 0 <= q < QUADS

        def sweep(eng, step):
            for q in range(-2, 4):
                step(q, q % 4, q // 4)
            with eng.Fori(1, QUADS // 4 - 1) as x:
                for i in range(4):
                    step(4 * x + i, i, x)
            for q in range(QUADS - 4, QUADS + 1):
                step(q, q % 4, q // 4)

        def at_position(k0, pos):
            v = QK[:, k0:k0 + 4].rearrange("r k (s p) -> r (k s) p", p=S)
            return v[:, :, pos] if isinstance(pos, int) else v[:, :, bass.ds(pos, 1)].rearrange("r x a -> r (x a)")

        def x_quad(t, q):
            at = slice(4 * q, 4 * q + 4) if isinstance(q, int) else bass.ds(4 * q, 4)
            v = t[:].rearrange("c (s p) -> c p s", p=S)[:, at]
            return v.unsqueeze(2).broadcast_to([C, 4, NG, T])

        def hexcols(t, x):
            return t[:, 512 * x:512 * x + 512] if isinstance(x, int) else t[:, bass.ds(512 * x, 512)]

        with nc.Block() as block:
            @block.gpsimd
            def _(pool):
                pool.tensor_copy(identb[:], ident[:])
                pool.memset(cm[:], 0.0)
                pool.memset(cmT[:], 0.0)
                pool.memset(gm[:], 0.0)
                pool.memset(nsel[:], 0.0).then_inc(u["f_consts"], 1)
                pool.wait_ge(u["f_consts"], 1)
                for g in range(4):
                    rows = slice(32 * g, 32 * g + 32)
                    pool.affine_select(out=cm[rows].rearrange("p (g t) -> p g t", g=4),
                                       in_=cm[rows].rearrange("p (g t) -> p g t", g=4), compare_op=ALU.is_ge,
                                       fill=LOWEST, base=0, pattern=[[0, 4], [-1, T]], channel_multiplier=1)
                    pool.affine_select(out=cmT[rows].rearrange("p (l s) -> p l s", l=4),
                                       in_=cmT[rows].rearrange("p (l s) -> p l s", l=4), compare_op=ALU.is_ge,
                                       fill=LOWEST, base=0, pattern=[[0, 4], [1, T]], channel_multiplier=-1)
                    pool.memset(gm[rows, HD * g:HD * g + HD], 1.0)
                nv = nsel[:].rearrange("r p (g t) -> r p g t", g=4)
                for k in range(2):
                    pool.affine_select(out=nv, in_=nv, compare_op=ALU.not_equal, fill=-1.0, base=-16 * k,
                                       pattern=[[-4, 4], [-1, 4], [0, T]], channel_multiplier=1
                                       ).then_inc(u["f_consts"], 1)
                    pool.wait_ge(u["f_consts"], 2 + k)

            @block.scalar
            def _(act):
                def step(q, i, x):
                    if has(q + 2):
                        after_alone(act, u["dv_psum"], q + 1, u["carrier3"])
                        act.activation(xq[0][i % 2][:], x_quad(xT[0], q + 2), ACT.Copy).then_inc(u["xq_hi"], 1)
                    if has(q):
                        act.wait_ge(u["dmT_psum"], q + 1)
                        after(act, u["dt_psum"], q)
                        act.activation(mT[:], MT[0:32, 0:64].bitcast(BF16), ACT.Copy).then_inc(u["dmT_ready"], 1)
                    done = i == 0 and has(q - 1)
                    if done:
                        act.wait_ge(u["pv_done"], q)
                        act.activation(Dn[:], D[:], ACT.Copy).then_inc(u["dd_sb"], 1)
                    if has(q):
                        act.wait_ge(u["dt_psum"], q + 1)
                        after(act, u["pv_done"], q - 1)
                        act.activation(P[i % 2][:].rearrange("p a x -> p (a x)"), TB[i % 2][:], ACT.Exp, scale=SCALE
                                       ).then_inc(u["dp_ready"], 1)
                    if done:
                        act.wait_ge(u["at_f"], x)
                        act.activation(hexcols(AT[0], x - 1), Af[:], ACT.Identity, bias=bv[:]).then_inc(u["at_hi"], 1)
                sweep(act, step)

            @block.vector
            def _(dve):
                dve.wait_ge(u["f_consts"], 3)

                def step(q, i, x):
                    if i == 1:
                        after(dve, u["at_lo"], x)
                    if has(q + 1):
                        dve.wait_ge(u["ds_psum"], q + 2)
                        after(dve, u["dm_ready"], q + 1)
                        dve.tensor_reduce(mx[:], SB[:].rearrange("p (a t) -> p a t", t=T), AX.X, ALU.max
                                          ).then_inc(u["ds_max"], 1)
                        dve.wait_ge(u["ds_max"], q + 2)
                        after(dve, u["dmT_psum"], q + 1)
                        dve.tensor_copy(m2[:, 0:16], mx[:]).then_inc(u["dm_hi"], 1)
                        dve.wait_ge(u["dm_hi"], q + 2)
                        dve.tensor_tensor(m2[:, 16:32], mx[:], m2[:, 0:16], ALU.subtract).then_inc(u["dm_ready"], 1)
                    done = i == 0 and has(q - 1)
                    if done:
                        dve.wait_ge(u["dd_sb"], x)
                        dve.reciprocal(Dr[:], Dn[:]).then_inc(u["dd_inv"], 1)
                        dve.wait_ge(u["dd_inv"], x)
                        dve.tensor_tensor(Af[:], O[:], Dr[:], ALU.mult).then_inc(u["at_f"], 1)
                    if has(q + 1):
                        dve.wait_ge(u["dv_psum"], q + 2)
                        after(dve, u["pv_done"], q)
                        dve.tensor_tensor(Vq[(i + 1) % 2][:], VM[:, 0:128].rearrange("p (a x) -> p a x", a=4),
                                          gm[:].unsqueeze(1).broadcast_to([128, 4, NG * HD]), ALU.mult
                                          ).then_inc(u["dv_ready"], 1)
                    if has(q + 2):
                        after_alone(dve, u["dv_psum"], q + 1, u["carrier3"])
                        dve.tensor_copy(xq[1][i % 2][:], x_quad(xT[1], q + 2)).then_inc(u["xq_lo"], 1)
                    if done:
                        dve.wait_ge(u["at_hi"], x)
                        dve.scalar_tensor_tensor(hexcols(AT[1], x - 1), Af[:], bv[:], hexcols(AT[0], x - 1),
                                                 ALU.add, ALU.subtract).then_inc(u["at_lo"], 1)
                sweep(dve, step)

            @block.tensor
            def _(pe):
                pe.wait_ge(u["f_consts"], 3)

                def step(q, i, x):
                    if has(q):
                        pe.wait_ge(u["dm_ready"], q + 1)
                        after(pe, u["dmT_ready"], q)
                        pe.transpose(MT[0:32, 0:64].bitcast(BF16), m2[:], identb[:]).then_inc(u["dmT_psum"], 1)
                    if has(q + 1):
                        after(pe, u["ds_max"], q + 1)
                        for p in range(4):
                            pe.matmul(SB[:, 128 * p:128 * p + 128], at_position(0, 4 * (q + 1) + p),
                                      at_position(4, 4 * (q + 1) + p), start=(p == 0), stop=False,
                                      skip_group_check=True)
                        pe.matmul(SB[:], identb[:], cm[:].unsqueeze(1).broadcast_to([128, 4, 128]),
                                  start=False, stop=True, skip_group_check=True).then_inc(u["ds_psum"], 1)
                    if has(q):
                        after(pe, u["dp_ready"], q - 1)
                        for p in range(4):
                            pe.matmul(TB[i % 2][:, 128 * p:128 * p + 128], at_position(4, 4 * q + p),
                                      at_position(0, 4 * q + p), start=(p == 0), stop=False, skip_group_check=True)
                        pe.matmul(TB[i % 2][:], identb[:], cmT[:].unsqueeze(1).broadcast_to([128, 4, 128]),
                                  start=False, stop=False, skip_group_check=True)
                    if has(q + 1):
                        after(pe, u["dv_ready"], q + 1)
                        pe.wait_ge(u["xq_hi"], q + 2)
                        pe.wait_ge(u["xq_lo"], q + 2)
                        for p in range(4):
                            last = split_product(pe, VM[:, 32 * p:32 * p + 32],
                                                 [t[(i + 1) % 2][:, p].rearrange("c g t -> c (g t)") for t in xq], [w[:] for w in wv])
                        last.then_inc(u["dv_psum"], 1)
                    if has(q):
                        pe.wait_ge(u["dmT_ready"], q + 1)
                        for p in range(4):
                            last = pe.matmul(TB[i % 2][:, 128 * p:128 * p + 128], nsel[:, p, :], mT[:],
                                             start=False, stop=True, skip_group_check=True)
                        last.then_inc(u["dt_psum"], 1)
                    if has(q - 1):
                        k = (i - 1) % 4
                        pe.wait_ge(u["dp_ready"], q)
                        pe.wait_ge(u["dv_ready"], q)
                        if k == 0:
                            after(pe, u["at_f"], x)
                        for p in range(4):
                            for l in range(4):
                                pe.matmul(O[32 * l:32 * l + 32, 128 * k + 32 * p:128 * k + 32 * p + 32],
                                          Vq[k % 2][:, p, :], P[k % 2][:, p, 32 * l:32 * l + 32],
                                          start=True, stop=True, tile_position=(0, 32 * l))
                        for l in range(4):
                            last = pe.matmul(D[32 * l:32 * l + 32, 128 * k:128 * k + 128], gm[:],
                                             P[k % 2][:, :, 32 * l:32 * l + 32], start=True, stop=True,
                                             tile_position=(0, 32 * l))
                        last.then_inc(u["pv_done"], 1)
                sweep(pe, step)
    return room


def experts1(nc, d, bank, keep, X3, H, AT, wp, out):
    ident, ones = keep["ident"], keep["ones"]
    NB, LAG, RING = 2 * NE, 3, 4
    GSTEPS = 12
    with ExitStack() as ctx:
        room = Room(nc, ctx, "moe")
        sb = room.sb
        w1r = sb("w1r", [C, NB, 128])
        w2r = sb("w2r", [128, NB, C])
        w1 = [sb(f"w1_{i}", [C, NB, 128], F16) for i in range(2)]
        w2 = [sb(f"w2_{i}", [128, NB, C], F16) for i in range(2)]
        rw = sb("rw", [NE, C])
        rT = sb("rT", [C, NE])
        r16 = [sb(f"r16_{i}", [C, NE], F16) for i in range(2)]
        lnw = sb("lnw2", [C, 1])
        lnb = sb("lnb2", [C, 1])
        lnbr = sb("lnbr", [C, 128])
        b1 = sb("b1", [128, NB])
        rb = sb("rb", [128, NE])
        before8 = sb("before8e", [128, NE, NE])
        half = sb("half3", [128, GB])
        xT = [sb(f"xTe{i}", [C, B * S], F16) for i in range(2)]
        st = sb("st3", [128, GB, 6])
        mv = sb("mv3", [128, GB, 2])
        rs = sb("rs3", [128, 2, GB])
        xn = sb("xn3", [S, GB, C])
        lg = sb("lg", [128, GB, NE])
        pr = sb("pr", [128, GB, NE])
        r1 = sb("r1", [128, 3, GB])
        c8 = sb("c8e", [128, 3, GB, NE, NE])
        cnt = sb("cnte", [128, GB, NE])
        sel = sb("sele", [128, GB, NE])
        wgt = sb("wgte", [128, B, NE])
        hm = sb("hme", [128, RING, N])
        hp = [sb(f"hpe{i}", [128, RING, N], F16) for i in range(2)]
        s = room.sems("""router_loaded moe_loaded e_consts e_rT e_rTs e_bias e_split e_b pj_psum ph_ready st_e mv_e eps_e
            rs_e r_ready xn_e xT_e_psum xTe_hi xTe_lo lg_psum g_in g_exp g_step wgt_ready up_psum gelu hi_e lo_e
            down_psum x4_step x4_ready stored carrier4""")
        UP, Y, PX, LG = bank[0:4], bank[4:6], bank[6], bank[7]

        def xg(t, g):
            return t[:, GB * g:GB * g + GB, :] if isinstance(g, int) else t[:, bass.ds(GB * g, GB), :]

        def nxt(g):
            return not isinstance(g, int) or g + 1 < G

        def cur(g):
            return not isinstance(g, int) or g >= 0

        def late(g, p, lag):
            h = g if p >= lag else g - 1
            return (h, (p - lag) % NB) if cur(h) else None

        with nc.Block() as block:
            @block.sync
            def _(sp):
                sp.dma_start(rw[:], d["L1_ffn_router_weight"]).then_inc(s["router_loaded"], 16)
                sp.dma_start(lnw[:], d["L1_ffn_ln2_weight"].rearrange("(h a) -> h a", a=1)).then_inc(s["router_loaded"], 16)
                sp.dma_start(lnb[:], d["L1_ffn_ln2_bias"].rearrange("(h a) -> h a", a=1)).then_inc(s["router_loaded"], 16)
                sp.dma_start(w1r[:].rearrange("c (e b) f -> c e (b f)", b=2),
                             d["L1_ffn_moe_w1"].rearrange("e c f -> c e f")).then_inc(s["moe_loaded"], 16)
                sp.dma_start(w2r[:].rearrange("i (e b) c -> i e b c", b=2),
                             d["L1_ffn_moe_w2"].rearrange("e (b i) c -> i e b c", b=2)).then_inc(s["moe_loaded"], 16)

                def store(g):
                    wait_alone(sp, s["x4_ready"], g + 1, s["carrier4"])
                    dst = out[GB * g:GB * g + GB] if isinstance(g, int) else out[bass.ds(GB * g, GB)]
                    sp.dma_start(dst.rearrange("b s c -> s b c"), xg(X3, g)).then_inc(s["stored"], 16)
                    wait_alone(sp, s["stored"], 16 * (g + 1), s["carrier4"])
                over_groups(sp, store, 0, G - 1)

            @block.gpsimd
            def _(pool):
                pool.memset(half[:], -0.5)
                pool.memset(before8[:], 1.0).then_inc(s["e_consts"], 1)
                pool.wait_ge(s["e_consts"], 1)
                pool.affine_select(out=before8[:], in_=before8[:], compare_op=ALU.is_gt, fill=0.0, base=0,
                                   pattern=[[1, NE], [-1, NE]], channel_multiplier=0).then_inc(s["e_consts"], 1)

                def step(g):
                    for p in range(NB):
                        if nxt(g) and p == 2:
                            wait_alone(pool, s["mv_e"], g + 2, s["carrier4"])
                            pool.tensor_scalar(rs[:, 0, :], mv[:, :, 1], 1.0, LN_EPS, ALU.mult, ALU.add
                                               ).then_inc(s["eps_e"], 1)
                            pool.wait_ge(s["eps_e"], g + 2)
                            pool.tensor_tensor(rs[:, 1, :], rs[:, 0, :], half[:], ALU.pow).then_inc(s["rs_e"], 1)
                        if nxt(g) and p == 9:
                            pool.tensor_tensor(xg(X3, g + 1), xg(X3, g + 1), xg(H, g + 1), ALU.add
                                               ).then_inc(s["r_ready"], 1)
                        if cur(g):
                            pool.wait_ge(s["hi_e"], NB * g + p + 1)
                            pool.tensor_tensor(hp[1][:, p % RING], hm[:, p % RING], hp[0][:, p % RING], ALU.subtract
                                               ).then_inc(s["lo_e"], 1)
                over_groups(pool, step, -1, G - 1)

            @block.scalar
            def _(act):
                act.wait_ge(s["e_rT"], 1)
                act.activation(rT[:], LG[:, 0:NE], ACT.Copy).then_inc(s["e_rTs"], 1)
                act.wait_ge(s["e_rTs"], 1)
                act.activation(r16[0][:], rT[:], ACT.Copy, scale=lnw[:])
                act.activation(lnbr[:], ones[:], ACT.Copy, scale=lnb[:]).then_inc(s["e_bias"], 1)
                act.wait_ge(s["moe_loaded"], 32)
                act.activation(w1[0][:], w1r[:], ACT.Copy, scale=lnw[:])
                act.activation(w2[0][:], w2r[:], ACT.Copy).then_inc(s["e_split"], 1)
                act.wait_ge(s["e_b"], 1)
                act.activation(b1[:], PX[:, 0:NB], ACT.Copy)
                act.activation(rb[:], PX[:, NB:NB + NE], ACT.Copy).then_inc(s["e_bias"], 1)
                act.wait_ge(s["e_bias"], 2)

                def step(g):
                    for p in range(NB):
                        k = NB * g + p
                        if cur(g):
                            act.wait_ge(s["up_psum"], k + 1)
                            after(act, s["lo_e"], k - RING + 1)
                            act.activation(hm[:, p % RING], UP[p % RING][:], ACT.Gelu_apprx_tanh, bias=b1[:, p:p + 1]
                                           ).then_inc(s["gelu"], 1)
                        if nxt(g) and p == 6:
                            act.wait_ge(s["xT_e_psum"], g + 2)
                            act.activation(tok(xT[0], g + 1), PX[:], ACT.Copy).then_inc(s["xTe_hi"], 1)
                        if nxt(g) and p == 9:
                            act.wait_ge(s["g_in"], g + 2)
                            act.activation(pr[:].rearrange("p b e -> p (b e)"), lg[:].rearrange("p b e -> p (b e)"),
                                           ACT.Exp).then_inc(s["g_exp"], 1)
                over_groups(act, step, -1, G - 1)

            @block.vector
            def _(dve):
                dve.wait_ge(s["e_bias"], 1)
                dve.scalar_tensor_tensor(r16[1][:], rT[:], lnw[:], r16[0][:], ALU.mult, ALU.subtract)
                dve.wait_ge(s["e_split"], 1)
                dve.scalar_tensor_tensor(w1[1][:], w1r[:], lnw[:], w1[0][:], ALU.mult, ALU.subtract)
                dve.tensor_tensor(w2[1][:], w2r[:], w2[0][:], ALU.subtract).then_inc(s["e_split"], 1)
                dve.wait_ge(s["e_bias"], 2)
                dve.wait_ge(s["e_consts"], 2)
                steps = 0

                def link(g, ins):
                    nonlocal steps
                    steps += 1
                    ins.then_inc(s["g_step"], 1)
                    dve.wait_ge(s["g_step"], GSTEPS * g + steps)

                def gate(g, p):
                    nonlocal steps
                    wide = [128, GB, NE]
                    deep = [128, GB, NE, NE]
                    if p == 8:
                        steps = 0
                        dve.wait_ge(s["lg_psum"], g + 1)
                        link(g, dve.tensor_tensor(lg[:], LG[:, 0:GB * NE].rearrange("p (b e) -> p b e", e=NE),
                                                  rb[:].unsqueeze(1).broadcast_to(wide), ALU.add))
                        link(g, dve.tensor_reduce(r1[:, 0], lg[:], AX.X, ALU.max))
                        dve.tensor_tensor(lg[:], lg[:], r1[:, 0].unsqueeze(2).broadcast_to(wide), ALU.subtract
                                          ).then_inc(s["g_in"], 1)
                    elif p == 10:
                        dve.wait_ge(s["g_exp"], g + 1)
                        link(g, dve.tensor_reduce(r1[:, 1], pr[:], AX.X, ALU.add))
                        link(g, dve.reciprocal(r1[:, 2], r1[:, 1]))
                        link(g, dve.tensor_tensor(pr[:], pr[:], r1[:, 2].unsqueeze(2).broadcast_to(wide), ALU.mult))
                    elif p == 11:
                        other = pr[:].unsqueeze(2).broadcast_to(deep)
                        own = pr[:].unsqueeze(3).broadcast_to(deep)
                        dve.tensor_tensor(c8[:, 0], other, own, ALU.is_gt)
                        link(g, dve.tensor_tensor(c8[:, 1], other, own, ALU.is_equal))
                    elif p == 12:
                        tie = before8[:].unsqueeze(1).broadcast_to(deep)
                        link(g, dve.tensor_tensor(c8[:, 2], c8[:, 1], tie, ALU.mult))
                        link(g, dve.tensor_tensor(c8[:, 1], c8[:, 0], c8[:, 2], ALU.add))
                    elif p == 13:
                        link(g, dve.tensor_reduce(cnt[:], c8[:, 1], AX.X, ALU.add))
                        link(g, dve.tensor_scalar(sel[:], cnt[:], 2.0, None, ALU.is_lt))
                        link(g, dve.tensor_tensor(sel[:], sel[:], pr[:], ALU.mult))
                        link(g, dve.tensor_copy(xg(wgt, g), sel[:]))
                        assert steps == GSTEPS

                def prep(g, p):
                    if p == 0:
                        wait_alone(dve, s["pj_psum"], g + 1, s["carrier4"])
                        h = xg(H, g).rearrange("p b c -> p (b c)")
                        dve.tensor_tensor(h, PX[:], h, ALU.add).then_inc(s["ph_ready"], 1)
                    elif p == 1:
                        wait_alone(dve, s["ph_ready"], g + 1, s["carrier4"])
                        for i in range(GB):
                            last = dve.bn_stats(st[:, i, :], xg(H, g)[:, i, :])
                        last.then_inc(s["st_e"], 1)
                        wait_alone(dve, s["st_e"], g + 1, s["carrier4"])
                        for i in range(GB):
                            last = dve.bn_aggr(mv[:, i, :], st[:, i, :])
                        last.then_inc(s["mv_e"], 1)
                    elif p == 4:
                        wait_alone(dve, s["rs_e"], g + 1, s["carrier4"])
                        for i in range(GB):
                            last = dve.tensor_scalar(xn[:, i, :], xg(H, g)[:, i, :], mv[:, i, 0:1],
                                                     rs[:, 1, i:i + 1], ALU.subtract, ALU.mult)
                        last.then_inc(s["xn_e"], 1)
                    elif p == 6:
                        dve.wait_ge(s["xTe_hi"], g + 1)
                        dve.tensor_tensor(tok(xT[1], g), PX[:], tok(xT[0], g), ALU.subtract).then_inc(s["xTe_lo"], 1)
                    else:
                        gate(g, p)

                def combine(at):
                    if at is None:
                        return
                    g, p = at
                    e = p // 2
                    wait_alone(dve, s["down_psum"], NB * g + p + 1, s["carrier4"])
                    if e == 0:
                        wait_alone(dve, s["r_ready"], g + 1, s["carrier4"])
                    else:
                        wait_alone(dve, s["x4_step"], (NE - 1) * g + e, s["carrier4"])
                    for i in range(GB):
                        x = xg(X3, g)[:, i, :]
                        w = xg(wgt, g)[:, i, e:e + 1]
                        last = dve.scalar_tensor_tensor(x, Y[e % 2][:, 128 * i:128 * i + 128], w, x, ALU.mult, ALU.add)
                    last.then_inc(s["x4_ready" if e == NE - 1 else "x4_step"], 1)

                def step(g):
                    for p in range(NB):
                        if cur(g):
                            dve.wait_ge(s["gelu"], NB * g + p + 1)
                            after(dve, s["down_psum"], NB * g + p - RING + 1)
                            dve.tensor_copy(hp[0][:, p % RING], hm[:, p % RING]).then_inc(s["hi_e"], 1)
                        if p % 2 == 0:
                            combine(late(g, p, LAG + 2))
                        if nxt(g):
                            prep(g + 1, p)
                over_groups(dve, step, -1, G - 1)
                for e in (NE - 3, NE - 2, NE - 1):
                    combine((G - 1, 2 * e + 1))

            @block.tensor
            def _(pe):
                pe.wait_ge(s["router_loaded"], 48)
                pe.transpose(LG[:, 0:NE], rw[:], ident[0:NE, 0:NE]).then_inc(s["e_rT"], 1)
                pe.wait_ge(s["e_bias"], 1)
                pe.wait_ge(s["moe_loaded"], 32)
                for p in range(NB):
                    pe.matmul(PX[:, p:p + 1], w1r[:, p], lnb[:], start=True, stop=True)
                pe.matmul(PX[:, NB:NB + NE], lnbr[:], rT[:], start=True, stop=True).then_inc(s["e_b"], 1)
                pe.wait_ge(s["e_split"], 2)
                pe.wait_ge(s["e_bias"], 2)

                def prep(g, p):
                    if p == 0:
                        after(pe, s["xTe_lo"], g)
                        for i in range(GB):
                            b = GB * g + i
                            a = [t[:].rearrange("r (p s) -> r s p", s=B)[:, b, :] if isinstance(b, int) else
                                 t[:].rearrange("r (p s) -> r s p", s=B)[:, bass.ds(b, 1), :]
                                 .rearrange("r a p -> r (a p)") for t in AT]
                            last = split_product(pe, PX[:, 128 * i:128 * i + 128], a, [w[:] for w in wp])
                        last.then_inc(s["pj_psum"], 1)
                    elif p == 5:
                        pe.wait_ge(s["xn_e"], g + 1)
                        for i in range(GB):
                            last = pe.transpose(PX[:, 128 * i:128 * i + 128], xn[:, i, :], ident[:])
                        last.then_inc(s["xT_e_psum"], 1)
                    elif p == 7:
                        pe.wait_ge(s["xTe_lo"], g + 1)
                        for i in range(GB):
                            last = split_product(pe, LG[:, NE * i:NE * i + NE], [tok(t, g, 128 * i, 128) for t in xT],
                                                 [r[:] for r in r16])
                        last.then_inc(s["lg_psum"], 1)

                def down(at):
                    if at is None:
                        return
                    g, p = at
                    e = p // 2
                    pe.wait_ge(s["lo_e"], NB * g + p + 1)
                    if p % 2 == 0:
                        if e >= 2:
                            pe.wait_ge(s["x4_step"], (NE - 1) * g + e - 1)
                        elif e == 0:
                            after(pe, s["x4_step"], (NE - 1) * g)
                        else:
                            after(pe, s["x4_ready"], g)
                    for i in range(GB):
                        cols = slice(128 * i, 128 * i + 128)
                        last = split_product(pe, Y[e % 2][:, cols], [h[:, p % RING, cols] for h in hp],
                                             [w[:, p] for w in w2], start=(p % 2 == 0 and i == 0),
                                             stop=(p % 2 == 1), skip_group_check=True)
                    last.then_inc(s["down_psum"], 1)

                def step(g):
                    for p in range(NB):
                        k = NB * g + p
                        if cur(g):
                            if p == 0:
                                pe.wait_ge(s["xTe_lo"], g + 1)
                            after(pe, s["gelu"], k - RING + 1)
                            split_product(pe, UP[p % RING][:], [w[:, p] for w in w1], [tok(t, g) for t in xT]
                                          ).then_inc(s["up_psum"], 1)
                        if nxt(g):
                            prep(g + 1, p)
                        down(late(g, p, LAG))
                over_groups(pe, step, -1, G - 1)
                for p in range(NB - LAG, NB):
                    down((G - 1, p))


def build(nc, d, out):
    with ExitStack() as ctx:
        room = Room(nc, ctx, "program")
        bank = [ctx.enter_context(nc.psum_tensor(f"bank{i}", [128, 512], F32)) for i in range(8)]
        keep = {
            "X": room.sb("X", [S, B, C]),
            "ident": room.sb("ident", [128, 128]),
            "ident16": room.sb("ident16", [128, 128], F16),
            "ones": room.sb("ones", [128, 128]),
        }
        X3 = room.sb("X3", [S, B, C])
        with ExitStack() as inner:
            keep["cT"] = [Room(nc, inner, "context").sb(f"cT{i}", [CT + 1, B * S], F16) for i in range(2)]
            layer0(nc, d, bank, keep).end()
            attention1(nc, d, bank, keep, X3).end()
        AT = [room.sb(f"AT{i}", [C, S * B], F16) for i in range(2)]
        wp = [room.sb(f"wp{i}", [C, C], F16) for i in range(2)]
        attention2(nc, d, bank, keep, X3, keep["X"], AT, wp)
        experts1(nc, d, bank, keep, X3, keep["X"], AT, wp, out)


def kernel(**inputs):
    import numpy as np
    import concourse.bacc as bacc
    from concourse.bass_utils import run_bass_kernel_spmd as run

    nc = bacc.Bacc("TRN2", target_bir_lowering=False, num_devices=1)
    arrays, d = {}, {}
    for name, value in inputs.items():
        a = np.ascontiguousarray(value)
        arrays["in_" + name] = a
        d[name] = nc.dram_tensor("in_" + name, a.shape, mybir.dt.from_np(a.dtype), kind="ExternalInput").ap()
    out = nc.dram_tensor("out_x", (B, S, C), F32, kind="ExternalOutput").ap()
    build(nc, d, out)
    r = run(nc, [arrays], core_ids=[0])
    return r.results[0]["out_x"]
```

```python
from contextlib import ExitStack

import concourse.bass as bass
from concourse import mybir

F32 = mybir.dt.float32
F16 = mybir.dt.float16
BF16 = mybir.dt.bfloat16
ALU = mybir.AluOpType
ACT = mybir.ActivationFunctionType
AX = mybir.AxisListType

B, S, C, CT = 32, 128, 128, 96
GB = 4
G = B // GB
N = GB * S
NE = 8
DV = 64
NH, HD = 16, 8
LN_EPS = 1e-5
COS_EPS = 1e-8
ROUTED_SCALE = 2.5
GATE_STEPS = 20
NBLK = NE * 64 // C + 1


def after(eng, sem, value):
    if not isinstance(value, int) or value > 0:
        eng.wait_ge(sem, value)


def wait_alone(eng, sem, value, carrier):
    eng.wait_ge(sem, value)
    if not isinstance(value, int):
        eng.sem_inc(carrier, 1)


def after_alone(eng, sem, value, carrier):
    if not isinstance(value, int) or value > 0:
        wait_alone(eng, sem, value, carrier)


def before(k, p):
    return k - 1 if p == 0 else k - 3 if p == 1 else k - 2


def over_groups(eng, step, first, last):
    step(first)
    step(first + 1)
    with eng.Fori(first + 2, last) as g:
        step(g)
    step(last)


class Room:

    def __init__(self, nc, ctx, part):
        self.nc, self.ctx, self.part, self.held = nc, ctx, part, []

    def sb(self, name, shape, dt=F32):
        return self.ctx.enter_context(self.nc.sbuf_tensor(name, shape, dt))

    def sems(self, names):
        got = {n: self.nc.alloc_semaphore(f"{self.part}_{n}") for n in names.split()}
        self.held += got.values()
        return got

    def end(self):
        self.nc.clear_and_free_semaphores(self.held)
        self.nc.all_engine_barrier()


def tok(t, g, lo=0, n=N, rows=None):
    at = g * N + lo
    cols = slice(at, at + n) if isinstance(g, int) else bass.ds(at, n)
    return t[:, cols] if rows is None else t[0:rows, cols]


def split_product(pe, ps, lhs, rhs, start=True, stop=True, **kw):
    pe.matmul(ps, lhs[0], rhs[0], start=start, stop=False, **kw)
    pe.matmul(ps, lhs[0], rhs[1], start=False, stop=False, **kw)
    return pe.matmul(ps, lhs[1], rhs[0], start=False, stop=stop, **kw)


def layer1_weights(room, d):
    sb = room.sb
    w = {
        "wq": sb("wq_raw", [C, C]), "wk": sb("wk_raw", [CT + 1, C]), "wv": sb("wv_raw", [CT + 1, C]),
        "wo": sb("wo", [C, C]), "bo": sb("bo", [1, C]), "bq": sb("bq_raw", [2, C]),
        "qw": sb("qw", [128, C]), "kvw": sb("kvw", [64, C]), "pw": sb("pw", [C, 128]),
        "ln1_w": sb("ln1_w", [C, 1]), "ln1_b": sb("ln1_b", [C, 1]),
        "rw": sb("rw", [NE, C]), "ln2_w": sb("ln2_w", [C, 1]), "ln2_b": sb("ln2_b", [C, 1]),
        "w1": sb("w1r", [C, 2 * NE, 128]), "w2": sb("w2r", [128, 2 * NE, C]),
    }
    moves = [
        (w["wq"][:], d["L1_xattn_Wq"]), (w["wo"][:], d["L1_xattn_Wo"]),
        (w["wk"][0:CT, :], d["L1_xattn_Wk"]), (w["wv"][0:CT, :], d["L1_xattn_Wv"]),
        (w["wk"][CT:CT + 1, :], d["L1_xattn_bk"].rearrange("(a c) -> a c", a=1)),
        (w["wv"][CT:CT + 1, :], d["L1_xattn_bv"].rearrange("(a c) -> a c", a=1)),
        (w["bq"][:], d["L1_xattn_bq"].partition_broadcast(2)),
        (w["bo"][:], d["L1_xattn_bo"].rearrange("(a c) -> a c", a=1)),
        (w["qw"][:], d["L1_ffn_qkv_weight"][0:128]), (w["kvw"][:], d["L1_ffn_qkv_weight"][128:192]),
        (w["pw"][:], d["L1_ffn_proj_weight"]), (w["rw"][:], d["L1_ffn_router_weight"]),
        (w["w1"][:].rearrange("c (e b) f -> c e (b f)", b=2), d["L1_ffn_moe_w1"].rearrange("e c f -> c e f")),
        (w["w2"][:].rearrange("i (e b) c -> i e b c", b=2),
         d["L1_ffn_moe_w2"].rearrange("e (b i) c -> i e b c", b=2)),
    ]
    moves += [(w[f"ln{i}_{k[0]}"][:], d[f"L1_ffn_ln{i}_{k}"].rearrange("(h a) -> h a", a=1))
              for i in (1, 2) for k in ("weight", "bias")]
    return w, moves


def layer0(nc, d, bank, keep):
    X, ident, ident16, ones, cT = keep["X"], keep["ident"], keep["ident16"], keep["ones"], keep["cT"]
    ctx_sum = keep["ctx_sum"]
    with ExitStack() as ctx:
        room = Room(nc, ctx, "layer0")
        sb = room.sb
        xT = [sb(f"xT{i}", [C, B * S], F16) for i in range(2)]
        wvh_raw = sb("wvh_raw", [DV, C])
        wth_raw = sb("wth_raw", [DV, CT])
        bv0 = sb("bv0", [DV, 1])
        bt0 = sb("bt0", [DV, 1])
        wv0 = [sb(f"wv0_{i}", [C, DV], F16) for i in range(2)]
        wt0 = [sb(f"wt0_{i}", [CT, DV], F16) for i in range(2)]
        gw_raw = sb("gw_raw", [C, NE])
        gw = [sb(f"gw{i}", [C, NE], F16) for i in range(2)]
        gbias = sb("gbias", [128, NE])
        w_raw = sb("w_raw", [128, 3, NBLK, 128])
        w0 = [sb(f"w0_{i}", [128, 3, NBLK, 128], F16) for i in range(2)]
        before4 = sb("before4", [128, 4, 4])
        before8 = sb("before8", [128, NE, NE])
        pick = sb("pick", [2 * NE, NBLK - 1, 128], F16)
        cload = sb("cload", [S, GB, CT])
        st = {k: sb("st" + k, [128, GB, 6]) for k in "AB"}
        mv = {k: sb("mv" + k, [128, GB, 2]) for k in "AB"}
        rs = {k: sb("rs" + k, [128, 2, GB]) for k in "AB"}
        half = sb("half", [128, 8])
        xn = {k: sb("xn" + k, [S, GB, C]) for k in "AB"}
        vt = [sb(f"vt{i}", [DV, N]) for i in range(2)]
        sq = sb("sq", [DV, 2, N])
        n2 = sb("n2", [128, 2 * GB])
        rn = sb("rn", [128, 2 * GB])
        dg = sb("dg", [128, GB, 128])
        wm = sb("wm", [128, GB, 128])
        th = sb("th", [128, GB, NE])
        sfc = sb("sfc", [128, GB, NE])
        gs = sb("gs", [128, GB, 4])
        c4 = sb("c4", [128, 3, GB, 4, 4])
        cnt4 = sb("cnt4", [128, 2, GB, 4])
        tmp8 = sb("tmp8", [128, GB, NE])
        c8 = sb("c8", [128, 3, GB, NE, NE])
        cnt8 = sb("cnt8", [128, GB, NE])
        sel = sb("sel", [128, GB, NE])
        den0 = sb("den0", [128, 2, GB])
        wgt = sb("wgt", [128, GB, NE])
        wst = sb("wst", [128, GB, 2 * NE], F16)
        eT = sb("eT", [2 * NE, B * S], F16)
        sg = sb("sg", [128, 2, N])
        su = sb("su", [128, 2, N])
        hm = sb("hm", [128, 2, N])
        hp = [sb(f"hp{i}", [128, NBLK, N], F16) for i in range(2)]
        xa = [sb(f"xa{i}", [C, N], F16) for i in range(2)]

        names = """consts bf_ready w_raw_loaded small_loaded gate_loaded wTr_ready w0_split w0t_split pow_const
            x_loaded c_loaded stA mvA epsA rsA xnA cT_psum xnT_psum cT_hi cT_lo xA_hi xA_lo vt_psum vt_sb
            sq_ready dots_psum n2_ready rn_ready dg_ready rb_psum wm_min wm_ready x1_ready
            stB mvB epsB rsB xnB xBT_psum xB_hi xB_lo logit_psum th_ready gate_step carrier wst_ready eT_psum eT_ready
            gu_psum sg_ready su_ready hm_ready hi_ready lo_ready down_psum x2_ready layer1_loaded"""
        s = room.sems(names)
        block = ctx.enter_context(nc.Block())

        def xg(g):
            return X[:, bass.ds(GB * g, GB), :] if not isinstance(g, int) else X[:, GB * g:GB * g + GB, :]

        P0, P1, PB, G0, G1, UP, WB, DN = bank
        GP = [G0, G1]

        def has(g):
            return not isinstance(g, int) or 0 <= g < G

        def sweep(eng, step):
            for g in range(-3, 1):
                step(g)
            with eng.Fori(1, G - 3) as g:
                step(g)
            for g in range(G - 3, G):
                step(g)

        @block.sync
        def _(sp):
            sp.dma_start(wvh_raw[:], d["L0_xattn_Wv"]).then_inc(s["small_loaded"], 16)
            sp.dma_start(wth_raw[:], d["L0_xattn_Wt"]).then_inc(s["small_loaded"], 16)
            sp.dma_start(bv0[:], d["L0_xattn_bv"].rearrange("(h a) -> h a", a=1)).then_inc(s["small_loaded"], 16)
            sp.dma_start(bt0[:], d["L0_xattn_bt"].rearrange("(h a) -> h a", a=1)).then_inc(s["small_loaded"], 16)
            sp.dma_start(gw_raw[:], d["L0_ffn_gate_w"]).then_inc(s["gate_loaded"], 16)
            sp.dma_start(gbias[:], d["L0_ffn_gate_bias"].partition_broadcast(128)).then_inc(s["gate_loaded"], 16)
            def load(g):
                src_x = d["x"][GB * g:GB * g + GB] if isinstance(g, int) else d["x"][bass.ds(GB * g, GB)]
                src_c = d["ctx_768"][GB * g:GB * g + GB] if isinstance(g, int) else d["ctx_768"][bass.ds(GB * g, GB)]
                sp.dma_start(xg(g), src_x.rearrange("b s c -> s b c")).then_inc(s["x_loaded"], 16)
                if not isinstance(g, int) or g > 0:
                    wait_alone(sp, s["cT_psum"], g, s["carrier"])
                sp.dma_start(cload[:], src_c.rearrange("b s c -> s b c")).then_inc(s["c_loaded"], 16)
                sp.wait_ge(s["x_loaded"], 16 * (g + 1))
                wait_alone(sp, s["c_loaded"], 16 * (g + 1), s["carrier"])
            over_groups(sp, load, 0, G - 1)
            for tile, source in keep["moves"]:
                sp.dma_start(tile, source).then_inc(s["layer1_loaded"], 16)
            sp.wait_ge(s["layer1_loaded"], 16 * len(keep["moves"]))

        @block.gpsimd
        def _(pool):
            pool.memset(ident[:], 0.0)
            pool.memset(ones[:], 1.0)
            pool.memset(half[:], -0.5)
            pool.memset(before4[:], 1.0)
            pool.memset(before8[:], 1.0).then_inc(s["consts"], 1)
            pool.wait_ge(s["consts"], 1)
            pool.affine_select(out=ident[:], in_=ident[:], compare_op=ALU.not_equal, fill=1.0, base=0,
                               pattern=[[-1, 128]], channel_multiplier=1).then_inc(s["consts"], 1)
            pool.affine_select(out=before4[:], in_=before4[:], compare_op=ALU.is_gt, fill=0.0, base=0,
                               pattern=[[1, 4], [-1, 4]], channel_multiplier=0)
            pool.affine_select(out=before8[:], in_=before8[:], compare_op=ALU.is_gt, fill=0.0, base=0,
                               pattern=[[1, NE], [-1, NE]], channel_multiplier=0)
            pv = pick[:].rearrange("r b (e i) -> r b e i", e=2)
            pool.wait_ge(s["consts"], 2)
            pool.tensor_copy(ident16[:], ident[:]).then_inc(s["consts"], 1)
            pool.memset(pick[:], 0.0).then_inc(s["consts"], 1)
            for k in range(2):
                pool.wait_ge(s["consts"], 4 + k)
                pool.affine_select(out=pv, in_=pv, compare_op=ALU.not_equal, fill=1.0, base=-NE * k,
                                   pattern=[[-2, NBLK - 1], [-1, 2], [0, 64]],
                                   channel_multiplier=1).then_inc(s["consts"], 1)

            def root(k, g):
                wait_alone(pool, s["mv" + k], g + 1, s["carrier"])
                pool.tensor_scalar(rs[k][:, 0, :], mv[k][:, :, 1], 1.0, LN_EPS, ALU.mult, ALU.add
                                   ).then_inc(s["eps" + k], 1)
                pool.wait_ge(s["eps" + k], g + 1)
                pool.tensor_tensor(rs[k][:, 1, :], rs[k][:, 0, :], half[:, 0:GB], ALU.pow).then_inc(s["rs" + k], 1)

            def cosines(g, part):
                if part == 1:
                    pool.wait_ge(s["vt_sb"], 2 * (g + 1))
                    for i in range(2):
                        last = pool.tensor_tensor(sq[:, i, :], vt[i][:], vt[i][:], ALU.mult)
                    last.then_inc(s["sq_ready"], 1)
                elif part == 2:
                    pool.wait_ge(s["n2_ready"], g + 1)
                    pool.tensor_tensor(rn[:], n2[:], half[:], ALU.pow).then_inc(s["rn_ready"], 1)
                    wait_alone(pool, s["rn_ready"], g + 1, s["carrier"])
                    for i in range(GB):
                        last = pool.tensor_scalar(dg[:, i, :], ident[:], rn[:, GB + i:GB + i + 1], 0.0,
                                                  ALU.mult, ALU.add)
                    last.then_inc(s["dg_ready"], 1)
                elif part == 3:
                    wait_alone(pool, s["wm_ready"], g + 1, s["carrier"])
                    pool.tensor_tensor(xg(g), xg(g), wm[:], ALU.add).then_inc(s["x1_ready"], 1)

            def lo(g, p):
                pool.wait_ge(s["hi_ready"], NBLK * g + p + 1)
                pool.tensor_tensor(hp[1][:, p, :], hm[:, p % 2, :], hp[0][:, p, :], ALU.subtract
                                   ).then_inc(s["lo_ready"], 1)

            def step(g):
                for p in range(NBLK):
                    if has(g + 2):
                        cosines(g + 2, p)
                    if p == 3 and has(g + 3):
                        root("A", g + 3)
                    if p == 4 and has(g + 2):
                        root("B", g + 2)
                    if has(g):
                        lo(g, p)
            sweep(pool, step)

        @block.scalar
        def _(act):
            for k, (routed, shared) in enumerate((("w_gate", "sw_gate"), ("w_up", "sw_up"))):
                act.dma_start(w_raw[:, k, 0:NBLK - 1, :].rearrange("p b (e i) -> p (b e) i", e=2),
                             d["L0_ffn_" + routed].rearrange("e h i -> h e i")).then_inc(s["w_raw_loaded"], 16)
                act.dma_start(w_raw[:, k, NBLK - 1, :], d["L0_ffn_" + shared]).then_inc(s["w_raw_loaded"], 16)
            act.dma_start(w_raw[:, 2, 0:NBLK - 1, :],
                         d["L0_ffn_w_down"].rearrange("(b e) i h -> (e i) b h", e=2)).then_inc(s["w_raw_loaded"], 16)
            act.dma_start(w_raw[:, 2, NBLK - 1, :], d["L0_ffn_sw_down"]).then_inc(s["w_raw_loaded"], 16)
            act.wait_ge(s["wTr_ready"], 1)
            act.activation(wv0[0][:], P0[:, 0:DV], ACT.Copy)
            act.activation(wt0[0][:], P0[0:CT, DV:2 * DV], ACT.Copy).then_inc(s["w0t_split"], 1)
            act.wait_ge(s["w_raw_loaded"], 16 * 6)
            for k in range(3):
                last = act.activation(w0[0][:, k], w_raw[:, k], ACT.Copy)
            act.wait_ge(s["gate_loaded"], 32)
            act.activation(gw[0][:], gw_raw[:], ACT.Copy).then_inc(s["w0_split"], 1)
            act.wait_ge(s["small_loaded"], 64)

            def prep(g, part):
                if part == 0:
                    act.wait_ge(s["xnT_psum"], g + 1)
                    after(act, s["vt_psum"], g)
                    act.activation(xa[0][:], P0[:], ACT.Copy).then_inc(s["xA_hi"], 1)
                    act.wait_ge(s["cT_psum"], g + 1)
                    act.activation(tok(cT[0], g, rows=CT), P1[0:CT, :], ACT.Copy).then_inc(s["cT_hi"], 1)
                elif part == 1:
                    act.wait_ge(s["vt_psum"], g + 1)
                    after(act, s["dots_psum"], g)
                    act.activation(vt[0][:], P0[0:DV, :], ACT.Identity, bias=bv0[:]).then_inc(s["vt_sb"], 1)
                    act.activation(vt[1][:], P1[0:DV, :], ACT.Identity, bias=bt0[:]).then_inc(s["vt_sb"], 1)

            def route(g, part):
                if part == 0:
                    act.wait_ge(s["xBT_psum"], g + 1)
                    act.activation(tok(xT[0], g), PB[:], ACT.Copy).then_inc(s["xB_hi"], 1)
                elif part == 1:
                    act.wait_ge(s["logit_psum"], g + 1)
                    act.activation(th[:].rearrange("p b e -> p (b e)"), PB[:, 0:GB * NE], ACT.Tanh,
                                   scale=0.5).then_inc(s["th_ready"], 1)
                elif part == 4:
                    act.wait_ge(s["eT_psum"], g + 1)
                    act.activation(tok(eT, g), PB[0:2 * NE, 0:N // 2].bitcast(F16), ACT.Copy).then_inc(s["eT_ready"], 1)

            def step(g):
                for p in range(NBLK):
                    k = NBLK * g + p
                    if has(g):
                        act.wait_ge(s["gu_psum"], k + 1)
                        after(act, s["hm_ready"], before(k, p) + 1)
                        act.activation(sg[:, p % 2, :], GP[p % 2][:], ACT.Silu).then_inc(s["sg_ready"], 1)
                    if has(g + 2):
                        prep(g + 2, p)
                    if has(g + 1):
                        route(g + 1, p)
                    if has(g):
                        act.wait_ge(s["hm_ready"], k + 1)
                        after(act, s["down_psum"], k - NBLK + 1)
                        act.activation(hp[0][:, p, :], hm[:, p % 2, :], ACT.Copy).then_inc(s["hi_ready"], 1)
            sweep(act, step)

        @block.vector
        def _(dve):
            dve.memset(cT[0][CT:CT + 1, :], 1.0)
            dve.memset(ctx_sum[CT:CT + 1, :], float(S))
            dve.memset(cT[1][CT:CT + 1, :], 0.0)
            dve.wait_ge(s["w0t_split"], 1)
            dve.tensor_tensor(wv0[1][:], P0[:, 0:DV], wv0[0][:], ALU.subtract)
            dve.tensor_tensor(wt0[1][:], P0[0:CT, DV:2 * DV], wt0[0][:], ALU.subtract).then_inc(s["w0t_split"], 1)
            dve.wait_ge(s["w0_split"], 1)
            dve.tensor_tensor(w0[1][:], w_raw[:], w0[0][:], ALU.subtract)
            dve.tensor_tensor(gw[1][:], gw_raw[:], gw[0][:], ALU.subtract).then_inc(s["w0_split"], 1)

            dve.wait_ge(s["consts"], 6)

            def stats(k, g):
                for i in range(GB):
                    last = dve.bn_stats(st[k][:, i, :], xg(g)[:, i, :])
                last.then_inc(s["st" + k], 1)
                wait_alone(dve, s["st" + k], g + 1, s["carrier"])
                for i in range(GB):
                    last = dve.bn_aggr(mv[k][:, i, :], st[k][:, i, :])
                last.then_inc(s["mv" + k], 1)

            def normalise(k, g):
                wait_alone(dve, s["rs" + k], g + 1, s["carrier"])
                for i in range(GB):
                    last = dve.tensor_scalar(xn[k][:, i, :], xg(g)[:, i, :], mv[k][:, i, 0:1], rs[k][:, 1, i:i + 1],
                                             ALU.subtract, ALU.mult)
                last.then_inc(s["xn" + k], 1)

            steps = 0

            def gate(g, part):
                nonlocal steps
                steps = 0 if part == 0 else steps

                def link(ins):
                    nonlocal steps
                    steps += 1
                    ins.then_inc(s["gate_step"], 1)
                    dve.wait_ge(s["gate_step"], GATE_STEPS * g + steps)

                def rank(values, n, room, mask):
                    shape = [128, GB, n, n]
                    other = values.unsqueeze(2).broadcast_to(shape)
                    own = values.unsqueeze(3).broadcast_to(shape)
                    tie = mask.unsqueeze(1).broadcast_to(shape)
                    dve.tensor_tensor(room[:, 0], other, own, ALU.is_gt)
                    link(dve.tensor_tensor(room[:, 1], other, own, ALU.is_equal))
                    link(dve.tensor_tensor(room[:, 2], room[:, 1], tie, ALU.mult))
                    link(dve.tensor_tensor(room[:, 1], room[:, 0], room[:, 2], ALU.add))

                if part == 0:
                    dve.wait_ge(s["th_ready"], g + 1)
                    link(dve.tensor_scalar(th[:], th[:], 0.5, 0.5, ALU.mult, ALU.add))
                    link(dve.tensor_tensor(sfc[:], th[:], gbias[:].unsqueeze(1).broadcast_to([128, GB, NE]), ALU.add))
                    pairs = sfc[:].rearrange("p b (q e) -> p b q e", e=2)
                    link(dve.tensor_tensor(gs[:], pairs[:, :, :, 0], pairs[:, :, :, 1], ALU.add))
                    rank(gs[:], 4, c4, before4[:])
                    link(dve.tensor_reduce(cnt4[:, 0], c4[:, 1], AX.X, ALU.add))
                    link(dve.tensor_scalar(cnt4[:, 1], cnt4[:, 0], 2.0, None, ALU.is_lt))
                    link(dve.tensor_tensor(tmp8[:].rearrange("p b (q e) -> p b q e", e=2), pairs,
                                           cnt4[:, 1].unsqueeze(3).broadcast_to([128, GB, 4, 2]), ALU.mult))
                else:
                    rank(tmp8[:], NE, c8, before8[:])
                    link(dve.tensor_reduce(cnt8[:], c8[:, 1], AX.X, ALU.add))
                    link(dve.tensor_scalar(sel[:], cnt8[:], 2.0, None, ALU.is_lt))
                    link(dve.tensor_tensor(sel[:], sel[:], sfc[:], ALU.mult))
                    link(dve.tensor_reduce(den0[:, 0], sel[:], AX.X, ALU.add))
                    link(dve.tensor_scalar(den0[:, 0], den0[:, 0], 1e-20, None, ALU.add))
                    link(dve.reciprocal(den0[:, 1], den0[:, 0]))
                    link(dve.scalar_tensor_tensor(wgt[:], sel[:], ROUTED_SCALE,
                                                  den0[:, 1].unsqueeze(2).broadcast_to([128, GB, NE]),
                                                  ALU.mult, ALU.mult))
                    link(dve.tensor_copy(wst[:, :, 0:NE], wgt[:]))
                    dve.tensor_tensor(wst[:, :, NE:], wgt[:], wst[:, :, 0:NE], ALU.subtract).then_inc(s["wst_ready"], 1)
                    assert steps == GATE_STEPS

            def prep(g, part):
                if part == 0:
                    dve.wait_ge(s["xA_hi"], g + 1)
                    dve.tensor_tensor(xa[1][:], P0[:], xa[0][:], ALU.subtract).then_inc(s["xA_lo"], 1)
                    dve.wait_ge(s["cT_hi"], g + 1)
                    sums = ctx_sum[0:CT, GB * g:GB * g + GB] if isinstance(g, int) else \
                        ctx_sum[0:CT, bass.ds(GB * g, GB)]
                    dve.tensor_reduce(sums, P1[0:CT, :].rearrange("c (b k) -> c b k", k=S), AX.X, ALU.add)
                    dve.tensor_tensor(tok(cT[1], g, rows=CT), P1[0:CT, :], tok(cT[0], g, rows=CT),
                                      ALU.subtract).then_inc(s["cT_lo"], 1)
                elif part == 2:
                    dve.wait_ge(s["dots_psum"], g + 1)
                    dve.tensor_scalar(n2[:], P1[:, 0:2 * GB], 1e-37, None, ALU.max).then_inc(s["n2_ready"], 1)
                elif part == 3:
                    dve.wait_ge(s["rb_psum"], g + 1)
                    after(dve, s["x1_ready"], g)
                    for i in range(GB):
                        last = dve.tensor_scalar(wm[:, i, :], P1[:, 128 * i:128 * i + 128], rn[:, i:i + 1],
                                                 1.0 / COS_EPS, ALU.mult, ALU.min)
                    last.then_inc(s["wm_min"], 1)
                    dve.wait_ge(s["wm_min"], g + 1)
                    wf = wm[:].rearrange("p b c -> p (b c)")
                    dve.tensor_tensor(wf, P0[:], wf, ALU.mult).then_inc(s["wm_ready"], 1)

            def route(g, part):
                if part == 0:
                    dve.wait_ge(s["xB_hi"], g + 1)
                    dve.tensor_tensor(tok(xT[1], g), PB[:], tok(xT[0], g), ALU.subtract).then_inc(s["xB_lo"], 1)
                elif part in (1, 2):
                    gate(g, part - 1)

            def step(g):
                for p in range(NBLK):
                    k = NBLK * g + p
                    if has(g) and p == 2:
                        add(g - 1)
                    if has(g):
                        i = p % 2
                        dve.wait_ge(s["sg_ready"], k + 1)
                        after(dve, s["lo_ready"], before(k, p) + 1)
                        if p < NBLK - 1:
                            dve.tensor_tensor(su[:, i, :], sg[:, i, :], UP[:], ALU.mult).then_inc(s["su_ready"], 1)
                            dve.wait_ge(s["su_ready"], (NBLK - 1) * g + p + 1)
                            dve.tensor_tensor(hm[:, i, :], su[:, i, :], WB[:], ALU.mult).then_inc(s["hm_ready"], 1)
                        else:
                            dve.tensor_tensor(hm[:, i, :], sg[:, i, :], UP[:], ALU.mult).then_inc(s["hm_ready"], 1)
                    if has(g + 2):
                        prep(g + 2, p)
                    if p == 3 and has(g + 3):
                        wait_alone(dve, s["x_loaded"], 16 * (g + 4), s["carrier"])
                        stats("A", g + 3)
                    if p == 4:
                        if has(g + 2):
                            wait_alone(dve, s["x1_ready"], g + 3, s["carrier"])
                            stats("B", g + 2)
                        if has(g + 3):
                            normalise("A", g + 3)
                        if has(g + 2):
                            normalise("B", g + 2)
                    if has(g + 1):
                        route(g + 1, p)

            def add(g):
                if isinstance(g, int) and g < 0:
                    return
                dve.wait_ge(s["down_psum"], NBLK * (g + 1))
                xf = xg(g).rearrange("p b c -> p (b c)")
                dve.tensor_tensor(xf, DN[:], xf, ALU.add).then_inc(s["x2_ready"], 1)
            sweep(dve, step)
            add(G - 1)

        @block.tensor
        def _(pe):
            pe.wait_ge(s["consts"], 3)
            pe.wait_ge(s["small_loaded"], 64)
            pe.transpose(P0[:, 0:DV], wvh_raw[:], ident[0:DV, 0:DV])
            pe.transpose(P0[0:CT, DV:2 * DV], wth_raw[:], ident[0:DV, 0:DV]).then_inc(s["wTr_ready"], 1)
            pe.wait_ge(s["w0t_split"], 2)

            def prep(g, part):
                if part == 0:
                    pe.wait_ge(s["xnA"], g + 1)
                    after(pe, s["wm_ready"], g)
                    for i in range(GB):
                        last = pe.transpose(P0[:, 128 * i:128 * i + 128], xn["A"][:, i, :], ident[:])
                    last.then_inc(s["xnT_psum"], 1)
                    pe.wait_ge(s["c_loaded"], 16 * (g + 1))
                    for i in range(GB):
                        last = pe.transpose(P1[0:CT, 128 * i:128 * i + 128], cload[:, i, :], ident[:])
                    last.then_inc(s["cT_psum"], 1)
                elif part == 1:
                    pe.wait_ge(s["xA_lo"], g + 1)
                    split_product(pe, P0[0:DV, :], [w[:] for w in wv0], [x[:] for x in xa])
                    pe.wait_ge(s["cT_lo"], g + 1)
                    split_product(pe, P1[0:DV, :], [w[:] for w in wt0],
                                  [tok(x, g, rows=CT) for x in cT]).then_inc(s["vt_psum"], 1)
                elif part == 2:
                    pe.wait_ge(s["vt_sb"], 2 * (g + 1))
                    for i in range(GB):
                        pe.matmul(P0[:, 128 * i:128 * i + 128], vt[0][:, 128 * i:128 * i + 128],
                                  vt[1][:, 128 * i:128 * i + 128], start=True, stop=True)
                    pe.wait_ge(s["sq_ready"], g + 1)
                    for j in range(2):
                        for i in range(GB):
                            last = pe.matmul(P1[:, GB * j + i:GB * j + i + 1], sq[:, j, 128 * i:128 * i + 128],
                                             ones[0:DV, 0:1], start=True, stop=True)
                    last.then_inc(s["dots_psum"], 1)
                elif part == 3:
                    pe.wait_ge(s["dg_ready"], g + 1)
                    pe.matmul(P1[:], ones[:], dg[:].rearrange("p b c -> p (b c)"), start=True, stop=True
                              ).then_inc(s["rb_psum"], 1)

            def route(g, part):
                if part == 0:
                    pe.wait_ge(s["xnB"], g + 1)
                    after(pe, s["eT_ready"], g)
                    for i in range(GB):
                        last = pe.transpose(PB[:, 128 * i:128 * i + 128], xn["B"][:, i, :], ident[:])
                    last.then_inc(s["xBT_psum"], 1)
                elif part == 1:
                    pe.wait_ge(s["xB_lo"], g + 1)
                    for i in range(GB):
                        last = split_product(pe, PB[:, NE * i:NE * i + NE], [tok(x, g, 128 * i, 128) for x in xT],
                                             [w[:] for w in gw])
                    last.then_inc(s["logit_psum"], 1)
                elif part == 4:
                    pe.wait_ge(s["wst_ready"], g + 1)
                    for i in range(GB):
                        last = pe.transpose(PB[0:2 * NE, 64 * i:64 * i + 64].bitcast(F16), wst[:, i, :], ident16[:])
                    last.then_inc(s["eT_psum"], 1)

            def up(g, p):
                k = NBLK * g + p
                i = p % 2
                if p == 0:
                    pe.wait_ge(s["eT_ready"], g + 1)
                x = [tok(t, g) for t in xT]
                after(pe, s["sg_ready"], before(k, p) + 1)
                split_product(pe, GP[i][:], [w[:, 0, p, :] for w in w0], x)
                after_alone(pe, s["hm_ready"], k, s["carrier"])
                last = split_product(pe, UP[:], [w[:, 1, p, :] for w in w0], x)
                if p < NBLK - 1:
                    last = pe.matmul(WB[:], pick[:, p, :], tok(eT, g), start=True, stop=True)
                last.then_inc(s["gu_psum"], 1)

            def down(g, p):
                if isinstance(g, int) and g < 0:
                    return
                pe.wait_ge(s["lo_ready"], NBLK * g + p + 1)
                if p == 0:
                    after(pe, s["x2_ready"], g)
                for i in range(GB):
                    cols = slice(128 * i, 128 * i + 128)
                    last = split_product(pe, DN[:, cols], [h[:, p, cols] for h in hp], [w[:, 2, p, :] for w in w0],
                                         start=(p == 0 and i == 0), stop=(p == NBLK - 1), skip_group_check=True)
                last.then_inc(s["down_psum"], 1)


            def step(g):
                if isinstance(g, int) and g == -1:
                    pe.wait_ge(s["w0_split"], 2)
                    pe.wait_ge(s["consts"], 6)
                for p in range(NBLK):
                    if has(g):
                        up(g, p)
                    if has(g + 2):
                        prep(g + 2, p)
                    if has(g + 1):
                        route(g + 1, p)
                    if has(g):
                        down(g if p >= 2 else g - 1, (p - 2) % NBLK)
            sweep(pe, step)
            down(G - 1, NBLK - 2)
            down(G - 1, NBLK - 1)
    return room


def attention1(nc, d, bank, keep, X3):
    X, ident, ident16, ones, cT = keep["X"], keep["ident"], keep["ident16"], keep["ones"], keep["cT"]
    SCALE = HD ** -0.5
    CLIP = 10000.0 / SCALE
    RING = 4
    U = NH // 4
    with ExitStack() as ctx:
        room = Room(nc, ctx, "cross")
        sb = room.sb
        w1 = keep["w"]
        wq_raw, wk_raw, wv_raw, wo, bo, bq_raw = (w1[n] for n in ("wq", "wk", "wv", "wo", "bo", "bq"))
        wq_c = [sb(f"wq_c{i}", [C, C], F16) for i in range(2)]
        wk_c = [sb(f"wk_c{i}", [CT + 1, C], F16) for i in range(2)]
        wv_c = [sb(f"wv_c{i}", [CT + 1, C], F16) for i in range(2)]
        bq_c = [sb(f"bq_c{i}", [2, C], F16) for i in range(3)]
        wq = [sb(f"wq{i}", [C, NH, 4, HD], F16) for i in range(2)]
        wk = [sb(f"wk{i}", [CT + 1, NH, 4, HD], F16) for i in range(2)]
        bq = sb("bq", [2, NH, 4, HD], F16)
        ones16 = sb("ones16", [2, 128], F16)
        low_rows = sb("low_rows", [128, 2])
        negsel = sb("negsel", [128, NH, 128], F16)
        st = sb("st1", [128, B, 6])
        mv = sb("mv1", [128, B, 2])
        rs = sb("rs1", [128, 2, B])
        half = sb("half1", [128, B])
        xn = sb("xn1", [S, C])
        xh = [sb(f"xh{i}", [C, S], F16) for i in range(2)]
        qhi = sb("qhi", [128, U * S], F16)
        khi = sb("khi", [128, U * S], F16)
        Qc = sb("Qc", [128, U * S], F16)
        Q = [[sb(f"Q{i}_{j}", [128, U * S], F16) for j in range(U)] for i in range(RING)]
        K = [sb(f"K{i}", [128, U * S], F16) for i in range(RING)]
        V = [sb(f"V{i}", [S, NH, 32]) for i in range(RING)]
        mx = sb("mx", [S, NH])
        m16 = sb("m16", [S, 128], F16)
        mT = sb("mT", [128, S], F16)
        P = [sb(f"P{i}", [S, 4 * S]) for i in range(RING)]
        OE = sb("OE", [128, U * S])
        dn = sb("dn", [S, NH])
        On = sb("On", [S, C])
        OT = sb("OT", [C, S])
        inv_sum = sb("inv_sum", [S, NH])
        ctx_mean = sb("ctx_mean", [CT + 1, B])
        mean_v = sb("mean_v", [C, B])
        bad = sb("bad", [128, 2])
        flat = [sb(f"flat{i}", [S, N]) for i in range(2)]
        s = room.sems("""small_const w_hi w_lo w_rep stats_a stats_b stats_c stats_d carrier1 xn_ready xT_psum
            xT_hi xT_lo k_psum k_hi k_ready q_psum q_hi q_stack q_act q_dve v_psum v_ready s_psum s_max m_ready mT_psum mT_ready
            t_psum t_clip t_neg p_ready o_psum oT_sb f_psum dn_ready o_norm a_psum a_sb y_psum x3_ready""")
        g_ = room.sems("inv_summed mean_psum mean_sb bad_psum bad_sum bad_ready flat_psum flat_ready flat_taken ctx_step")
        block = ctx.enter_context(nc.Block())
        S0, S1, T0, T1, QK, M, O, F = bank
        SB, TB = [S0, S1], [T0, T1]

        def has(b):
            return not isinstance(b, int) or 0 <= b < B

        def sweep(eng, step):
            for b in range(-3, RING):
                step(b, b % RING)
            with eng.Fori(1, B // RING - 1) as q:
                for i in range(RING):
                    step(q * RING + i, i)
            for b in range(B - RING, B + 2):
                step(b, b % RING)

        def batch(t, b):
            return t[:, b, :] if isinstance(b, int) else t[:, bass.ds(b, 1), :].rearrange("p a c -> p (a c)")

        def btok(t, b):
            return t[:, b * S:b * S + S] if isinstance(b, int) else t[:, bass.ds(b * S, S)]

        def head(t, h):
            return t[:, 128 * h:128 * h + 128]

        def place(op, i, j):
            rows = slice(32 * j, 32 * j + 32)
            return op(Q[i][j][rows, :], Qc[rows, :])

        @block.gpsimd
        def _(pool):
            pool.memset(half[:], -0.5)
            pool.memset(ones16[:], 1.0)
            for t in (wq[0], wq[1], wk[0], wk[1], bq):
                last = pool.memset(t[:], 0.0)
            last.then_inc(s["small_const"], 1)
            for t in Q:
                for j in range(U):
                    pool.memset(t[j][:], 0.0)
            for t in V:
                pool.memset(t[:, :, 0:HD], 0.0)
                pool.memset(t[:, :, HD:HD + 1], 1.0)
                last = pool.memset(t[:, :, HD + 1:], 0.0)
            last.then_inc(s["small_const"], 1)
            pool.wait_ge(s["stats_b"], 1)
            pool.tensor_scalar(rs[:, 0, :], mv[:, :, 1], 1.0, LN_EPS, ALU.mult, ALU.add).then_inc(s["stats_c"], 1)
            pool.wait_ge(s["stats_c"], 1)
            pool.tensor_tensor(rs[:, 1, :], rs[:, 0, :], half[:], ALU.pow).then_inc(s["stats_d"], 1)
            pool.memset(inv_sum[:], 0.0).then_inc(g_["inv_summed"], 1)

            def step(b, i):
                if has(b - 1):
                    wait_alone(pool, s["dn_ready"], b, s["carrier1"])
                    wait_alone(pool, g_["inv_summed"], b, s["carrier1"])
                    pool.tensor_tensor(inv_sum[:], inv_sum[:], dn[:], ALU.add).then_inc(g_["inv_summed"], 1)
            sweep(pool, step)

        @block.scalar
        def _(act):
            for raw, c in ((wq_raw, wq_c), (wk_raw, wk_c), (wv_raw, wv_c), (bq_raw, bq_c)):
                last = act.activation(c[0][:], raw[:], ACT.Copy)
            last.then_inc(s["w_hi"], 1)
            act.wait_ge(s["w_lo"], 3)
            act.wait_ge(s["small_const"], 1)
            for w, c in ((wq, wq_c), (wk, wk_c)):
                rows = c[0].shape[0]
                for i in range(2):
                    last = act.activation(w[i][:, :, 0:3, :], c[i][:].rearrange("p (h d) -> p h d", d=HD).unsqueeze(2)
                                          .broadcast_to([rows, NH, 3, HD]), ACT.Copy)
            last = act.activation(bq[:, :, 0:3, :], bq_c[2][:].rearrange("p (h d) -> p h d", d=HD).unsqueeze(2)
                                  .broadcast_to([2, NH, 3, HD]), ACT.Copy)
            last.then_inc(s["w_rep"], 1)

            def exp(b, j, i):
                u = U * b + j
                act.wait_ge(s["t_neg"], u + 1)
                after(act, s["o_psum"], u - 3)
                act.activation(P[j][:], TB[j % 2][:], ACT.Exp, scale=SCALE).then_inc(s["p_ready"], 1)

            def step(b, i):
                i2 = (i + 2) % RING
                if has(b - 1):
                    exp(b - 1, U - 1, (i - 1) % RING)
                if has(b):
                    act.wait_ge(s["mT_psum"], b + 1)
                    after(act, s["t_neg"], U * b)
                    act.activation(mT[:], M[:, 256:256 + S // 2].bitcast(F16), ACT.Copy).then_inc(s["mT_ready"], 1)
                if has(b + 2):
                    act.wait_ge(s["xT_psum"], b + 3)
                    after(act, s["q_psum"], b + 2)
                    act.activation(xh[0][:], M[:, 0:S], ACT.Copy).then_inc(s["xT_hi"], 1)
                if has(b + 2):
                    act.wait_ge(s["k_psum"], b + 3)
                    after(act, s["k_ready"], b + 2)
                    act.activation(khi[:], QK[:], ACT.Copy, scale=low_rows[:, 1:2]).then_inc(s["k_hi"], 1)
                if has(b):
                    exp(b, 0, i)
                if has(b - 2):
                    act.wait_ge(s["a_psum"], b - 1)
                    after(act, s["y_psum"], b - 2)
                    act.activation(OT[:], F[:, 0:S], ACT.Copy).then_inc(s["a_sb"], 1)
                if has(b + 2):
                    act.wait_ge(s["v_psum"], b + 3)
                    after(act, s["o_psum"], U * (b - 1))
                    act.activation(V[i2][:, :, 0:HD], M[:, S:2 * S].rearrange("p (h d) -> p h d", d=HD), ACT.Copy
                                   ).then_inc(s["v_ready"], 1)
                if has(b - 1):
                    act.wait_ge(s["o_psum"], U * b)
                    after(act, s["f_psum"], b - 1)
                    act.activation(OE[:], O[:], ACT.Copy).then_inc(s["oT_sb"], 1)
                if has(b):
                    exp(b, 1, i)
                if has(b + 2):
                    act.wait_ge(s["q_psum"], b + 3)
                    after(act, s["q_stack"], b + 2)
                    act.activation(qhi[:], QK[:], ACT.Copy, scale=low_rows[:, 0:1]).then_inc(s["q_hi"], 1)
                if has(b):
                    exp(b, 2, i)
                if has(b + 2):
                    act.wait_ge(s["q_stack"], b + 3)
                    for j in range(2):
                        last = place(lambda o, x: act.activation(o, x, ACT.Copy), i2, j)
                    last.then_inc(s["q_act"], 1)
            act.wait_ge(s["small_const"], 2)
            sweep(act, step)
            act.wait_ge(g_["mean_psum"], 1)
            act.activation(mean_v[:], T1[:, 0:B], ACT.Copy).then_inc(g_["mean_sb"], 1)

        @block.vector
        def _(dve):
            dve.tensor_scalar(ctx_mean[:], keep["ctx_sum"][:], 1.0 / S, None, ALU.mult).then_inc(g_["ctx_step"], 1)
            dve.wait_ge(s["w_hi"], 1)
            for raw, c in ((wq_raw, wq_c), (wk_raw, wk_c), (wv_raw, wv_c), (bq_raw, bq_c)):
                last = dve.tensor_tensor(c[1][:], raw[:], c[0][:], ALU.subtract)
            last.then_inc(s["w_lo"], 1)
            dve.wait_ge(s["w_lo"], 1)
            dve.tensor_scalar(bq_c[2][:], bq_c[1][:], ident[0:2, 1:2], None, ALU.mult).then_inc(s["w_lo"], 1)
            dve.wait_ge(s["w_lo"], 2)
            dve.scalar_tensor_tensor(bq_c[2][:], bq_c[0][:], ident[0:2, 0:1], bq_c[2][:], ALU.mult, ALU.add
                                     ).then_inc(s["w_lo"], 1)
            dve.memset(m16[:], 0.0)
            for b in range(B):
                last = dve.bn_stats(st[:, b, :], X[:, b, :])
            last.then_inc(s["stats_a"], 1)
            idv = ident[:].rearrange("p (j r d) -> p j r d", r=4, d=HD)
            dve.tensor_reduce(low_rows[:, 0:1], idv[:, :, 2, :], AX.XY, ALU.add)
            dve.tensor_reduce(low_rows[:, 1:2], idv[:, :, 1, :], AX.XY, ALU.add)
            dve.tensor_scalar(negsel[:], ident[:, 0:NH].unsqueeze(2).broadcast_to([128, NH, 128]), -1.0, None, ALU.mult)
            dve.wait_ge(s["stats_a"], 1)
            for b in range(B):
                last = dve.bn_aggr(mv[:, b, :], st[:, b, :])
            last.then_inc(s["stats_b"], 1)
            dve.wait_ge(s["stats_d"], 1)

            def normalise(b):
                if has(b):
                    after_alone(dve, s["xT_psum"], b, s["carrier1"])
                    m, r = ((mv[:, b, 0:1], rs[:, 1, b:b + 1]) if isinstance(b, int) else
                            (mv[:, bass.ds(b, 1), 0:1].rearrange("p a c -> p (a c)"), rs[:, 1, bass.ds(b, 1)]))
                    dve.tensor_scalar(xn[:], batch(X, b), m, r, ALU.subtract, ALU.mult).then_inc(s["xn_ready"], 1)

            def clip(b, j):
                if has(b):
                    dve.wait_ge(s["t_psum"], U * b + j + 1)
                    dve.tensor_scalar(TB[j % 2][:], TB[j % 2][:], -CLIP, CLIP, ALU.max, ALU.min
                                      ).then_inc(s["t_clip"], 1)

            def maxima(b, j):
                if has(b):
                    dve.wait_ge(s["s_psum"], U * b + j + 1)
                    if j == 0:
                        after(dve, s["m_ready"], b)
                    dve.tensor_reduce(mx[:, 4 * j:4 * j + 4], SB[j % 2][:].rearrange("p (h k) -> p h k", h=4), AX.X,
                                      ALU.max).then_inc(s["s_max"], 1)

            def step(b, i):
                i2 = (i + 2) % RING
                clip(b, 0)
                maxima(b + 1, 0)
                if has(b + 2):
                    dve.wait_ge(s["xT_hi"], b + 3)
                    dve.tensor_tensor(xh[1][:], M[:, 0:S], xh[0][:], ALU.subtract).then_inc(s["xT_lo"], 1)
                if has(b + 2):
                    dve.wait_ge(s["k_hi"], b + 3)
                    dve.tensor_tensor(K[i2][:], QK[:], khi[:], ALU.subtract).then_inc(s["k_ready"], 1)
                clip(b, 1)
                maxima(b + 1, 1)
                clip(b, 2)
                maxima(b + 1, 2)
                if has(b + 2):
                    dve.wait_ge(s["q_hi"], b + 3)
                    after(dve, s["q_act"], b + 2)
                    dve.tensor_tensor(Qc[:], QK[:], qhi[:], ALU.subtract).then_inc(s["q_stack"], 1)
                    dve.wait_ge(s["q_stack"], b + 3)
                    for j in range(2, U):
                        last = place(dve.tensor_copy, i2, j)
                    last.then_inc(s["q_dve"], 1)
                if has(b - 2):
                    wait_alone(dve, s["y_psum"], b - 1, s["carrier1"])
                    dve.tensor_tensor(batch(X3, b - 2), F[:, S:2 * S], batch(X, b - 2), ALU.add
                                      ).then_inc(s["x3_ready"], 1)
                clip(b, 3)
                normalise(b + 3)
                maxima(b + 1, 3)
                if has(b + 1):
                    dve.wait_ge(s["s_max"], U * (b + 2))
                    after(dve, s["mT_psum"], b + 1)
                    dve.tensor_scalar(m16[:, 0:NH], mx[:], -CLIP, CLIP, ALU.max, ALU.min).then_inc(s["m_ready"], 1)
                if has(b - 1):
                    fv = F[:].rearrange("p (j h w) -> p j h w", h=4, w=32)
                    dve.wait_ge(s["f_psum"], b)
                    after(dve, g_["inv_summed"], b)
                    dve.reciprocal(dn[:].rearrange("p (j h) -> p j h", h=4), fv[:, :, :, HD]).then_inc(s["dn_ready"], 1)
                    dve.wait_ge(s["dn_ready"], b)
                    after(dve, s["a_psum"], b - 1)
                    dve.tensor_tensor(On[:].rearrange("p (h j d) -> p j h d", h=4, d=HD), fv[:, :, :, 0:HD],
                                      dn[:].rearrange("p (j h) -> p j h", h=4).unsqueeze(3)
                                      .broadcast_to([S, U, 4, HD]), ALU.mult).then_inc(s["o_norm"], 1)
            dve.wait_ge(s["small_const"], 2)
            sweep(dve, step)
            dve.wait_ge(g_["bad_psum"], 1)
            dve.tensor_reduce(bad[:, 0:1], T0[:, 0:NH], AX.X, ALU.add).then_inc(g_["bad_sum"], 1)
            dve.wait_ge(g_["bad_sum"], 1)
            dve.tensor_tensor(bad[:, 1:2], bad[:, 0:1], bad[:, 0:1], ALU.not_equal).then_inc(g_["bad_ready"], 1)
            dve.wait_ge(g_["bad_ready"], 1)
            dve.wait_ge(s["x3_ready"], B)
            for g in range(G):
                at = slice(GB * g, GB * g + GB)
                x3 = X3[:, at, :].rearrange("p b c -> p (b c)")
                dve.wait_ge(g_["flat_psum"], g + 1)
                after(dve, g_["flat_taken"], g - 1)
                dve.tensor_tensor(flat[g % 2][:], SB[g % 2][:], X[:, at, :].rearrange("p b c -> p (b c)"), ALU.add
                                  ).then_inc(g_["flat_ready"], 1)
                dve.wait_ge(g_["flat_ready"], g + 1)
                dve.copy_predicated(x3, bad[:, 1:2].bitcast(mybir.dt.uint32).broadcast_to([S, N]), flat[g % 2][:]
                                    ).then_inc(g_["flat_taken"], 1)

        @block.tensor
        def _(pe):
            pe.wait_ge(s["w_rep"], 1)

            def score(b, j, i):
                after(pe, s["s_max"], U * b + j - 1)
                for h in range(4):
                    last = pe.matmul(SB[j % 2][:, 128 * h:128 * h + 128], head(Q[i][j], h), head(K[i], h),
                                     start=True, stop=True)
                last.then_inc(s["s_psum"], 1)

            def score_t(b, j, i):
                after(pe, s["p_ready"], U * b + j - 1)
                for h in range(4):
                    last = pe.matmul(TB[j % 2][:, 128 * h:128 * h + 128], head(K[i], h), head(Q[i][j], h),
                                     start=(h == 0), stop=False, skip_group_check=True)
                last.then_inc(s["t_psum"], 1)

            def less_max(b, j):
                pe.wait_ge(s["mT_ready"], b + 1)
                pe.wait_ge(s["t_clip"], U * b + j + 1)
                for h in range(4):
                    last = pe.matmul(TB[j % 2][:, 128 * h:128 * h + 128], negsel[:, 4 * j + h, :], mT[:],
                                     start=False, stop=True, skip_group_check=True)
                last.then_inc(s["t_neg"], 1)

            def values(b, j, i):
                pe.wait_ge(s["p_ready"], U * b + j + 1)
                if j == 0:
                    pe.wait_ge(s["v_ready"], b + 1)
                    after(pe, s["oT_sb"], b)
                for h in range(4):
                    last = pe.matmul(O[32 * h:32 * h + 32, 128 * j:128 * j + 128], V[i][:, 4 * h + j, :],
                                     P[j][:, 128 * h:128 * h + 128], start=True, stop=True, tile_position=(0, 32 * h))
                last.then_inc(s["o_psum"], 1)

            def project(b, i, w, x, done, bias=False):
                for j in range(U):
                    cols = QK[:, 128 * j:128 * j + 128]
                    if bias:
                        pe.matmul(cols, bq[:, 4 * j:4 * j + 4].rearrange("p h r d -> p (h r d)"), ones16[:],
                                  start=True, stop=False)
                    last = split_product(pe, cols, [a[:, 4 * j:4 * j + 4].rearrange("p h r d -> p (h r d)") for a in w],
                                         x, start=not bias)
                last.then_inc(done, 1)

            def step(b, i):
                i1, b1 = (i + 1) % RING, b + 1
                ip = (i - 1) % RING
                if has(b1):
                    pe.wait_ge(s["k_ready"], b + 2)
                    pe.wait_ge(s["q_act"], b + 2)
                    pe.wait_ge(s["q_dve"], b + 2)
                    score(b1, 0, i1)
                if has(b - 1):
                    less_max(b - 1, 3)
                if has(b):
                    score_t(b, 0, i)
                if has(b + 2):
                    after(pe, s["q_stack"], b + 2)
                    project(b + 2, i, wk, [btok(c, b + 2) for c in cT], s["k_psum"])
                if has(b + 2):
                    pe.wait_ge(s["xn_ready"], b + 3)
                    after(pe, s["v_ready"], b + 2)
                    pe.transpose(M[:, 0:S], xn[:], ident[:]).then_inc(s["xT_psum"], 1)
                if has(b):
                    pe.wait_ge(s["m_ready"], b + 1)
                    pe.transpose(M[:, 256:256 + S // 2].bitcast(F16), m16[:], ident16[:]).then_inc(s["mT_psum"], 1)
                if has(b - 1):
                    values(b - 1, 2, ip)
                if has(b - 2):
                    pe.wait_ge(s["o_norm"], b - 1)
                    pe.transpose(F[:, 0:S], On[:], ident[:]).then_inc(s["a_psum"], 1)
                if has(b1):
                    score(b1, 1, i1)
                if has(b):
                    less_max(b, 0)
                    score_t(b, 1, i)
                if has(b - 1):
                    values(b - 1, 3, ip)
                if has(b + 2):
                    pe.wait_ge(s["xT_lo"], b + 3)
                    split_product(pe, M[:, S:2 * S], [btok(c, b + 2) for c in cT], [w[:] for w in wv_c]
                                  ).then_inc(s["v_psum"], 1)
                if has(b1):
                    score(b1, 2, i1)
                if has(b):
                    less_max(b, 1)
                    score_t(b, 2, i)
                    values(b, 0, i)
                if has(b + 2):
                    pe.wait_ge(s["xT_lo"], b + 3)
                    pe.wait_ge(s["k_ready"], b + 3)
                    project(b + 2, i, wq, [x[:] for x in xh], s["q_psum"], bias=True)
                if has(b - 2):
                    pe.wait_ge(s["a_sb"], b - 1)
                    pe.matmul(F[:, S:2 * S], OT[:], wo[:], start=True, stop=False)
                    pe.matmul(F[:, S:2 * S], ones[0:1, :], bo[:], start=False, stop=True).then_inc(s["y_psum"], 1)
                if has(b1):
                    score(b1, 3, i1)
                if has(b):
                    less_max(b, 2)
                    score_t(b, 3, i)
                if has(b - 1):
                    pe.wait_ge(s["oT_sb"], b)
                    after(pe, s["x3_ready"], b - 1)
                    for j in range(U):
                        last = pe.transpose(F[:, 128 * j:128 * j + 128], OE[:, 128 * j:128 * j + 128], ident[:])
                    last.then_inc(s["f_psum"], 1)
                if has(b):
                    values(b, 1, i)
            sweep(pe, step)

            pe.wait_ge(g_["inv_summed"], B + 1)
            pe.wait_ge(g_["ctx_step"], 1)
            pe.wait_ge(s["t_neg"], U * B)
            pe.wait_ge(s["p_ready"], U * B)
            pe.wait_ge(s["s_max"], U * B)
            pe.matmul(T0[:, 0:NH], ones[:], inv_sum[:], start=True, stop=True).then_inc(g_["bad_psum"], 1)
            pe.matmul(T1[:, 0:B], wv_raw[:], ctx_mean[:], start=True, stop=True).then_inc(g_["mean_psum"], 1)
            pe.wait_ge(g_["mean_sb"], 1)
            for g in range(G):
                after(pe, g_["flat_ready"], g - 1)
                for i in range(GB):
                    cols = SB[g % 2][:, 128 * i:128 * i + 128]
                    b = GB * g + i
                    pe.matmul(cols, mean_v[:, b:b + 1].broadcast_to([C, S]), wo[:], start=True, stop=False)
                    last = pe.matmul(cols, ones[0:1, :], bo[:], start=False, stop=True)
                last.then_inc(g_["flat_psum"], 1)
    return room


def attention2(nc, d, bank, keep, X3, H, AT, wp):
    ident, ident16, ones = keep["ident"], keep["ident16"], keep["ones"]
    NG, T = 4, B
    R = 3 * NG * HD
    SCALE = HD ** -0.5
    QUADS = S // 4
    LOWEST = -3.0e38
    with ExitStack() as ctx:
        room = Room(nc, ctx, "causal")
        sb = room.sb
        qw, kvw, pw, lnw, lnb = (keep["w"][n] for n in ("qw", "kvw", "pw", "ln1_w", "ln1_b"))
        pwp = sb("pwp", [C, 128])
        wT = sb("wT", [C, 192])
        w8f = sb("w8f", [C, 8, R])
        w8 = [sb(f"w8_{i}", [C, 8, R], F16) for i in range(2)]
        wvr = sb("wvr", [C, 4, NG * HD])
        wv = [sb(f"wvd{i}", [C, NG * HD], F16) for i in range(2)]
        low = sb("low", [R, 2])
        b8 = sb("b8", [R, 8])
        b8m = sb("b8m", [R, 8])
        bv = sb("bvd", [128, 1])
        st = sb("st2", [128, B, 6])
        mv = sb("mv2", [128, B, 2])
        rs = sb("rs2", [128, 6, B])
        half = sb("half2", [128, B])
        xn = sb("xn2", [S, GB, C])
        xT = [sb(f"xTd{i}", [C, B * S], F16) for i in range(2)]
        hm = sb("hmd", [R, 4, N], F16)
        QK = sb("QKd", [R, 8, B * S], F16)
        s = room.sems("""d_consts d_raw d_wT d_pwp d_pT d_stack d_hi d_lo d_bias d_b8 d_stats d_mv
            d_rs h_ready dxn dT_psum dT_hi dT_lo e_psum e_hi e_ready carrier2""")
        PT, PB = bank[0], bank[2:6]

        with nc.Block() as block:
            @block.gpsimd
            def _(pool):
                pool.memset(w8f[:], 0.0)
                pool.memset(half[:], -0.5).then_inc(s["d_consts"], 1)
                pool.wait_ge(s["d_mv"], 1)

                def link(ins, n):
                    ins.then_inc(s["d_rs"], 1)
                    pool.wait_ge(s["d_rs"], n)
                link(pool.tensor_scalar(rs[:, 0, :], mv[:, :, 1], 1.0, LN_EPS, ALU.mult, ALU.add), 1)
                link(pool.tensor_tensor(rs[:, 1, :], rs[:, 0, :], half[:], ALU.pow), 2)
                link(pool.tensor_tensor(rs[:, 2, :], rs[:, 1, :], rs[:, 1, :], ALU.mult), 3)
                link(pool.tensor_tensor(rs[:, 2, :], rs[:, 2, :], mv[:, :, 1], ALU.mult), 4)
                link(pool.tensor_scalar(rs[:, 3, :], rs[:, 2, :], 1.0, LN_EPS, ALU.mult, ALU.add), 5)
                link(pool.tensor_tensor(rs[:, 4, :], rs[:, 3, :], half[:], ALU.pow), 6)
                link(pool.tensor_tensor(rs[:, 5, :], rs[:, 4, :], rs[:, 1, :], ALU.mult), 7)
                for b in range(B):
                    last = pool.tensor_scalar(H[:, b, :], X3[:, b, :], mv[:, b, 0:1], rs[:, 1, b:b + 1],
                                              ALU.subtract, ALU.mult)
                last.then_inc(s["h_ready"], 1)

            @block.scalar
            def _(act):
                act.activation(pwp[:].rearrange("p (l g d) -> p l g d", l=4, d=HD),
                               pw[:].rearrange("p (g l d) -> p l g d", l=4, d=HD), ACT.Copy).then_inc(s["d_pwp"], 1)
                act.wait_ge(s["d_raw"], 1)
                act.activation(wT[:], bank[0][:, 0:192], ACT.Copy).then_inc(s["d_wT"], 1)
                act.wait_ge(s["d_wT"], 1)
                act.wait_ge(s["d_consts"], 1)
                wq = wT[:, 0:128].rearrange("p (g l d) -> p l g d", l=4, d=HD)
                w8v = w8f[:].rearrange("p k (r g d) -> p k r g d", g=NG, d=HD)
                for l in range(4):
                    for r in range(3):
                        act.activation(w8v[:, l, r], wq[:, l], ACT.Copy)
                for g in range(NG):
                    act.activation(w8v[:, 4 + g, :, g, :], wT[:, 128 + HD * g:136 + HD * g].unsqueeze(1)
                                   .broadcast_to([C, 3, HD]), ACT.Copy)
                act.activation(wvr[:], wT[:, 160:192].unsqueeze(1).broadcast_to([C, 4, NG * HD]), ACT.Copy
                               ).then_inc(s["d_stack"], 1)
                act.wait_ge(s["d_stack"], 1)
                act.activation(w8[0][:], w8f[:], ACT.Copy, scale=lnw[:])
                act.activation(wv[0][:], wvr[:, 0, :], ACT.Copy, scale=lnw[:])
                act.wait_ge(s["d_pT"], 1)
                act.activation(wp[0][:], bank[1][:, 0:128], ACT.Copy).then_inc(s["d_hi"], 1)
                act.wait_ge(s["d_bias"], 1)
                act.activation(b8[:], bank[2][0:R, 0:8], ACT.Copy)
                act.activation(bv[:], bank[3][:, 0:1], ACT.Copy).then_inc(s["d_b8"], 1)
                act.wait_ge(s["d_b8"], 3)

                def hi(g):
                    act.wait_ge(s["dT_psum"], g + 1)
                    act.activation(tok(xT[0], g), PT[:], ACT.Copy).then_inc(s["dT_hi"], 1)

                def step(g):
                    for k in range(8):
                        if not isinstance(g, int) or g >= 0:
                            act.wait_ge(s["e_psum"], 8 * g + k + 1)
                            after(act, s["e_ready"], 8 * g + k - 3)
                            act.activation(hm[:, k % 4], PB[k % 4][0:R, :], ACT.Identity, bias=b8m[:, k:k + 1],
                                           scale=low[:, k // 4:k // 4 + 1]).then_inc(s["e_hi"], 1)
                        if k == 5 and (not isinstance(g, int) or g + 1 < G):
                            hi(g + 1)
                over_groups(act, step, -1, G - 1)

            @block.vector
            def _(dve):
                for b in range(B):
                    last = dve.bn_stats(st[:, b, :], X3[:, b, :])
                last.then_inc(s["d_stats"], 1)
                dve.wait_ge(s["d_stats"], 1)
                for b in range(B):
                    last = dve.bn_aggr(mv[:, b, :], st[:, b, :])
                last.then_inc(s["d_mv"], 1)
                idv = ident[0:R, 0:R].rearrange("p (r x) -> p r x", r=3)
                dve.tensor_reduce(low[:, 0:1], idv[:, 2, :], AX.X, ALU.add)
                dve.tensor_reduce(low[:, 1:2], idv[:, 1, :], AX.X, ALU.add)
                dve.wait_ge(s["d_hi"], 1)
                dve.tensor_tensor(wp[1][:], bank[1][:, 0:128], wp[0][:], ALU.subtract)
                dve.scalar_tensor_tensor(w8[1][:], w8f[:], lnw[:], w8[0][:], ALU.mult, ALU.subtract)
                dve.scalar_tensor_tensor(wv[1][:], wvr[:, 0, :], lnw[:], wv[0][:], ALU.mult, ALU.subtract
                                         ).then_inc(s["d_lo"], 1)
                dve.wait_ge(s["d_b8"], 1)
                dve.wait_ge(s["d_lo"], 1)
                for k in range(2):
                    dve.tensor_scalar(b8m[:, 4 * k:4 * k + 4], b8[:, 4 * k:4 * k + 4], low[:, k:k + 1], None, ALU.mult
                                      ).then_inc(s["d_b8"], 1)
                dve.wait_ge(s["d_rs"], 7)

                def normalise(g):
                    after_alone(dve, s["dT_psum"], g, s["carrier2"])
                    for i in range(GB):
                        if isinstance(g, int):
                            b = GB * g + i
                            m, r, x = mv[:, b, 0:1], rs[:, 5, b:b + 1], X3[:, b, :]
                        else:
                            at = bass.ds(GB * g + i, 1)
                            m, r = mv[:, at, 0:1].rearrange("p a c -> p (a c)"), rs[:, 5, at]
                            x = X3[:, at, :].rearrange("p a c -> p (a c)")
                        last = dve.tensor_scalar(xn[:, i, :], x, m, r, ALU.subtract, ALU.mult)
                    last.then_inc(s["dxn"], 1)

                def step(g):
                    for k in range(8):
                        if k == 0 and (not isinstance(g, int) or g + 1 < G):
                            normalise(g + 1)
                        if not isinstance(g, int) or g >= 0:
                            dve.wait_ge(s["e_hi"], 8 * g + k + 1)
                            dst = QK[:, k, g * N:g * N + N] if isinstance(g, int) else QK[:, k, bass.ds(g * N, N)]
                            dve.scalar_tensor_tensor(dst, PB[k % 4][0:R, :], b8[:, k:k + 1], hm[:, k % 4],
                                                     ALU.add, ALU.subtract).then_inc(s["e_ready"], 1)
                        if k == 5 and (not isinstance(g, int) or g + 1 < G):
                            dve.wait_ge(s["dT_hi"], g + 2)
                            dve.tensor_tensor(tok(xT[1], g + 1), PT[:], tok(xT[0], g + 1), ALU.subtract
                                              ).then_inc(s["dT_lo"], 1)
                over_groups(dve, step, -1, G - 1)

            @block.tensor
            def _(pe):
                pe.transpose(bank[0][:, 0:128], qw[:], ident[:])
                pe.transpose(bank[0][:, 128:192], kvw[:], ident[0:64, 0:64]).then_inc(s["d_raw"], 1)
                pe.wait_ge(s["d_pwp"], 1)
                pe.transpose(bank[1][:, 0:128], pwp[:], ident[:]).then_inc(s["d_pT"], 1)
                pe.wait_ge(s["d_stack"], 1)
                for k in range(8):
                    pe.matmul(bank[2][0:R, k:k + 1], w8f[:, k], lnb[:], start=True, stop=True)
                pe.matmul(bank[3][:, 0:1], wvr[:].rearrange("p l x -> p (l x)"), lnb[:], start=True, stop=True
                          ).then_inc(s["d_bias"], 1)
                pe.wait_ge(s["d_b8"], 3)
                pe.wait_ge(s["d_lo"], 1)

                def step(g):
                    for k in range(8):
                        if not isinstance(g, int) or g >= 0:
                            if k == 0:
                                pe.wait_ge(s["dT_lo"], g + 1)
                            after(pe, s["e_ready"], 8 * g + k - 3)
                            split_product(pe, PB[k % 4][0:R, :], [w[:, k] for w in w8], [tok(x, g) for x in xT]
                                          ).then_inc(s["e_psum"], 1)
                        if k == 3 and (not isinstance(g, int) or g + 1 < G):
                            pe.wait_ge(s["dxn"], g + 2)
                            after(pe, s["dT_lo"], g + 1)
                            for i in range(GB):
                                last = pe.transpose(PT[:, 128 * i:128 * i + 128], xn[:, i, :], ident[:])
                            last.then_inc(s["dT_psum"], 1)
                over_groups(pe, step, -1, G - 1)

        identb = sb("identb", [128, 128], BF16)
        cm = sb("cm", [128, 128], BF16)
        cmT = sb("cmT", [128, 128], BF16)
        gm = sb("gm", [128, NG * HD])
        nsel = sb("nsel", [32, 4, 128], BF16)
        mx = sb("mxd", [128, 16])
        m2 = sb("m2", [128, 32], BF16)
        mT = sb("mTd", [32, 128], BF16)
        Vq = [sb(f"Vq{i}", [128, 4, NG * HD]) for i in range(2)]
        xq = [[sb(f"xq{k}_{i}", [C, 4, NG, T], F16) for i in range(2)] for k in range(2)]
        P = [sb(f"Pd{i}", [128, 4, 128]) for i in range(2)]
        Dn = sb("Dn", [128, 512])
        Dr = sb("Dr", [128, 512])
        Of = sb("Of", [128, 512])
        Af = sb("Af", [128, 512])
        u = room.sems("""f_consts f_ident ds_psum ds_max dm_hi dm_ready dmT_psum dmT_ready dt_psum dp_ready dv_psum
            dv_ready pv_done dd_sb dd_inv at_f at_hi at_lo xq_hi xq_lo carrier3""")
        SB, T0, T1, VM, MT, O, D = bank[:7]
        TB = [T0, T1]

        def has(q):
            return not isinstance(q, int) or 0 <= q < QUADS

        def past(x):
            return not isinstance(x, int) or x > 0

        def sweep(eng, step):
            for q in range(-2, 4):
                step(q, q % 4, q // 4)
            with eng.Fori(1, QUADS // 4 - 1) as x:
                for i in range(4):
                    step(4 * x + i, i, x)
            for q in range(QUADS - 4, QUADS + 4):
                step(q, q % 4, q // 4)

        def at_position(k0, pos):
            v = QK[:, k0:k0 + 4].rearrange("r k (s p) -> r (k s) p", p=S)
            return v[:, :, pos] if isinstance(pos, int) else v[:, :, bass.ds(pos, 1)].rearrange("r x a -> r (x a)")

        def x_quad(t, q):
            at = slice(4 * q, 4 * q + 4) if isinstance(q, int) else bass.ds(4 * q, 4)
            v = t[:].rearrange("c (s p) -> c p s", p=S)[:, at]
            return v.unsqueeze(2).broadcast_to([C, 4, NG, T])

        def hexcols(t, x):
            return t[:, 512 * x:512 * x + 512] if isinstance(x, int) else t[:, bass.ds(512 * x, 512)]

        with nc.Block() as block:
            @block.gpsimd
            def _(pool):
                pool.tensor_copy(identb[:], ident[:])
                pool.memset(cm[:], 0.0)
                pool.memset(cmT[:], 0.0)
                pool.memset(gm[:], 0.0)
                pool.memset(nsel[:], 0.0).then_inc(u["f_consts"], 1)
                pool.wait_ge(u["f_consts"], 1)
                for g in range(4):
                    rows = slice(32 * g, 32 * g + 32)
                    pool.affine_select(out=cm[rows].rearrange("p (g t) -> p g t", g=4),
                                       in_=cm[rows].rearrange("p (g t) -> p g t", g=4), compare_op=ALU.is_ge,
                                       fill=LOWEST, base=0, pattern=[[0, 4], [-1, T]], channel_multiplier=1)
                    pool.affine_select(out=cmT[rows].rearrange("p (l s) -> p l s", l=4),
                                       in_=cmT[rows].rearrange("p (l s) -> p l s", l=4), compare_op=ALU.is_ge,
                                       fill=LOWEST, base=0, pattern=[[0, 4], [1, T]], channel_multiplier=-1)
                    pool.memset(gm[rows, HD * g:HD * g + HD], 1.0)
                nv = nsel[:].rearrange("r p (g t) -> r p g t", g=4)
                for k in range(2):
                    pool.affine_select(out=nv, in_=nv, compare_op=ALU.not_equal, fill=-1.0, base=-16 * k,
                                       pattern=[[-4, 4], [-1, 4], [0, T]], channel_multiplier=1
                                       ).then_inc(u["f_consts"], 1)
                    pool.wait_ge(u["f_consts"], 2 + k)

            @block.scalar
            def _(act):
                def step(q, i, x):
                    if has(q + 2):
                        after_alone(act, u["dv_psum"], q + 1, u["carrier3"])
                        act.activation(xq[0][i % 2][:], x_quad(xT[0], q + 2), ACT.Copy).then_inc(u["xq_hi"], 1)
                    if has(q):
                        act.wait_ge(u["dmT_psum"], q + 1)
                        after(act, u["dt_psum"], q)
                        act.activation(mT[:], MT[0:32, 0:64].bitcast(BF16), ACT.Copy).then_inc(u["dmT_ready"], 1)
                    if i == 0 and has(q - 1):
                        act.wait_ge(u["pv_done"], q)
                        act.activation(Dn[:], D[:], ACT.Copy)
                        act.activation(Of[:], O[:], ACT.Copy).then_inc(u["dd_sb"], 1)
                    if has(q):
                        act.wait_ge(u["dt_psum"], q + 1)
                        after(act, u["pv_done"], q - 1)
                        act.activation(P[i % 2][:].rearrange("p a x -> p (a x)"), TB[i % 2][:], ACT.Exp, scale=SCALE
                                       ).then_inc(u["dp_ready"], 1)
                    if i == 3 and past(x):
                        act.wait_ge(u["at_f"], 4 * x)
                        act.activation(hexcols(AT[0], x - 1), Af[:], ACT.Identity, bias=bv[:]).then_inc(u["at_hi"], 1)
                sweep(act, step)

            @block.vector
            def _(dve):
                dve.wait_ge(u["f_consts"], 3)

                def step(q, i, x):
                    if has(q + 1):
                        dve.wait_ge(u["ds_psum"], q + 2)
                        after(dve, u["dm_ready"], q + 1)
                        dve.tensor_reduce(mx[:], SB[:].rearrange("p (a t) -> p a t", t=T), AX.X, ALU.max
                                          ).then_inc(u["ds_max"], 1)
                        dve.wait_ge(u["ds_max"], q + 2)
                        after(dve, u["dmT_psum"], q + 1)
                        dve.tensor_copy(m2[:, 0:16], mx[:]).then_inc(u["dm_hi"], 1)
                        dve.wait_ge(u["dm_hi"], q + 2)
                        dve.tensor_tensor(m2[:, 16:32], mx[:], m2[:, 0:16], ALU.subtract).then_inc(u["dm_ready"], 1)
                    if past(x):
                        cols = slice(128 * i, 128 * i + 128)
                        dve.wait_ge(u["dd_sb"], x)
                        dve.reciprocal(Dr[:, cols], Dn[:, cols]).then_inc(u["dd_inv"], 1)
                        dve.wait_ge(u["dd_inv"], 4 * (x - 1) + i + 1)
                        dve.tensor_tensor(Af[:, cols], Of[:, cols], Dr[:, cols], ALU.mult).then_inc(u["at_f"], 1)
                    if has(q + 1):
                        dve.wait_ge(u["dv_psum"], q + 2)
                        after(dve, u["pv_done"], q)
                        dve.tensor_tensor(Vq[(i + 1) % 2][:], VM[:, 0:128].rearrange("p (a x) -> p a x", a=4),
                                          gm[:].unsqueeze(1).broadcast_to([128, 4, NG * HD]), ALU.mult
                                          ).then_inc(u["dv_ready"], 1)
                    if has(q + 2):
                        after_alone(dve, u["dv_psum"], q + 1, u["carrier3"])
                        dve.tensor_copy(xq[1][i % 2][:], x_quad(xT[1], q + 2)).then_inc(u["xq_lo"], 1)
                    if i == 3 and past(x):
                        dve.wait_ge(u["at_hi"], x)
                        dve.scalar_tensor_tensor(hexcols(AT[1], x - 1), Af[:], bv[:], hexcols(AT[0], x - 1),
                                                 ALU.add, ALU.subtract).then_inc(u["at_lo"], 1)
                        dve.wait_ge(u["at_lo"], x)
                sweep(dve, step)

            @block.tensor
            def _(pe):
                pe.wait_ge(u["f_consts"], 3)

                def step(q, i, x):
                    if has(q):
                        pe.wait_ge(u["dm_ready"], q + 1)
                        after(pe, u["dmT_ready"], q)
                        pe.transpose(MT[0:32, 0:64].bitcast(BF16), m2[:], identb[:]).then_inc(u["dmT_psum"], 1)
                    if has(q + 1):
                        after(pe, u["ds_max"], q + 1)
                        for p in range(4):
                            pe.matmul(SB[:, 128 * p:128 * p + 128], at_position(0, 4 * (q + 1) + p),
                                      at_position(4, 4 * (q + 1) + p), start=(p == 0), stop=False,
                                      skip_group_check=True)
                        pe.matmul(SB[:], identb[:], cm[:].unsqueeze(1).broadcast_to([128, 4, 128]),
                                  start=False, stop=True, skip_group_check=True).then_inc(u["ds_psum"], 1)
                    if has(q):
                        after(pe, u["dp_ready"], q - 1)
                        for p in range(4):
                            pe.matmul(TB[i % 2][:, 128 * p:128 * p + 128], at_position(4, 4 * q + p),
                                      at_position(0, 4 * q + p), start=(p == 0), stop=False, skip_group_check=True)
                        pe.matmul(TB[i % 2][:], identb[:], cmT[:].unsqueeze(1).broadcast_to([128, 4, 128]),
                                  start=False, stop=False, skip_group_check=True)
                    if has(q + 1):
                        after(pe, u["dv_ready"], q + 1)
                        pe.wait_ge(u["xq_hi"], q + 2)
                        pe.wait_ge(u["xq_lo"], q + 2)
                        for p in range(4):
                            last = split_product(pe, VM[:, 32 * p:32 * p + 32],
                                                 [t[(i + 1) % 2][:, p].rearrange("c g t -> c (g t)") for t in xq], [w[:] for w in wv])
                        last.then_inc(u["dv_psum"], 1)
                    if has(q):
                        pe.wait_ge(u["dmT_ready"], q + 1)
                        for p in range(4):
                            last = pe.matmul(TB[i % 2][:, 128 * p:128 * p + 128], nsel[:, p, :], mT[:],
                                             start=False, stop=True, skip_group_check=True)
                        last.then_inc(u["dt_psum"], 1)
                    if has(q - 1):
                        k = (i - 1) % 4
                        pe.wait_ge(u["dp_ready"], q)
                        pe.wait_ge(u["dv_ready"], q)
                        if k == 0:
                            after(pe, u["dd_sb"], x)
                        for p in range(4):
                            for l in range(4):
                                pe.matmul(O[32 * l:32 * l + 32, 128 * k + 32 * p:128 * k + 32 * p + 32],
                                          Vq[k % 2][:, p, :], P[k % 2][:, p, 32 * l:32 * l + 32],
                                          start=True, stop=True, tile_position=(0, 32 * l))
                        for l in range(4):
                            last = pe.matmul(D[32 * l:32 * l + 32, 128 * k:128 * k + 128], gm[:],
                                             P[k % 2][:, :, 32 * l:32 * l + 32], start=True, stop=True,
                                             tile_position=(0, 32 * l))
                        last.then_inc(u["pv_done"], 1)
                sweep(pe, step)
    return room


def experts1(nc, d, bank, keep, X3, H, AT, wp, out):
    ident, ones = keep["ident"], keep["ones"]
    NB, LAG, RING, HR = 2 * NE, 4, 4, 8
    GSTEPS = 12
    with ExitStack() as ctx:
        room = Room(nc, ctx, "moe")
        sb = room.sb
        w1r, w2r, rw, lnw, lnb = (keep["w"][n] for n in ("w1", "w2", "rw", "ln2_w", "ln2_b"))
        w1 = [sb(f"w1_{i}", [C, NB, 128], F16) for i in range(2)]
        w2 = [sb(f"w2_{i}", [128, NB, C], F16) for i in range(2)]
        rT = sb("rT", [C, NE])
        r16 = [sb(f"r16_{i}", [C, NE], F16) for i in range(2)]
        lnbr = sb("lnbr", [C, 128])
        b1 = sb("b1", [128, NB])
        rb = sb("rb", [128, NE])
        before8 = sb("before8e", [128, NE, NE])
        half = sb("half3", [128, GB])
        xT = [sb(f"xTe{i}", [C, B * S], F16) for i in range(2)]
        st = sb("st3", [128, GB, 6])
        mv = sb("mv3", [128, GB, 2])
        rs = sb("rs3", [128, 2, GB])
        xn = sb("xn3", [S, GB, C])
        lg = sb("lg", [128, GB, NE])
        pr = sb("pr", [128, GB, NE])
        r1 = sb("r1", [128, 3, GB])
        c8 = sb("c8e", [128, 3, GB, NE, NE])
        cnt = sb("cnte", [128, GB, NE])
        sel = sb("sele", [128, GB, NE])
        wgt = sb("wgte", [128, B, NE])
        hm = sb("hme", [128, RING, N])
        hp = [sb(f"hpe{i}", [128, HR, N], F16) for i in range(2)]
        s = room.sems("""e_consts e_rT e_rTs e_bias e_split e_b pj_psum ph_ready st_e mv_e eps_e
            rs_e r_ready xn_e xT_e_psum xTe_hi xTe_lo lg_psum g_in g_exp g_step wgt_ready up_psum gelu hi_e lo_e
            down_psum x4_step x4_ready stored carrier4""")
        UP, Y, PX, LG = bank[0:4], bank[4:6], bank[6], bank[7]

        def xg(t, g):
            return t[:, GB * g:GB * g + GB, :] if isinstance(g, int) else t[:, bass.ds(GB * g, GB), :]

        def nxt(g):
            return not isinstance(g, int) or g + 1 < G

        def cur(g):
            return not isinstance(g, int) or g >= 0

        def late(g, p, lag):
            h = g if p >= lag else g - 1
            return (h, (p - lag) % NB) if cur(h) else None

        with nc.Block() as block:
            @block.sync
            def _(sp):
                def store(g):
                    wait_alone(sp, s["x4_ready"], g + 1, s["carrier4"])
                    dst = out[GB * g:GB * g + GB] if isinstance(g, int) else out[bass.ds(GB * g, GB)]
                    sp.dma_start(dst.rearrange("b s c -> s b c"), xg(X3, g)).then_inc(s["stored"], 16)
                    wait_alone(sp, s["stored"], 16 * (g + 1), s["carrier4"])
                over_groups(sp, store, 0, G - 1)

            @block.gpsimd
            def _(pool):
                pool.memset(half[:], -0.5)
                pool.memset(before8[:], 1.0).then_inc(s["e_consts"], 1)
                pool.wait_ge(s["e_consts"], 1)
                pool.affine_select(out=before8[:], in_=before8[:], compare_op=ALU.is_gt, fill=0.0, base=0,
                                   pattern=[[1, NE], [-1, NE]], channel_multiplier=0).then_inc(s["e_consts"], 1)

                def step(g):
                    for p in range(NB):
                        if nxt(g) and p == 1:
                            wait_alone(pool, s["mv_e"], g + 2, s["carrier4"])
                            pool.tensor_scalar(rs[:, 0, :], mv[:, :, 1], 1.0, LN_EPS, ALU.mult, ALU.add
                                               ).then_inc(s["eps_e"], 1)
                            pool.wait_ge(s["eps_e"], g + 2)
                            pool.tensor_tensor(rs[:, 1, :], rs[:, 0, :], half[:], ALU.pow).then_inc(s["rs_e"], 1)
                        if nxt(g) and p == 9:
                            pool.tensor_tensor(xg(X3, g + 1), xg(X3, g + 1), xg(H, g + 1), ALU.add
                                               ).then_inc(s["r_ready"], 1)
                        if cur(g):
                            pool.wait_ge(s["hi_e"], NB * g + p + 1)
                            pool.tensor_tensor(hp[1][:, p % HR], hm[:, p % RING], hp[0][:, p % HR], ALU.subtract
                                               ).then_inc(s["lo_e"], 1)
                over_groups(pool, step, -1, G - 1)

            @block.scalar
            def _(act):
                act.wait_ge(s["e_rT"], 1)
                act.activation(rT[:], LG[:, 0:NE], ACT.Copy).then_inc(s["e_rTs"], 1)
                act.wait_ge(s["e_rTs"], 1)
                act.activation(r16[0][:], rT[:], ACT.Copy, scale=lnw[:])
                act.activation(lnbr[:], ones[:], ACT.Copy, scale=lnb[:]).then_inc(s["e_bias"], 1)
                act.activation(w1[0][:], w1r[:], ACT.Copy, scale=lnw[:])
                act.activation(w2[0][:], w2r[:], ACT.Copy).then_inc(s["e_split"], 1)
                act.wait_ge(s["e_b"], 1)
                act.activation(b1[:], PX[:, 0:NB], ACT.Copy)
                act.activation(rb[:], PX[:, NB:NB + NE], ACT.Copy).then_inc(s["e_bias"], 1)
                act.wait_ge(s["e_bias"], 2)

                def step(g):
                    for p in range(NB):
                        k = NB * g + p
                        if cur(g):
                            act.wait_ge(s["up_psum"], k + 1)
                            after(act, s["lo_e"], k - RING + 1)
                            act.activation(hm[:, p % RING], UP[p % RING][:], ACT.Gelu_apprx_tanh, bias=b1[:, p:p + 1]
                                           ).then_inc(s["gelu"], 1)
                        if nxt(g) and p == 6:
                            act.wait_ge(s["xT_e_psum"], g + 2)
                            act.activation(tok(xT[0], g + 1), PX[:], ACT.Copy).then_inc(s["xTe_hi"], 1)
                        if nxt(g) and p == 10:
                            act.wait_ge(s["g_in"], g + 2)
                            act.activation(pr[:].rearrange("p b e -> p (b e)"), lg[:].rearrange("p b e -> p (b e)"),
                                           ACT.Exp).then_inc(s["g_exp"], 1)
                over_groups(act, step, -1, G - 1)

            @block.vector
            def _(dve):
                dve.wait_ge(s["e_bias"], 1)
                dve.scalar_tensor_tensor(r16[1][:], rT[:], lnw[:], r16[0][:], ALU.mult, ALU.subtract)
                dve.wait_ge(s["e_split"], 1)
                dve.scalar_tensor_tensor(w1[1][:], w1r[:], lnw[:], w1[0][:], ALU.mult, ALU.subtract)
                dve.tensor_tensor(w2[1][:], w2r[:], w2[0][:], ALU.subtract).then_inc(s["e_split"], 1)
                dve.wait_ge(s["e_bias"], 2)
                dve.wait_ge(s["e_consts"], 2)
                steps = 0

                def link(g, ins):
                    nonlocal steps
                    steps += 1
                    ins.then_inc(s["g_step"], 1)
                    dve.wait_ge(s["g_step"], GSTEPS * g + steps)

                def gate(g, p):
                    nonlocal steps
                    wide = [128, GB, NE]
                    deep = [128, GB, NE, NE]
                    if p == 9:
                        steps = 0
                        dve.wait_ge(s["lg_psum"], g + 1)
                        link(g, dve.tensor_tensor(lg[:], LG[:, 0:GB * NE].rearrange("p (b e) -> p b e", e=NE),
                                                  rb[:].unsqueeze(1).broadcast_to(wide), ALU.add))
                        link(g, dve.tensor_reduce(r1[:, 0], lg[:], AX.X, ALU.max))
                        dve.tensor_tensor(lg[:], lg[:], r1[:, 0].unsqueeze(2).broadcast_to(wide), ALU.subtract
                                          ).then_inc(s["g_in"], 1)
                    elif p == 11:
                        dve.wait_ge(s["g_exp"], g + 1)
                        link(g, dve.tensor_reduce(r1[:, 1], pr[:], AX.X, ALU.add))
                        link(g, dve.reciprocal(r1[:, 2], r1[:, 1]))
                        link(g, dve.tensor_tensor(pr[:], pr[:], r1[:, 2].unsqueeze(2).broadcast_to(wide), ALU.mult))
                    elif p == 12:
                        other = pr[:].unsqueeze(2).broadcast_to(deep)
                        own = pr[:].unsqueeze(3).broadcast_to(deep)
                        dve.tensor_tensor(c8[:, 0], other, own, ALU.is_gt)
                        link(g, dve.tensor_tensor(c8[:, 1], other, own, ALU.is_equal))
                    elif p == 13:
                        tie = before8[:].unsqueeze(1).broadcast_to(deep)
                        link(g, dve.tensor_tensor(c8[:, 2], c8[:, 1], tie, ALU.mult))
                        link(g, dve.tensor_tensor(c8[:, 1], c8[:, 0], c8[:, 2], ALU.add))
                    elif p == 14:
                        link(g, dve.tensor_reduce(cnt[:], c8[:, 1], AX.X, ALU.add))
                        link(g, dve.tensor_scalar(sel[:], cnt[:], 2.0, None, ALU.is_lt))
                        link(g, dve.tensor_tensor(sel[:], sel[:], pr[:], ALU.mult))
                        link(g, dve.tensor_copy(xg(wgt, g), sel[:]))
                        assert steps == GSTEPS

                def prep(g, p):
                    if p == 0:
                        wait_alone(dve, s["pj_psum"], g + 1, s["carrier4"])
                        h = xg(H, g).rearrange("p b c -> p (b c)")
                        dve.tensor_tensor(h, PX[:], h, ALU.add).then_inc(s["ph_ready"], 1)
                    elif p == 1:
                        wait_alone(dve, s["ph_ready"], g + 1, s["carrier4"])
                        for i in range(GB):
                            last = dve.bn_stats(st[:, i, :], xg(H, g)[:, i, :])
                        last.then_inc(s["st_e"], 1)
                        wait_alone(dve, s["st_e"], g + 1, s["carrier4"])
                        for i in range(GB):
                            last = dve.bn_aggr(mv[:, i, :], st[:, i, :])
                        last.then_inc(s["mv_e"], 1)
                    elif p == 3:
                        wait_alone(dve, s["rs_e"], g + 1, s["carrier4"])
                        for i in range(GB):
                            last = dve.tensor_scalar(xn[:, i, :], xg(H, g)[:, i, :], mv[:, i, 0:1],
                                                     rs[:, 1, i:i + 1], ALU.subtract, ALU.mult)
                        last.then_inc(s["xn_e"], 1)
                    elif p == 6:
                        dve.wait_ge(s["xTe_hi"], g + 1)
                        dve.tensor_tensor(tok(xT[1], g), PX[:], tok(xT[0], g), ALU.subtract).then_inc(s["xTe_lo"], 1)
                    else:
                        gate(g, p)

                def combine(at):
                    if at is None:
                        return
                    g, p = at
                    e = p // 2
                    wait_alone(dve, s["down_psum"], NB * g + p + 1, s["carrier4"])
                    if e == 0:
                        wait_alone(dve, s["r_ready"], g + 1, s["carrier4"])
                    else:
                        wait_alone(dve, s["x4_step"], (NE - 1) * g + e, s["carrier4"])
                    for i in range(GB):
                        x = xg(X3, g)[:, i, :]
                        w = xg(wgt, g)[:, i, e:e + 1]
                        last = dve.scalar_tensor_tensor(x, Y[e % 2][:, 128 * i:128 * i + 128], w, x, ALU.mult, ALU.add)
                    last.then_inc(s["x4_ready" if e == NE - 1 else "x4_step"], 1)

                def step(g):
                    for p in range(NB):
                        if cur(g):
                            dve.wait_ge(s["gelu"], NB * g + p + 1)
                            after(dve, s["down_psum"], NB * g + p - HR + 1)
                            dve.tensor_copy(hp[0][:, p % HR], hm[:, p % RING]).then_inc(s["hi_e"], 1)
                        if p % 2 == 0:
                            combine(late(g, p, LAG + 1))
                        if nxt(g):
                            prep(g + 1, p)
                over_groups(dve, step, -1, G - 1)
                for e in (NE - 3, NE - 2, NE - 1):
                    combine((G - 1, 2 * e + 1))

            @block.tensor
            def _(pe):
                pe.transpose(LG[:, 0:NE], rw[:], ident[0:NE, 0:NE]).then_inc(s["e_rT"], 1)
                pe.wait_ge(s["e_bias"], 1)
                for p in range(NB):
                    pe.matmul(PX[:, p:p + 1], w1r[:, p], lnb[:], start=True, stop=True)
                pe.matmul(PX[:, NB:NB + NE], lnbr[:], rT[:], start=True, stop=True).then_inc(s["e_b"], 1)
                pe.wait_ge(s["e_split"], 2)
                pe.wait_ge(s["e_bias"], 2)

                def prep(g, p):
                    if p == 0:
                        after(pe, s["xTe_lo"], g)
                        for i in range(GB):
                            b = GB * g + i
                            a = [t[:].rearrange("r (p s) -> r s p", s=B)[:, b, :] if isinstance(b, int) else
                                 t[:].rearrange("r (p s) -> r s p", s=B)[:, bass.ds(b, 1), :]
                                 .rearrange("r a p -> r (a p)") for t in AT]
                            last = split_product(pe, PX[:, 128 * i:128 * i + 128], a, [w[:] for w in wp])
                        last.then_inc(s["pj_psum"], 1)
                    elif p == 6:
                        pe.wait_ge(s["xn_e"], g + 1)
                        for i in range(GB):
                            last = pe.transpose(PX[:, 128 * i:128 * i + 128], xn[:, i, :], ident[:])
                        last.then_inc(s["xT_e_psum"], 1)
                    elif p == 9:
                        pe.wait_ge(s["xTe_lo"], g + 1)
                        for i in range(GB):
                            last = split_product(pe, LG[:, NE * i:NE * i + NE], [tok(t, g, 128 * i, 128) for t in xT],
                                                 [r[:] for r in r16])
                        last.then_inc(s["lg_psum"], 1)

                def down(at):
                    if at is None:
                        return
                    g, p = at
                    e = p // 2
                    pe.wait_ge(s["lo_e"], NB * g + p + 1)
                    if p % 2 == 0:
                        if e >= 2:
                            pe.wait_ge(s["x4_step"], (NE - 1) * g + e - 1)
                        elif e == 0:
                            after(pe, s["x4_step"], (NE - 1) * g)
                        else:
                            after(pe, s["x4_ready"], g)
                    for i in range(GB):
                        cols = slice(128 * i, 128 * i + 128)
                        last = split_product(pe, Y[e % 2][:, cols], [h[:, p % HR, cols] for h in hp],
                                             [w[:, p] for w in w2], start=(p % 2 == 0 and i == 0),
                                             stop=(p % 2 == 1), skip_group_check=True)
                    last.then_inc(s["down_psum"], 1)

                def step(g):
                    for p in range(NB):
                        k = NB * g + p
                        if cur(g):
                            if p == 0:
                                pe.wait_ge(s["xTe_lo"], g + 1)
                            after(pe, s["gelu"], k - RING + 1)
                            split_product(pe, UP[p % RING][:], [w[:, p] for w in w1], [tok(t, g) for t in xT]
                                          ).then_inc(s["up_psum"], 1)
                        if nxt(g):
                            prep(g + 1, p)
                        down(late(g, p, LAG))
                over_groups(pe, step, -1, G - 1)
                for p in range(NB - LAG, NB):
                    down((G - 1, p))


def build(nc, d, out):
    with ExitStack() as ctx:
        room = Room(nc, ctx, "program")
        bank = [ctx.enter_context(nc.psum_tensor(f"bank{i}", [128, 512], F32)) for i in range(8)]
        keep = {
            "X": room.sb("X", [S, B, C]),
            "ident": room.sb("ident", [128, 128]),
            "ident16": room.sb("ident16", [128, 128], F16),
            "ones": room.sb("ones", [128, 128]),
        }
        keep["ctx_sum"] = room.sb("ctx_sum", [CT + 1, B])
        keep["w"], keep["moves"] = layer1_weights(room, d)
        X3 = room.sb("X3", [S, B, C])
        with ExitStack() as inner:
            keep["cT"] = [Room(nc, inner, "context").sb(f"cT{i}", [CT + 1, B * S], F16) for i in range(2)]
            layer0(nc, d, bank, keep).end()
            attention1(nc, d, bank, keep, X3).end()
        AT = [room.sb(f"AT{i}", [C, S * B], F16) for i in range(2)]
        wp = [room.sb(f"wp{i}", [C, C], F16) for i in range(2)]
        attention2(nc, d, bank, keep, X3, keep["X"], AT, wp)
        experts1(nc, d, bank, keep, X3, keep["X"], AT, wp, out)


def kernel(**inputs):
    import numpy as np
    import concourse.bacc as bacc
    from concourse.bass_utils import run_bass_kernel_spmd as run

    nc = bacc.Bacc("TRN2", target_bir_lowering=False, num_devices=1)
    arrays, d = {}, {}
    for name, value in inputs.items():
        a = np.ascontiguousarray(value)
        arrays["in_" + name] = a
        d[name] = nc.dram_tensor("in_" + name, a.shape, mybir.dt.from_np(a.dtype), kind="ExternalInput").ap()
    out = nc.dram_tensor("out_x", (B, S, C), F32, kind="ExternalOutput").ap()
    build(nc, d, out)
    r = run(nc, [arrays], core_ids=[0])
    return r.results[0]["out_x"]
```
